# Optimizing a Trainium2 kernel written in Bass

```python
import numpy as np
import jax
import jax.numpy as jnp

def _softmax(x, axis=-1):
    return jax.nn.softmax(x, axis=axis)

def _gelu(x):
    return jax.nn.gelu(x, approximate=True)

def _silu(x):
    return jax.nn.silu(x)

def _sigmoid(x):
    return jax.nn.sigmoid(x)

def _layernorm(x, axis=-1, eps=1e-05):
    m = jnp.mean(x, axis=axis, keepdims=True)
    v = jnp.var(x, axis=axis, keepdims=True)
    return (x - m) / jnp.sqrt(v + eps)

def _scatter_add(tgt, idx, src, axis=0):
    return tgt.at[idx].add(src)

def _segment_sum(src, seg, n):
    return jax.ops.segment_sum(src, seg, n)
kernel_name = 'mk_conv_attn_hybrid_d4_conv_nhwc128_r4_fb3479'

def setup_inputs(seed: int=0):
    np.random.seed(seed)
    _w = jnp.asarray

    def _rec_inputs():
        import jax
        import jax.numpy as jnp
        _gk = jax.random.key(seed)
        x = -0.0005207 + 1.001 * jax.random.normal(jax.random.fold_in(_gk, 1), (4, 16, 16, 32), jnp.float32)
        return x
    x = _rec_inputs()

    def _L0_conv_setup():
        import jax, jax.numpy as jnp
        import numpy as np
        B, H, W, C = (4, 16, 16, 32)
        G = 4
        HC = C // G
        K = 3
        K2 = K * K
        PAD = K // 2
        SCALE = HC ** (-0.5)

        def conv2d(x, w, padding=1, dilation=1, groups=1):
            return jax.lax.conv_general_dilated(x, w, (1, 1), [(padding, padding), (padding, padding)], rhs_dilation=(dilation, dilation), dimension_numbers=('NCHW', 'OIHW', 'NCHW'), feature_group_count=groups)

        def pconv(x, w):
            c4 = w.shape[0]
            return jnp.concatenate([conv2d(x[:, :c4], w, padding=1), x[:, c4:]], axis=1)

        def conv1x1(x, w, b):
            return jnp.einsum('bchw,oc->bohw', x, w) + b[None, :, None, None]

        def deform_sample(img, offset, mask, dilation, pad):
            b, cg, h, w = img.shape
            ky, kx = jnp.meshgrid(jnp.arange(K), jnp.arange(K), indexing='ij')
            base_y = (ky.reshape(-1) * dilation - pad).astype(img.dtype)
            base_x = (kx.reshape(-1) * dilation - pad).astype(img.dtype)
            off = offset.reshape(b, K2, 2, h, w)
            py = jnp.arange(h, dtype=img.dtype)[None, None, :, None] + base_y[None, :, None, None] + off[:, :, 0]
            px = jnp.arange(w, dtype=img.dtype)[None, None, None, :] + base_x[None, :, None, None] + off[:, :, 1]
            y0 = jnp.floor(py)
            x0 = jnp.floor(px)
            wy = py - y0
            wx = px - x0
            flat = img.reshape(b, cg, h * w)

            def gather(iy, ix):
                valid = ((iy >= 0) & (iy < h) & (ix >= 0) & (ix < w)).astype(img.dtype)
                idx = (jnp.clip(iy, 0, h - 1) * w + jnp.clip(ix, 0, w - 1)).astype(jnp.int32)
                g = jax.vmap(lambda f, i: jnp.take(f, i, axis=1))(flat, idx.reshape(b, -1))
                return g.reshape(b, cg, K2, h, w) * valid[:, None]
            wy_ = wy[:, None]
            wx_ = wx[:, None]
            out = gather(y0, x0) * (1 - wy_) * (1 - wx_) + gather(y0, x0 + 1) * (1 - wy_) * wx_ + gather(y0 + 1, x0) * wy_ * (1 - wx_) + gather(y0 + 1, x0 + 1) * wy_ * wx_
            return out * mask[:, None]
        key = jax.random.key(seed)
        ks = jax.random.split(key, 14)
        d = {}
        d['x'] = jax.random.normal(ks[0], (B, H, W, C), jnp.float32)
        d['w_qkv'] = jax.random.normal(ks[1], (C, 3 * C), jnp.float32) * C ** (-0.5)
        d['b_qkv'] = jax.random.normal(ks[2], (3 * C,), jnp.float32) * 0.02
        d['w_dw'] = jax.random.normal(ks[3], (3 * C, 1, 3, 3), jnp.float32) * 0.2
        d['b_dw'] = jax.random.normal(ks[4], (3 * C,), jnp.float32) * 0.02
        d['pconv_off_w'] = jax.random.normal(ks[5], (G, C // 4, C // 4, 3, 3), jnp.float32) * 0.05
        d['w_off'] = jax.random.normal(ks[6], (G, 2 * K2, C), jnp.float32) * 0.01
        d['b_off'] = jax.random.normal(ks[7], (G, 2 * K2), jnp.float32) * 0.01
        d['pconv_mask_w'] = jax.random.normal(ks[8], (C // 4, C // 4, 3, 3), jnp.float32) * 0.05
        d['w_mask'] = jax.random.normal(ks[9], (K2, C), jnp.float32) * 0.01
        d['b_mask'] = jax.random.normal(ks[10], (K2,), jnp.float32) * 0.01
        d['w_proj'] = jax.random.normal(ks[11], (C, C), jnp.float32) * C ** (-0.5)
        d['b_proj'] = jax.random.normal(ks[12], (C,), jnp.float32) * 0.02
        return d
    _L0_conv_all = _L0_conv_setup()
    _L0_conv_in = {k: v for k, v in _L0_conv_all.items() if k in ('w_qkv', 'b_qkv', 'w_dw', 'b_dw', 'pconv_off_w', 'w_off', 'b_off', 'pconv_mask_w', 'w_mask', 'b_mask', 'w_proj', 'b_proj')}
    del _L0_conv_all

    def _L1_conv_setup():
        import jax, jax.numpy as jnp
        import numpy as np
        from jax import lax
        TEMPERATURE = 30.0
        BN_EPS = 1e-05
        key = jax.random.key(seed)
        ks = jax.random.split(key, 9)
        B, H, W, C_in = (32, 16, 16, 32)
        n_filters, r_filters, n_kernels = (32, 4, 4)
        x = jax.random.normal(ks[0], (B, H, W, C_in), dtype=jnp.float32)
        reduction_kernel = jax.random.normal(ks[1], (C_in, r_filters), dtype=jnp.float32) * 0.02
        attention_kernel = jax.random.normal(ks[2], (r_filters, n_kernels), dtype=jnp.float32) * 0.02
        conv_kernels = jax.random.normal(ks[3], (n_kernels, 3, 3, C_in, n_filters), dtype=jnp.float32) * 0.05
        bias = jax.random.normal(ks[4], (n_kernels, n_filters), dtype=jnp.float32) * 0.05
        bn_scale = jax.random.uniform(ks[5], (n_filters,), dtype=jnp.float32, minval=0.5, maxval=1.5)
        bn_bias = jax.random.normal(ks[6], (n_filters,), dtype=jnp.float32) * 0.1
        bn_mean = jax.random.normal(ks[7], (n_filters,), dtype=jnp.float32) * 0.1
        bn_var = jax.random.uniform(ks[8], (n_filters,), dtype=jnp.float32, minval=0.5, maxval=1.5)
        return {'x': x, 'reduction_kernel': reduction_kernel, 'attention_kernel': attention_kernel, 'conv_kernels': conv_kernels, 'bias': bias, 'bn_scale': bn_scale, 'bn_bias': bn_bias, 'bn_mean': bn_mean, 'bn_var': bn_var}
    _L1_conv_all = _L1_conv_setup()
    _L1_conv_in = {k: v for k, v in _L1_conv_all.items() if k in ('reduction_kernel', 'attention_kernel', 'conv_kernels', 'bias', 'bn_scale', 'bn_bias', 'bn_mean', 'bn_var')}
    del _L1_conv_all

    def _L2_attn_setup():
        import jax, jax.numpy as jnp
        import numpy as np
        NEG = -1000000000000.0
        key = jax.random.key(seed)
        k1, k2, k3, k4 = jax.random.split(key, 4)
        B, T, D, U = (4, 1024, 32, 32)
        query = jax.random.normal(k1, (B, T, D), dtype=jnp.float32)
        s = 1.0 / np.sqrt(D)
        Wq = jax.random.normal(k2, (D, U), dtype=jnp.float32) * s
        Wk = jax.random.normal(k3, (D, U), dtype=jnp.float32) * s
        Wv = jax.random.normal(k4, (D, U), dtype=jnp.float32) * s
        return {'query': query, 'Wq': Wq, 'Wk': Wk, 'Wv': Wv}
    _L2_attn_all = _L2_attn_setup()
    _L2_attn_in = {k: v for k, v in _L2_attn_all.items() if k in ('Wq', 'Wk', 'Wv')}
    del _L2_attn_all

    def _L2_ffn_setup():
        import jax, jax.numpy as jnp
        import numpy as np
        B, N, D, C, E, K = (8, 2048, 32, 32, 8, 2)
        key = jax.random.key(seed)
        k0, k1, k2 = jax.random.split(key, 3)
        x = jax.random.normal(k0, (B, N, D), dtype=jnp.float32)
        router_w = jax.random.normal(k1, (D, E), dtype=jnp.float32) * 0.05
        router_b = jnp.zeros((E,), dtype=jnp.float32)
        expert_w = jax.random.normal(k2, (E, D, C), dtype=jnp.float32) * (1.0 / np.sqrt(D))
        expert_b = jnp.zeros((E, C), dtype=jnp.float32)
        return {'x': x, 'router_w': router_w, 'router_b': router_b, 'expert_w': expert_w, 'expert_b': expert_b}
    _L2_ffn_all = _L2_ffn_setup()
    _L2_ffn_in = {k: v for k, v in _L2_ffn_all.items() if k in ('router_w', 'router_b', 'expert_w', 'expert_b')}
    del _L2_ffn_all

    def _L3_attn_setup():
        import jax, jax.numpy as jnp
        import numpy as np
        B, S, D, H = (4, 1024, 32, 16)
        DH = D * H
        key = jax.random.key(seed)
        ks = jax.random.split(key, 10)
        sc = lambda fan: 1.0 / np.sqrt(fan)
        return {'x': jax.random.normal(ks[0], (B, S, D), jnp.float32), 'mask': jnp.ones((B, S), jnp.bool_), 'wq_w': jax.random.normal(ks[1], (DH, D), jnp.float32) * sc(D), 'wq_b': jax.random.normal(ks[2], (DH,), jnp.float32) * 0.01, 'wk_w': jax.random.normal(ks[3], (DH, D), jnp.float32) * sc(D), 'wk_b': jax.random.normal(ks[4], (DH,), jnp.float32) * 0.01, 'wv_w': jax.random.normal(ks[5], (DH, D), jnp.float32) * sc(D), 'wv_b': jax.random.normal(ks[6], (DH,), jnp.float32) * 0.01, 'dense_w': jax.random.normal(ks[7], (D, DH), jnp.float32) * sc(DH), 'dense_b': jax.random.normal(ks[8], (D,), jnp.float32) * 0.01}
    _L3_attn_all = _L3_attn_setup()
    _L3_attn_in = {k: v for k, v in _L3_attn_all.items() if k in ('mask', 'wq_w', 'wq_b', 'wk_w', 'wk_b', 'wv_w', 'wv_b', 'dense_w', 'dense_b')}
    del _L3_attn_all

    def _L3_ffn_setup():
        import jax, jax.numpy as jnp
        import numpy as np
        PADDED_SL = 2048
        TEMPERATURE = 1.0
        SIGMA_POW = 0.25

        def _stu_conv(phi, u, n):
            b, sl, d = u.shape
            sgn = jnp.where(jnp.arange(sl) % 2 == 0, 1.0, -1.0).astype(u.dtype)
            sgn3 = sgn[None, :, None]
            Vf = jnp.fft.rfft(phi, n=n, axis=0)
            Uf_p = jnp.fft.rfft(u, n=n, axis=1)
            Uf_m = jnp.fft.rfft(u * sgn3, n=n, axis=1)
            U_plus = jnp.fft.irfft(Vf[None, :, :, None] * Uf_p[:, :, None, :], n=n, axis=1)[:, :sl]
            U_minus = jnp.fft.irfft(Vf[None, :, :, None] * Uf_m[:, :, None, :], n=n, axis=1)[:, :sl]
            U_minus = U_minus * sgn[None, :, None, None]
            return (U_plus, U_minus)

        def _compute_spectral(u, sigma, phi, Mpp, Mpm):
            U_plus, U_minus = _stu_conv(phi, u, PADDED_SL)
            s = sigma ** SIGMA_POW
            out = jnp.einsum('btkd,k,kde->bte', U_plus, s, Mpp)
            out = out + jnp.einsum('btkd,k,kde->bte', U_minus, s, Mpm)
            return out

        def _compute_ar_u(Mu, u):
            sl = u.shape[1]
            out = jnp.zeros(u.shape[:2] + (Mu.shape[-1],), dtype=u.dtype)
            for i in range(Mu.shape[0]):
                ui = jnp.pad(u, ((0, 0), (i, 0), (0, 0)))[:, :sl]
                out = out + jnp.einsum('btd,de->bte', ui, Mu[i])
            return out

        def _stu(u, sigma, phi, Mu, Mpp, Mpm):
            return _compute_spectral(u, sigma, phi, Mpp, Mpm) + _compute_ar_u(Mu, u)
        key = jax.random.key(seed)
        ks = jax.random.split(key, 8)
        b, sl, d, K, k_u = (2, 1024, 32, 16, 3)
        x = jax.random.normal(ks[0], (b, sl, d), dtype=jnp.float32)
        sigma = jax.random.uniform(ks[1], (K,), dtype=jnp.float32, minval=0.001, maxval=1.0)
        phi = jax.random.normal(ks[2], (sl, K), dtype=jnp.float32) / np.sqrt(sl)
        M_u = jax.random.normal(ks[3], (4, k_u, d, d), dtype=jnp.float32) * 0.02
        M_phi_plus = jax.random.normal(ks[4], (4, K, d, d), dtype=jnp.float32) * 0.02
        M_phi_minus = jax.random.normal(ks[5], (4, K, d, d), dtype=jnp.float32) * 0.02
        log_weights = jnp.ones((4,), dtype=jnp.float32)
        u01 = jax.random.uniform(ks[6], (4,), dtype=jnp.float32, minval=1e-06, maxval=1.0 - 1e-06)
        gumbel = -jnp.log(-jnp.log(u01))
        return {'x': x, 'sigma': sigma, 'phi': phi, 'M_u': M_u, 'M_phi_plus': M_phi_plus, 'M_phi_minus': M_phi_minus, 'log_weights': log_weights, 'gumbel': gumbel}
    _L3_ffn_all = _L3_ffn_setup()
    _L3_ffn_in = {k: v for k, v in _L3_ffn_all.items() if k in ('sigma', 'phi', 'M_u', 'M_phi_plus', 'M_phi_minus', 'log_weights', 'gumbel')}
    del _L3_ffn_all
    return {'x': x, 'L0_conv_w_qkv': _L0_conv_in['w_qkv'], 'L0_conv_b_qkv': _L0_conv_in['b_qkv'], 'L0_conv_w_dw': _L0_conv_in['w_dw'], 'L0_conv_b_dw': _L0_conv_in['b_dw'], 'L0_conv_pconv_off_w': _L0_conv_in['pconv_off_w'], 'L0_conv_w_off': _L0_conv_in['w_off'], 'L0_conv_b_off': _L0_conv_in['b_off'], 'L0_conv_pconv_mask_w': _L0_conv_in['pconv_mask_w'], 'L0_conv_w_mask': _L0_conv_in['w_mask'], 'L0_conv_b_mask': _L0_conv_in['b_mask'], 'L0_conv_w_proj': _L0_conv_in['w_proj'], 'L0_conv_b_proj': _L0_conv_in['b_proj'], 'L1_conv_reduction_kernel': _L1_conv_in['reduction_kernel'], 'L1_conv_attention_kernel': _L1_conv_in['attention_kernel'], 'L1_conv_conv_kernels': _L1_conv_in['conv_kernels'], 'L1_conv_bias': _L1_conv_in['bias'], 'L1_conv_bn_scale': _L1_conv_in['bn_scale'], 'L1_conv_bn_bias': _L1_conv_in['bn_bias'], 'L1_conv_bn_mean': _L1_conv_in['bn_mean'], 'L1_conv_bn_var': _L1_conv_in['bn_var'], 'L2_attn_Wq': _L2_attn_in['Wq'], 'L2_attn_Wk': _L2_attn_in['Wk'], 'L2_attn_Wv': _L2_attn_in['Wv'], 'L2_ffn_router_w': _L2_ffn_in['router_w'], 'L2_ffn_router_b': _L2_ffn_in['router_b'], 'L2_ffn_expert_w': _L2_ffn_in['expert_w'], 'L2_ffn_expert_b': _L2_ffn_in['expert_b'], 'L3_attn_mask': _L3_attn_in['mask'], 'L3_attn_wq_w': _L3_attn_in['wq_w'], 'L3_attn_wq_b': _L3_attn_in['wq_b'], 'L3_attn_wk_w': _L3_attn_in['wk_w'], 'L3_attn_wk_b': _L3_attn_in['wk_b'], 'L3_attn_wv_w': _L3_attn_in['wv_w'], 'L3_attn_wv_b': _L3_attn_in['wv_b'], 'L3_attn_dense_w': _L3_attn_in['dense_w'], 'L3_attn_dense_b': _L3_attn_in['dense_b'], 'L3_ffn_sigma': _L3_ffn_in['sigma'], 'L3_ffn_phi': _L3_ffn_in['phi'], 'L3_ffn_M_u': _L3_ffn_in['M_u'], 'L3_ffn_M_phi_plus': _L3_ffn_in['M_phi_plus'], 'L3_ffn_M_phi_minus': _L3_ffn_in['M_phi_minus'], 'L3_ffn_log_weights': _L3_ffn_in['log_weights'], 'L3_ffn_gumbel': _L3_ffn_in['gumbel']}

def reference(x, L0_conv_w_qkv, L0_conv_b_qkv, L0_conv_w_dw, L0_conv_b_dw, L0_conv_pconv_off_w, L0_conv_w_off, L0_conv_b_off, L0_conv_pconv_mask_w, L0_conv_w_mask, L0_conv_b_mask, L0_conv_w_proj, L0_conv_b_proj, L1_conv_reduction_kernel, L1_conv_attention_kernel, L1_conv_conv_kernels, L1_conv_bias, L1_conv_bn_scale, L1_conv_bn_bias, L1_conv_bn_mean, L1_conv_bn_var, L2_attn_Wq, L2_attn_Wk, L2_attn_Wv, L2_ffn_router_w, L2_ffn_router_b, L2_ffn_expert_w, L2_ffn_expert_b, L3_attn_mask, L3_attn_wq_w, L3_attn_wq_b, L3_attn_wk_w, L3_attn_wk_b, L3_attn_wv_w, L3_attn_wv_b, L3_attn_dense_w, L3_attn_dense_b, L3_ffn_sigma, L3_ffn_phi, L3_ffn_M_u, L3_ffn_M_phi_plus, L3_ffn_M_phi_minus, L3_ffn_log_weights, L3_ffn_gumbel):
    import jax
    import jax.numpy as jnp

    def _L0_conv_ref(x, w_qkv, b_qkv, w_dw, b_dw, pconv_off_w, w_off, b_off, pconv_mask_w, w_mask, b_mask, w_proj, b_proj):
        import jax, jax.numpy as jnp
        import numpy as np
        B, H, W, C = (4, 16, 16, 32)
        G = 4
        HC = C // G
        K = 3
        K2 = K * K
        PAD = K // 2
        SCALE = HC ** (-0.5)

        def conv2d(x, w, padding=1, dilation=1, groups=1):
            return jax.lax.conv_general_dilated(x, w, (1, 1), [(padding, padding), (padding, padding)], rhs_dilation=(dilation, dilation), dimension_numbers=('NCHW', 'OIHW', 'NCHW'), feature_group_count=groups)

        def pconv(x, w):
            c4 = w.shape[0]
            return jnp.concatenate([conv2d(x[:, :c4], w, padding=1), x[:, c4:]], axis=1)

        def conv1x1(x, w, b):
            return jnp.einsum('bchw,oc->bohw', x, w) + b[None, :, None, None]

        def deform_sample(img, offset, mask, dilation, pad):
            b, cg, h, w = img.shape
            ky, kx = jnp.meshgrid(jnp.arange(K), jnp.arange(K), indexing='ij')
            base_y = (ky.reshape(-1) * dilation - pad).astype(img.dtype)
            base_x = (kx.reshape(-1) * dilation - pad).astype(img.dtype)
            off = offset.reshape(b, K2, 2, h, w)
            py = jnp.arange(h, dtype=img.dtype)[None, None, :, None] + base_y[None, :, None, None] + off[:, :, 0]
            px = jnp.arange(w, dtype=img.dtype)[None, None, None, :] + base_x[None, :, None, None] + off[:, :, 1]
            y0 = jnp.floor(py)
            x0 = jnp.floor(px)
            wy = py - y0
            wx = px - x0
            flat = img.reshape(b, cg, h * w)

            def gather(iy, ix):
                valid = ((iy >= 0) & (iy < h) & (ix >= 0) & (ix < w)).astype(img.dtype)
                idx = (jnp.clip(iy, 0, h - 1) * w + jnp.clip(ix, 0, w - 1)).astype(jnp.int32)
                g = jax.vmap(lambda f, i: jnp.take(f, i, axis=1))(flat, idx.reshape(b, -1))
                return g.reshape(b, cg, K2, h, w) * valid[:, None]
            wy_ = wy[:, None]
            wx_ = wx[:, None]
            out = gather(y0, x0) * (1 - wy_) * (1 - wx_) + gather(y0, x0 + 1) * (1 - wy_) * wx_ + gather(y0 + 1, x0) * wy_ * (1 - wx_) + gather(y0 + 1, x0 + 1) * wy_ * wx_
            return out * mask[:, None]
        b, h, w, c = x.shape
        n = h * w
        qkv = x @ w_qkv + b_qkv
        qkv = conv2d(qkv.transpose(0, 3, 1, 2), w_dw, padding=1, groups=3 * c) + b_dw[None, :, None, None]
        qkv = qkv.transpose(0, 2, 3, 1)
        q = qkv[..., :c]
        kv = qkv[..., c:].reshape(b, h, w, 2, G, HC).transpose(3, 0, 4, 5, 1, 2)
        q_img = q.transpose(0, 3, 1, 2)
        mask = jax.nn.sigmoid(conv1x1(pconv(q_img, pconv_mask_w), w_mask, b_mask))
        k_list, v_list = ([], [])
        for i in range(G):
            off = conv1x1(pconv(q_img, pconv_off_w[i]), w_off[i], b_off[i])
            dil = 2 * i + 1
            k_list.append(deform_sample(kv[0, :, i], off, mask, dil, dil * PAD))
            v_list.append(deform_sample(kv[1, :, i], off, mask, dil, dil * PAD))
        ks_ = jnp.stack(k_list, 1).reshape(b, G, HC, K2, n)
        vs_ = jnp.stack(v_list, 1).reshape(b, G, HC, K2, n)
        qf = (q.reshape(b, n, G, HC) * SCALE).transpose(0, 2, 1, 3)
        attn = jax.nn.softmax(jnp.einsum('bgnc,bgckn->bgnk', qf, ks_), axis=-1)
        out = jnp.einsum('bgnk,bgckn->bgnc', attn, vs_)
        out = out.transpose(0, 2, 1, 3).reshape(b, h, w, c)
        return out @ w_proj + b_proj

    def _L1_conv_ref(x, reduction_kernel, attention_kernel, conv_kernels, bias, bn_scale, bn_bias, bn_mean, bn_var):
        import jax, jax.numpy as jnp
        import numpy as np
        from jax import lax
        TEMPERATURE = 30.0
        BN_EPS = 1e-05
        B = x.shape[0]
        pool = jnp.mean(x, axis=(1, 2))
        pool_red = jax.nn.relu(pool @ reduction_kernel)
        attention = jax.nn.softmax(pool_red @ attention_kernel / TEMPERATURE, axis=-1)
        w_mixed = jnp.einsum('bk,khwio->bhwio', attention, conv_kernels)

        def per_sample_conv(xi, wi):
            return lax.conv_general_dilated(xi[None], wi, window_strides=(1, 1), padding='SAME', dimension_numbers=('NHWC', 'HWIO', 'NHWC'))[0]
        y = jax.vmap(per_sample_conv)(x, w_mixed)
        b_mixed = attention @ bias
        y = y + b_mixed[:, None, None, :]
        inv = bn_scale * lax.rsqrt(bn_var + BN_EPS)
        y = (y - bn_mean) * inv + bn_bias
        return jax.nn.relu(y)

    def _L2_attn_ref(query, Wq, Wk, Wv):
        import jax, jax.numpy as jnp
        import numpy as np
        NEG = -1000000000000.0
        q = jnp.einsum('btd,du->btu', query, Wq)
        k = jnp.einsum('btd,du->btu', query, Wk)
        v = jnp.einsum('btd,du->btu', query, Wv)
        T = v.shape[1]
        scores = jnp.einsum('bqu,bku->bqk', q, k) / jnp.sqrt(jnp.asarray(T, jnp.float32))
        causal = jnp.tril(jnp.ones((T, T), dtype=jnp.float32))
        scores = scores + NEG * (1.0 - causal)
        attn = jax.nn.softmax(scores, axis=-1)
        context = jnp.einsum('bqk,bku->bqu', attn, v)
        return context

    def _L2_ffn_ref(x, router_w, router_b, expert_w, expert_b):
        import jax, jax.numpy as jnp
        import numpy as np
        B, N, D, C, E, K = (8, 2048, 32, 32, 8, 2)
        router_probs = jax.nn.softmax(x @ router_w + router_b, axis=-1)
        top_p, top_i = jax.lax.top_k(router_probs, K)
        top_p = top_p / jnp.sum(top_p, axis=-1, keepdims=True)
        expert_out = jnp.einsum('bnd,edc->bnec', x, expert_w) + expert_b
        gathered = jnp.take_along_axis(expert_out, top_i[..., None], axis=2)
        return jnp.einsum('bnk,bnkc->bnc', top_p, gathered)

    def _L3_attn_ref(x, mask, wq_w, wq_b, wk_w, wk_b, wv_w, wv_b, dense_w, dense_b):
        import jax, jax.numpy as jnp
        import numpy as np
        B, S, D, H = (4, 1024, 32, 16)
        DH = D * H
        b, s, d = x.shape
        h = wq_w.shape[0] // d
        q = (x @ wq_w.T + wq_b).reshape(b, s, h, d)
        k = (x @ wk_w.T + wk_b).reshape(b, s, h, d)
        v = (x @ wv_w.T + wv_b).reshape(b, s, h, d)
        q = jax.nn.elu(q) + 1.0
        k = jax.nn.elu(k) + 1.0
        pos = 1.57 * jnp.arange(s, dtype=x.dtype) / s
        cos = jnp.cos(pos)[None, :, None, None]
        sin = jnp.sin(pos)[None, :, None, None]
        q_cos, q_sin = (q * cos, q * sin)
        k_cos, k_sin = (k * cos, k * sin)
        kv_cos = jnp.einsum('bshx,bshz->bhxz', k_cos, v)
        kv_sin = jnp.einsum('bshx,bshz->bhxz', k_sin, v)
        qkv = jnp.einsum('bshx,bhxz->bshz', q_cos, kv_cos) + jnp.einsum('bshx,bhxz->bshz', q_sin, kv_sin)
        denom = 1.0 / (jnp.einsum('bshd,bhd->bsh', q_cos, k_cos.sum(axis=1)) + jnp.einsum('bshd,bhd->bsh', q_sin, k_sin.sum(axis=1)) + 1e-05)
        o = qkv * denom[..., None]
        concat = o.reshape(b, s, h * d)
        return concat @ dense_w.T + dense_b

    def _L3_ffn_ref(x, sigma, phi, M_u, M_phi_plus, M_phi_minus, log_weights, gumbel):
        import jax, jax.numpy as jnp
        import numpy as np
        PADDED_SL = 2048
        TEMPERATURE = 1.0
        SIGMA_POW = 0.25

        def _stu_conv(phi, u, n):
            b, sl, d = u.shape
            sgn = jnp.where(jnp.arange(sl) % 2 == 0, 1.0, -1.0).astype(u.dtype)
            sgn3 = sgn[None, :, None]
            Vf = jnp.fft.rfft(phi, n=n, axis=0)
            Uf_p = jnp.fft.rfft(u, n=n, axis=1)
            Uf_m = jnp.fft.rfft(u * sgn3, n=n, axis=1)
            U_plus = jnp.fft.irfft(Vf[None, :, :, None] * Uf_p[:, :, None, :], n=n, axis=1)[:, :sl]
            U_minus = jnp.fft.irfft(Vf[None, :, :, None] * Uf_m[:, :, None, :], n=n, axis=1)[:, :sl]
            U_minus = U_minus * sgn[None, :, None, None]
            return (U_plus, U_minus)

        def _compute_spectral(u, sigma, phi, Mpp, Mpm):
            U_plus, U_minus = _stu_conv(phi, u, PADDED_SL)
            s = sigma ** SIGMA_POW
            out = jnp.einsum('btkd,k,kde->bte', U_plus, s, Mpp)
            out = out + jnp.einsum('btkd,k,kde->bte', U_minus, s, Mpm)
            return out

        def _compute_ar_u(Mu, u):
            sl = u.shape[1]
            out = jnp.zeros(u.shape[:2] + (Mu.shape[-1],), dtype=u.dtype)
            for i in range(Mu.shape[0]):
                ui = jnp.pad(u, ((0, 0), (i, 0), (0, 0)))[:, :sl]
                out = out + jnp.einsum('btd,de->bte', ui, Mu[i])
            return out

        def _stu(u, sigma, phi, Mu, Mpp, Mpm):
            return _compute_spectral(u, sigma, phi, Mpp, Mpm) + _compute_ar_u(Mu, u)
        T = x.shape[1]
        outs = []
        for i, frac in enumerate((1, 2, 4, 8)):
            xi = x[:, :T // frac]
            si = _stu(xi, sigma, phi, M_u[i], M_phi_plus[i], M_phi_minus[i])
            si = jnp.pad(si, ((0, 0), (0, T - si.shape[1]), (0, 0)))
            outs.append(si)
        y_soft = jax.nn.softmax((log_weights + gumbel) / TEMPERATURE)
        y_hard = jax.nn.one_hot(jnp.argmax(y_soft), 4, dtype=y_soft.dtype)
        weights = y_hard - jax.lax.stop_gradient(y_soft) + y_soft
        stacked = jnp.stack(outs, axis=-1)
        return jnp.sum(stacked * weights, axis=-1)

    def _gn(v, G=32, eps=1e-05):
        B_, H_, W_, C_ = v.shape
        g = v.reshape(B_, H_, W_, G, C_ // G)
        m = jnp.mean(g, axis=(1, 2, 4), keepdims=True)
        s = jnp.var(g, axis=(1, 2, 4), keepdims=True)
        return ((g - m) / jnp.sqrt(s + eps)).reshape(v.shape)

    def _ln_c(v, eps=1e-06):
        m = jnp.mean(v, axis=-1, keepdims=True)
        s = jnp.var(v, axis=-1, keepdims=True)
        return (v - m) / jnp.sqrt(s + eps)

    def _ln_t(v, eps=1e-05):
        m = jnp.mean(v, axis=-1, keepdims=True)
        s = jnp.var(v, axis=-1, keepdims=True)
        return (v - m) / jnp.sqrt(s + eps)

    def _to_tokens(v):
        B_, H_, W_, C_ = v.shape
        return v.reshape(B_, H_ * W_, C_)

    def _from_tokens(t, like):
        return t.reshape(like.shape)
    x = x + _L0_conv_ref(_gn(x), L0_conv_w_qkv, L0_conv_b_qkv, L0_conv_w_dw, L0_conv_b_dw, L0_conv_pconv_off_w, L0_conv_w_off, L0_conv_b_off, L0_conv_pconv_mask_w, L0_conv_w_mask, L0_conv_b_mask, L0_conv_w_proj, L0_conv_b_proj)
    x = x + _L1_conv_ref(_gn(x), L1_conv_reduction_kernel, L1_conv_attention_kernel, L1_conv_conv_kernels, L1_conv_bias, L1_conv_bn_scale, L1_conv_bn_bias, L1_conv_bn_mean, L1_conv_bn_var)
    t = _to_tokens(x)
    t = t + _L2_attn_ref(_ln_t(t), L2_attn_Wq, L2_attn_Wk, L2_attn_Wv)
    t = t + _L2_ffn_ref(_ln_t(t), L2_ffn_router_w, L2_ffn_router_b, L2_ffn_expert_w, L2_ffn_expert_b)
    t = t + _L3_attn_ref(_ln_t(t), L3_attn_mask, L3_attn_wq_w, L3_attn_wq_b, L3_attn_wk_w, L3_attn_wk_b, L3_attn_wv_w, L3_attn_wv_b, L3_attn_dense_w, L3_attn_dense_b)
    t = t + _L3_ffn_ref(_ln_t(t), L3_ffn_sigma, L3_ffn_phi, L3_ffn_M_u, L3_ffn_M_phi_plus, L3_ffn_M_phi_minus, L3_ffn_log_weights, L3_ffn_gumbel)
    x = _from_tokens(t, x)
    return x

_drawn_inputs = setup_inputs


def setup_inputs(seed=0):
    import zlib

    import numpy as np

    out = dict(_drawn_inputs(seed))
    spreads = {'L2_ffn_router_b': (0.0, 0.1),
     'L2_ffn_expert_b': (0.0, 0.1),
     'L3_ffn_log_weights': (1.0, 0.2)}
    factors = {'L0_conv_pconv_off_w': 2.979,
     'L0_conv_pconv_mask_w': 8.0,
     'L3_attn_wq_w': 4.958,
     'L3_attn_wq_b': 8.0,
     'L3_attn_wk_b': 8.0,
     'L3_attn_wv_b': 7.193,
     'L3_attn_dense_b': 7.163}
    for name, (base, spread) in spreads.items():
        noise = np.random.default_rng([zlib.crc32(name.encode()), seed]).standard_normal(out[name].shape)
        drawn = base * np.exp(spread * noise) if base else spread * noise
        out[name] = jnp.asarray(drawn.astype(out[name].dtype))
    for name, factor in factors.items():
        out[name] = (out[name] * factor).astype(out[name].dtype)
    return out
```

```python
from contextlib import ExitStack

import concourse.bass as bass
from concourse import mybir

F32 = mybir.dt.float32
BF16 = mybir.dt.bfloat16
ALU = mybir.AluOpType
ACT = mybir.ActivationFunctionType
AX = mybir.AxisListType

P = 128
B, H, W, C = 4, 16, 16, 32
N = H * W
NH = N // P
T = B * NH
G, HC, K2 = 4, 8, 9
J = G * K2
NOFF = J * 2 + K2
KV = 2 * HC
SLOT = 4 * KV
HP, WP = H + 2, W + 2
E = 8
NHEAD, D = 16, 32
HG = NHEAD * D // P
NF = 16
KU = 3
NSC = 4
STU = 2 * NF * D + KU * D
ROUND = 1.5 * 2.0 ** 23
BANK = 512

CST = (("ident", P), ("bmask", B), ("base", NH * 2 * J), ("boff", NOFF), ("pidx", 2), ("cs", 2 * NH),
       ("sgn", 1), ("tokidx", NH), ("lt4", 16), ("lt8", 64), ("neghalf", 8), ("quarter", NF), ("frac", NSC),
       ("gumbel", NSC), ("logw", NSC))
FRONT = (("wqkv", 3 * P), ("wdw", 27), ("bqkv", 3), ("bdw", 3))
L1 = (("wproj", P), ("bproj", 1), ("red", 4), ("convk", 4 * K2 * C), ("kbias", 4), ("bnscale", 1),
      ("bnbias", 1), ("bnmean", 1), ("bnvar", 1))
L2 = (("wq", P), ("wk", P), ("wv", P), ("causal", 3 * P))
L3 = (("dense", HG * D), ("blocks", P), ("denseb", D))


def width(block):
    return sum(n for _, n in block)


def columns(tensor, block):
    out, at = {}, 0
    for name, n in block:
        out[name] = tensor[:, at:at + n]
        at += n
    return out


class Steps:

    def __init__(self, semaphore, names):
        self.sem, self.names, self.said = semaphore, names.split(), 0

    def __getitem__(self, name):
        return self.names.index(name) + 1

    def step(self, name):
        assert self.names[self.said] == name, (self.names[self.said], name)
        self.said += 1
        return 1


def hybrid(nc, x_ch, cst_d, front_d, pw_d, l1_d, attk_d, l2_d, moe_d, l3w_d, l3_d, ex_d, stu_d, toep_d, out, DBG=()):
    with ExitStack() as ctx:
        def sb(name, shape, dt=F32):
            return ctx.enter_context(nc.sbuf_tensor(name, shape, dt))

        def sem(name):
            return ctx.enter_context(nc.semaphore(name))

        x = sb("x", [P, N])
        cst = sb("cst", [P, width(CST)])
        front = sb("front", [P, width(FRONT)])
        aug = sb("aug", [C + 1, T * P])[:]
        l1 = sb("l1", [P, width(L1)])
        attk = sb("attk", [4, 4])
        l2 = sb("l2", [P, width(L2)])
        moe = sb("moe", [C + 1, E * C + E])
        l3w = sb("l3w", [C + 1, 3 * NHEAD * D])
        l3 = sb("l3", [P, width(L3)])
        ex = sb("ex", [NHEAD, HG * P])
        stu_fq = sb("stu_fq", [P, NSC * STU + NF])
        stu, fq = stu_fq[0:D, :], stu_fq[:, 0:4096]
        c, f, p1, p2, p3 = columns(cst, CST), columns(front, FRONT), columns(l1, L1), columns(l2, L2), columns(l3, L3)
        ident = c["ident"]
        identb = sb("identb", [P, P], BF16)
        neg1 = sb("neg1", [P, 1])
        pos1 = sb("pos1", [P, 1])

        stats = sb("stats", [P, 6])
        moments = sb("moments", [P, 2])
        var_eps = sb("var_eps", [P, T])
        rstd = sb("rstd", [P, T])
        bn_var_eps = sb("bn_var_eps", [P, 1])
        bn_inv = sb("bn_inv", [P, 1])
        xg = sb("xg", [P, N])
        qkv_pad = sb("qkv_pad", [P, 3 * HP * WP])
        q_flat = sb("q_flat", [P, 3 * (N + 2 * (W + 1))])
        kv = sb("kv", [P, 2 * (N + WP)])
        comp = sb("comp", [P, K2 * NOFF])
        q_tok = sb("q_tok", [P, T * C])
        base = sb("base_b", [P, NH * 2 * J])
        w4 = sb("w4", [P, T * J * 4])
        gate_m = sb("gate_m", [P, T * K2])
        mask_x = sb("mask_x", [P, T * J])
        index = sb("index", [P, T * J], BF16)
        table = sb("table", [P, 2 * 3 * B * G * SLOT], BF16)
        indexb = sb("indexb", [P, 2 * J * P], BF16)
        onehot = sb("onehot", [P, 2 * 2 * J * P], BF16)
        arena = sb("arena", [P, 15296])
        dots = sb("dots", [P, NH * J * 4])
        logit = sb("logit", [P, NH * J])
        peak = sb("peak", [P, NH * G])
        pexp = sb("pexp", [P, NH * J])
        psum_ = sb("psum_", [P, NH * G])
        pinv = sb("pinv", [P, NH * G])
        w4p = sb("w4p", [P, NH * J * 4])
        mixed = sb("mixed", [P, NH * C])
        att = sb("att", [P, T * C])
        x1 = sb("x1", [P, N])
        x1_pad = sb("x1_pad", [P, HP * WP])
        pool = sb("pool", [P, 1])
        pool_bd = sb("pool_bd", [P, B])
        pool_red = sb("pool_red", [4, P])
        kmax = sb("kmax", [P, 1])
        kexp = sb("kexp", [P, 4])
        ksum_ = sb("ksum_", [P, 1])
        kinv = sb("kinv", [P, 1])
        katt = sb("katt", [P, 4])
        bmix = sb("bmix", [P, 4])
        bsum = sb("bsum", [P, 1])
        bshift = sb("bshift", [P, 1])
        x2t = xg
        lsum = sb("lsum", [P, T])
        lneg = sb("lneg", [P, T])
        lvar = sb("lvar", [P, T])
        ln = sb("ln", [P, T * C])
        smax = sb("smax", [P, T])
        ssum = sb("ssum", [P, T])
        sinv = sb("sinv", [P, T])
        rlog = sb("rlog", [P, T * E])
        rank = sb("rank", [P, T * E])
        chosen = sb("chosen", [P, T * E])
        rmax = sb("rmax", [P, T])
        rexp = sb("rexp", [P, T * E])
        rsum = sb("rsum", [P, T])
        ks_bd = sb("ks_bd", [P, 16 * 4 * 2])
        ks_sb = sb("ks_sb", [P, 16 * 2])
        zsel = sb("zsel", [P, NSC])
        zmax = sb("zmax", [P, 1])
        zsum = sb("zsum", [P, 1])
        soft = sb("soft", [P, NSC])
        zgt = sb("zgt", [P, NSC * NSC])
        zeq = sb("zeq", [P, NSC * NSC])
        hard = sb("hard", [P, NSC])
        wsel = sb("wsel", [P, NSC])
        length = sb("length", [P, 1])
        window = sb("window", [P, NH])
        winsgn = sb("winsgn", [P, NH])
        sig4 = sb("sig4", [D, NF])
        msel = sb("msel", [D, STU])

        gath = arena[:, 0:2 * NH * J * SLOT]
        fk, vcos, vsin = (arena[:, i * 4096:(i + 1) * 4096] for i in range(3))
        den_t = vcos[0:NHEAD, 0:T * P]
        vv, toep = arena[:, 0:NF * BANK], vsin
        att_ch, y1, x2, ctx_n, qc, kc, vt, ln_ch, x4d, stu_m = (
            arena[:, 12288 + i * N:12288 + (i + 1) * N] for i in range(10))
        side = 2 * NH * J * SLOT
        pos, near, away, hat0, hat1 = (arena[:, side + i * T * 2 * J:side + (i + 1) * T * 2 * J] for i in range(5))
        prod = arena[:, side:side + NH * J * 4 * HC]
        side += 5 * T * 2 * J
        hats = arena[:, side:side + 2 * T * 2 * J]
        side += 2 * T * 2 * J
        rest = arena[:, side:side + 4 * BANK]
        mpart = arena[0:D, side:side + STU]
        late = onehot[:].bitcast(F32)
        pw = late[0:C, 0:5 * K2 * P + NOFF]
        kv_t, gated = late[:, 0:4096], late[:, 4096:4096 + T * C * E]
        req, shifted = late[:, 0:T * E * E], late[0:D, 4096:4096 + B * (N + KU - 1)]
        prob, prob_t = late[:, 6144:6144 + B * 3 * P], late[:, 7680:7680 + B * 3 * P]
        late3 = table[:].bitcast(F32)
        sm, den, wmix = late3[0:D, 0:2 * NF * D], late3[:, 2048:2048 + T * NHEAD], late3[:, 2304:2304 + K2 * C]
        x3t, x4t, x5t, x6t = (late3[:, 1024 + i * N:1024 + (i + 1) * N] for i in range(4))
        lcen, lsq = comp[:, 0:T * C], comp[:, T * C:2 * T * C]
        late2 = indexb[:].bitcast(F32)
        score, mcs, den2 = late2[:, 0:1536], late2[:, 1536:2560], late2[:, 2560:2816]
        wmix_bd, rgt = late2[:, 2816:2816 + K2 * P], late2[:, 3968:3968 + T * E * E]

        ps = ctx.enter_context(nc.psum_tensor("ps", [P, 8, BANK], F32))

        d_x, d_cst, d_front, d_pw, d_l1, d_l2, d_moe, d_l3, d_stu, d_toep, d_out = (
            sem("loaded_" + n) for n in ("x", "cst", "front", "pw", "l1", "l2", "moe", "l3", "stu", "toep", "out"))

        v0 = Steps(sem("vector_front"), "identb neg1 pos1 ones base stats moments eps xg "
                   + " ".join(f"q{t}" for t in range(K2)) + " shift0 shift2 "
                   + " ".join(f"k{t} v{t}" for t in range(K2))
                   + " pos clamp near0 near1 near index rest0 rest1 rest2 rest3 low0 low1 low2 low3"
                   + " away hat0a hat0 gate gate1 sigmoid maskx hatm w4")
        a0 = Steps(sem("scalar_front"), "comp0 comp1 q k v qtok high0 high1 high2 high3 mid0 mid1 mid2 mid3"
                   " sigexp hat1a hat1")
        t0 = Steps(sem("tensor_front"), "q k v comp qtok offsets table0 table1 table2 table3")
        g0 = Steps(sem("pool_steps"), "qkvpad qpad kvpad xpad rstd0 bnvar bninv sigma "
                   + " ".join(f"m{i} a{i}" for i in range(NSC)) + " sm"
                   + " rstd1 rstd2 rstd3 rstd4 shiftpad rstd5")
        s_bc = sem("index_spread")
        s_bce = sem("index_copied")
        s_oh = sem("onehot_ready")
        s_gp = sem("samples_in_psum")
        s_ge = sem("samples_copied")
        s_un = sem("unit_gathered")
        PAIR = ("prodk dots wdots logit peak sub expsum inv w4p prodv mixed att").split()
        v1 = Steps(sem("vector_pairs"), " ".join(f"{n}{b}" for b in range(B) for n in PAIR))
        s_px = sem("attention_exp")

        t2 = Steps(sem("tensor_conv"), "attT proj poolred katt conv x2T")
        a2 = Steps(sem("scalar_conv"), "attT poolred kexp y1")
        v2 = Steps(sem("vector_conv"), "x1 stats moments eps xpad pool poolbd kmax kneg kinv katt mix0 mix1 mix2 mix3"
                   " mixbd bmix bsum binv bcent bshift x2 x2t")
        LN = "sum neg cen sq var eps ln "
        v3 = Steps(sem("vector_attn"), LN + "kc score smax0 smax1 sneg sinv pt1 pt3 ctx x3")
        a3 = Steps(sem("scalar_attn"), "lnT qc vt " + " ".join(f"exp{t}" for t in range(T)) + " pt0 pt2")
        t3 = Steps(sem("tensor_attn"), "lnT qc kc vt score pt0 pt1 pt2 pt3 pv")
        v4 = Steps(sem("vector_moe"), LN + "aug1 rlog rgt req reqlt rsum rank rmax rsub chosen esel esum einv gated y ynorm x4")
        a4 = Steps(sem("scalar_moe"), "aug0 rexp")
        t4 = Steps(sem("tensor_moe"), "aug0 aug1 router experts")
        v5 = Steps(sem("vector_linear"), LN + "aug1 "
                   + " ".join(f"fk{t}" for t in range(T)) + " " + " ".join(f"fq{i}" for i in range(8))
                   + " " + " ".join(f"kvt{i}" for i in range(8)) + " ksb den20 den21 den deneps deninv"
                   + " " + " ".join(f"qn{i}" for i in range(8)) + " cos0 cos1 bias sin0 x5")
        a5 = Steps(sem("scalar_linear"), "aug0 " + " ".join(f"ek{t} vc{t} vs{t}" for t in range(T)) + " "
                   + " ".join(f"eq{i}" for i in range(8)) + " ks mcs0 mcs1 denT0 denT1")
        t5 = Steps(sem("tensor_linear"), "aug0 aug1 " + " ".join(f"k{t} v{t}" for t in range(T)) + " "
                   + " ".join(f"q{i}" for i in range(8)) + " "
                   + " ".join(f"kv{i}" for i in range(8)) + " ks mcs den denT "
                   + " ".join(f"qn{i}" for i in range(8)) + " out")
        vz = Steps(sem("vector_select"), "z zmax zneg zinv soft zgt zeq zeqlt zadd rank hard diff w lenp length win winsgn lbias")
        az = Steps(sem("scalar_select"), "exp")
        v6 = Steps(sem("vector_stu"), LN + "aug1 " + " ".join(f"vm{t}" for t in range(T)) + " m0 m1 y0 y1 x6")
        a6 = Steps(sem("scalar_stu"), "aug0 " + " ".join(f"vp{t}" for t in range(T)))
        t6 = Steps(sem("tensor_stu"), "aug0 aug1 " + " ".join(f"v{t}" for t in range(T)) + " out")

        block = ctx.enter_context(nc.Block())

        img = lambda ap: ap.rearrange("p (y x) -> p y x", y=H)
        qkvp = qkv_pad[:].rearrange("p (j y x) -> p j y x", j=3, y=HP)
        qf = q_flat[:].rearrange("p (v n) -> p v n", v=3)
        q_mid = qf[:, 1, W + 1:W + 1 + N]
        xp = x1_pad[:].rearrange("p (y x) -> p y x", y=HP)
        kvv = kv[:].rearrange("p (j n) -> p j n", j=2)
        compv = comp[:].rearrange("p (t n) -> p t n", t=K2)
        tabv = table[:].rearrange("p (q r s k d) -> p q r s k d", q=2, r=3, s=B * G, k=4)
        ohv = onehot[:].rearrange("p (u q j n) -> p u q j n", u=2, q=2, j=J)
        ixb = indexb[:].rearrange("p (u j n) -> p u j n", u=2, j=J)
        gv = gath.rearrange("p (r s d) -> p r s d", r=2, s=NH * J)
        tok = lambda ap: ap.rearrange("p (t c) -> p t c", t=T)
        tokhb = lambda ap: ap.rearrange("p (h b c) -> p h b c", b=B, h=NH)
        augt = aug.rearrange("p (t n) -> p t n", t=T)
        sh = shifted.rearrange("p (b n) -> p b n", b=B)
        GRP = NH * J // 8

        def rep(ap, n):
            return ap.unsqueeze(len(ap.shape)).broadcast_to(list(ap.shape) + [n])

        @block.sync
        def _(sp):
            sp.dma_start(x[:], x_ch).then_inc(d_x, 16)
            sp.dma_start(front[:], front_d).then_inc(d_front, 16)
            sp.dma_start(pw, pw_d).then_inc(d_pw, 16)
            sp.dma_start(l1[:], l1_d).then_inc(d_l1, 16)
            sp.dma_start(attk[:], attk_d).then_inc(d_l1, 16)
            sp.dma_start(l2[:], l2_d).then_inc(d_l2, 16)
            sp.dma_start(moe[:], moe_d).then_inc(d_moe, 16)
            sp.dma_start(l3w[:], l3w_d).then_inc(d_l3, 16)
            sp.dma_start(l3[:], l3_d).then_inc(d_l3, 16)
            sp.dma_start(ex[:], ex_d).then_inc(d_l3, 16)
            sp.wait_ge(t5.sem, t5["ks"])
            sp.dma_start(toep, toep_d).then_inc(d_toep, 16)
            sp.wait_ge(v6.sem, v6["x6"])
            sp.dma_start(out, x6t).then_inc(d_out, 16)
            sp.wait_ge(d_out, 16)

        @block.gpsimd
        def _(pool_e):
            nc.gpsimd.memset(qkv_pad[:], 0.0).then_inc(g0.sem, g0.step("qkvpad"))
            nc.gpsimd.memset(q_flat[:], 0.0).then_inc(g0.sem, g0.step("qpad"))
            nc.gpsimd.memset(kv[:], 0.0).then_inc(g0.sem, g0.step("kvpad"))
            nc.gpsimd.memset(x1_pad[:], 0.0).then_inc(g0.sem, g0.step("xpad"))

            def power(out_ap, in_ap, exponent, name):
                nc.gpsimd.tensor_tensor(out=out_ap, in0=in_ap, in1=exponent, op=ALU.pow).then_inc(g0.sem, g0.step(name))

            pool_e.wait_ge(d_cst, 16)
            pool_e.wait_ge(v0.sem, v0["eps"])
            power(rstd[:, 0:1], var_eps[:, 0:1], c["neghalf"][:, 0:1], "rstd0")
            pool_e.wait_ge(d_l1, 32)
            nc.gpsimd.tensor_scalar(bn_var_eps[:], p1["bnvar"], 1e-5, None, ALU.add).then_inc(g0.sem, g0.step("bnvar"))
            pool_e.wait_ge(g0.sem, g0["bnvar"])
            power(bn_inv[:], bn_var_eps[:], c["neghalf"][:, 0:1], "bninv")
            pool_e.wait_ge(d_stu, 16)
            power(sig4[:], stu[:, NSC * STU:], c["quarter"][0:D, :], "sigma")
            pool_e.wait_ge(vz.sem, vz["w"])
            for i in range(NSC):
                dst = msel if i == 0 else mpart
                if i > 1:
                    pool_e.wait_ge(g0.sem, g0[f"a{i - 1}"])
                nc.gpsimd.tensor_scalar(dst[:], stu[:, i * STU:(i + 1) * STU], wsel[0:D, i:i + 1], None, ALU.mult)\
                    .then_inc(g0.sem, g0.step(f"m{i}"))
                pool_e.wait_ge(g0.sem, g0[f"m{i}"])
                if i == 0:
                    nc.gpsimd.memset(mpart, 0.0).then_inc(g0.sem, g0.step("a0"))
                    pool_e.wait_ge(g0.sem, g0["a0"])
                else:
                    nc.gpsimd.tensor_tensor(out=msel[:], in0=msel[:], in1=mpart, op=ALU.add)\
                        .then_inc(g0.sem, g0.step(f"a{i}"))
            pool_e.wait_ge(g0.sem, g0[f"a{NSC - 1}"])
            pool_e.wait_ge(s_un, T)
            nc.gpsimd.tensor_tensor(
                out=sm.rearrange("p (m k e) -> p m k e", m=2, k=NF),
                in0=msel[:, 0:2 * NF * D].rearrange("p (m k e) -> p m k e", m=2, k=NF),
                in1=rep(sig4[:].unsqueeze(1).broadcast_to([D, 2, NF]), D), op=ALU.mult).then_inc(g0.sem, g0.step("sm"))
            pool_e.wait_ge(v2.sem, v2["eps"])
            power(rstd[:, 0:1], var_eps[:, 0:1], c["neghalf"][:, 0:1], "rstd1")
            for i, v in enumerate((v3, v4, v5, v6)):
                pool_e.wait_ge(v.sem, v["eps"])
                power(rstd[:], var_eps[:], c["neghalf"], f"rstd{i + 2}")
                if v is v5:
                    nc.gpsimd.memset(shifted, 0.0).then_inc(g0.sem, g0.step("shiftpad"))

        @block.scalar
        def _(act):
            act.dma_start(cst[:], cst_d).then_inc(d_cst, 16)
            act.dma_start(stu, stu_d).then_inc(d_stu, 16)

            def copy(out_ap, in_ap, steps, name, scale=1.0):
                nc.scalar.activation(out_ap, in_ap, ACT.Copy, scale=scale).then_inc(steps.sem, steps.step(name))

            act.wait_ge(t0.sem, t0["comp"])
            copy(compv[:, 0:5, :].rearrange("p t n -> p (t n)"), ps[:, 6, 0:5 * NOFF], a0, "comp0")
            copy(compv[:, 5:9, :].rearrange("p t n -> p (t n)"), ps[:, 7, 0:4 * NOFF], a0, "comp1")
            act.wait_ge(g0.sem, g0["qkvpad"])
            act.wait_ge(d_front, 16)
            for j, (name, src) in enumerate((("q", ps[:, 0, 0:N]), ("k", ps[:, 0, N:2 * N]), ("v", ps[:, 1, 0:N]))):
                if j == 0:
                    act.wait_ge(t0.sem, t0["v"])
                nc.scalar.activation(qkvp[:, j, 1:1 + H, 1:1 + W], img(src), ACT.Identity, bias=f["bqkv"][:, j:j + 1])\
                    .then_inc(a0.sem, a0.step(name))
            act.wait_ge(t0.sem, t0["qtok"])
            copy(q_tok[:].rearrange("p (b h c) -> p h b c", b=B, h=NH),
                 ps[:, 1, N:2 * N].rearrange("p (h b c) -> p h b c", h=NH, b=B), a0, "qtok", HC ** -0.5)
            def tab(i, part):
                return tabv[:, i // 2, part, :, :, (i % 2) * HC:(i % 2 + 1) * HC]
            corner = lambda ap: ap.rearrange("p (k s d) -> p s k d", k=4, s=B * G)
            TB = (0, 1, 6, 7)
            for i in range(4):
                act.wait_ge(t0.sem, t0[f"table{i}"])
                copy(tab(i, 0), corner(ps[:, TB[i], :]), a0, f"high{i}")
            for i in range(4):
                act.wait_ge(v0.sem, v0[f"rest{i}"])
                copy(tab(i, 1), rest[:, i * BANK:(i + 1) * BANK].rearrange("p (s k d) -> p s k d", s=B * G, k=4),
                     a0, f"mid{i}")
            act.wait_ge(v0.sem, v0["gate"])
            nc.scalar.activation(gate_m[:], gate_m[:], ACT.Exp, scale=-1.0).then_inc(a0.sem, a0.step("sigexp"))
            act.wait_ge(v0.sem, v0["away"])
            nc.scalar.activation(hat1, away, ACT.Abs, bias=neg1[:]).then_inc(a0.sem, a0.step("hat1a"))
            act.wait_ge(a0.sem, a0["hat1a"])
            nc.scalar.activation(hats.rearrange("p (n z) -> p n z", z=2)[:, :, 1], hat1, ACT.Relu,
                                 bias=pos1[:], scale=-1.0).then_inc(a0.sem, a0.step("hat1"))

            def index_group(u, i):
                n = u * 9 + i
                act.wait_ge(s_bc, n + 1)
                if i == 0 and u >= 2:
                    act.wait_ge(s_oh, 2 * (u - 1))
                nc.scalar.activation(ixb[:, u % 2, 4 * i:4 * i + 4, :].rearrange("p j n -> p (j n)"),
                                     ps[:, n % 2, :], ACT.Copy).then_inc(s_bce, 1)

            def sample_group(n):
                b, i = n // GRP, n % GRP
                act.wait_ge(s_gp, n + 1)
                if i == 0 and b >= 2:
                    act.wait_ge(v1.sem, v1[f"prodv{b - 2}"])
                nc.scalar.activation(gv[:, b % 2, 8 * i:8 * i + 8, :].rearrange("p s d -> p (s d)"),
                                     ps[:, 2 + n % 4, :], ACT.Copy).then_inc(s_ge, 1)

            def pair_exp(b):
                act.wait_ge(v1.sem, v1[f"sub{b}"])
                nc.scalar.activation(pexp[:], logit[:], ACT.Exp).then_inc(s_px, 1)

            act.wait_ge(vz.sem, vz["zneg"])
            nc.scalar.activation(soft[:], zsel[:], ACT.Exp, bias=zmax[:], accum_out=zsum[:]).then_inc(az.sem, az.step("exp"))
            for i in range(9):
                index_group(0, i)
            done = 0
            for u in range(T):
                for i in range(9):
                    if u + 1 < T:
                        index_group(u + 1, i)
                    while 8 * (done + 1) <= u * J + 4 * i + 4:
                        sample_group(done)
                        done += 1
                    if i == 6 and u in (3, 5, 7):
                        pair_exp((u - 3) // 2)
            pair_exp(B - 1)

            act.wait_ge(t2.sem, t2["attT"])
            act.wait_ge(g0.sem, g0["sm"])
            copy(att_ch, ps[:, 0, 0:N], a2, "attT")
            act.wait_ge(t2.sem, t2["poolred"])
            nc.scalar.activation(pool_red[:].rearrange("p (b c) -> p b c", b=B), rep(ps[0:4, 2, 0:B], C), ACT.Relu).then_inc(a2.sem, a2.step("poolred"))
            act.wait_ge(v2.sem, v2["kneg"])
            nc.scalar.activation(kexp[:], ps[:, 3, 0:4], ACT.Exp, scale=1.0 / 30.0, bias=kmax[:], accum_out=ksum_[:])\
                .then_inc(a2.sem, a2.step("kexp"))
            act.wait_ge(t2.sem, t2["conv"])
            act.wait_ge(v2.sem, v2["bshift"])
            nc.scalar.activation(y1, ps[:, 4, 0:N], ACT.Relu, bias=bshift[:], scale=bn_inv[:])\
                .then_inc(a2.sem, a2.step("y1"))

            act.wait_ge(t3.sem, t3["lnT"])
            copy(ln_ch, ps[:, 0, 0:N], a3, "lnT")
            act.wait_ge(t3.sem, t3["qc"])
            copy(qc, ps[:, 1, 0:N], a3, "qc")
            act.wait_ge(t3.sem, t3["vt"])
            copy(vt, ps[:, 3, 0:N], a3, "vt")
            sc = score.rearrange("p (b k) -> p b k", b=B)
            pr = prob.rearrange("p (b k) -> p b k", b=B)
            act.wait_ge(v3.sem, v3["sneg"])
            for t in range(T):
                b, h = t % B, t // B
                keys = slice(0, P) if h == 0 else slice(P, 3 * P)
                nc.scalar.activation(pr[:, b, keys], sc[:, b, keys], ACT.Exp, bias=smax[:, t:t + 1],
                                     accum_out=ssum[:, t:t + 1]).then_inc(a3.sem, a3.step(f"exp{t}"))
            for b in (0, 2):
                act.wait_ge(t3.sem, t3[f"pt{b}"])
                copy(prob_t[:, b * 3 * P:(b + 1) * 3 * P], ps[:, b, 0:3 * P], a3, f"pt{b}")

            act.wait_ge(t4.sem, t4["aug0"])
            copy(aug[0:C, 0:4 * P], ps[0:C, 0, :], a4, "aug0")
            act.wait_ge(v4.sem, v4["rsub"])
            nc.scalar.activation(rexp[:], rexp[:], ACT.Exp).then_inc(a4.sem, a4.step("rexp"))

            act.wait_ge(t5.sem, t5["aug0"])
            copy(aug[0:C, 0:4 * P], ps[0:C, 0, :], a5, "aug0")
            for t in range(T):
                h = t // B
                blk = slice(t * BANK, (t + 1) * BANK)
                act.wait_ge(t5.sem, t5[f"k{t}"])
                nc.scalar.activation(fk[:, blk], ps[:, 2 + 2 * (t % 2), :], ACT.Exp, bias=neg1[:])\
                    .then_inc(a5.sem, a5.step(f"ek{t}"))
                act.wait_ge(t5.sem, t5[f"v{t}"])
                copy(vcos[:, blk], ps[:, 3 + 2 * (t % 2), :], a5, f"vc{t}", c["cs"][:, 2 * h:2 * h + 1])
                copy(vsin[:, blk], ps[:, 3 + 2 * (t % 2), :], a5, f"vs{t}", c["cs"][:, 2 * h + 1:2 * h + 2])
            for i in range(8):
                act.wait_ge(t5.sem, t5[f"q{i}"])
                nc.scalar.activation(fq[:, i * BANK:(i + 1) * BANK], ps[:, 6 + i % 2, :], ACT.Exp, bias=neg1[:])\
                    .then_inc(a5.sem, a5.step(f"eq{i}"))
            act.wait_ge(t5.sem, t5["ks"])
            copy(ks_sb[:], ps[:, 4, 0:32], a5, "ks")
            act.wait_ge(t5.sem, t5["mcs"])
            copy(mcs[:, 0:BANK], ps[:, 2, :], a5, "mcs0")
            copy(mcs[:, BANK:], ps[:, 3, :], a5, "mcs1")
            act.wait_ge(t5.sem, t5["denT"])
            copy(den_t[:, 0:BANK], ps[0:NHEAD, 6, :], a5, "denT0")
            copy(den_t[:, BANK:], ps[0:NHEAD, 7, :], a5, "denT1")

            act.wait_ge(g0.sem, g0["shiftpad"])
            act.wait_ge(t6.sem, t6["aug0"])
            copy(sh[:, :, KU - 1:KU - 1 + P], ps[0:D, 0, :].rearrange("p (b n) -> p b n", b=B), a6, "aug0")
            for t in range(T):
                b, h = t % B, t // B
                act.wait_ge(t6.sem, t6[f"v{t}"])
                copy(vv.rearrange("p (k h b m e) -> p k h b m e", k=NF, h=NH, b=B, m=2)[:, :, h, b, 0, :],
                     ps[:, 2 + 2 * (t % 2), :].rearrange("p (k e) -> p k e", k=NF), a6, f"vp{t}")

        @block.vector
        def _(dve):
            nv = nc.vector

            def layernorm(src, v, pool_step):
                X = tok(src)
                nv.reduce_sum(lsum[:], X, axis=AX.X).then_inc(v.sem, v.step("sum"))
                dve.wait_ge(v.sem, v["sum"])
                nv.tensor_scalar(lneg[:], lsum[:], -1.0 / C, None, ALU.mult).then_inc(v.sem, v.step("neg"))
                dve.wait_ge(v.sem, v["neg"])
                nv.tensor_tensor(out=tok(lcen), in0=X, in1=rep(lneg[:], C), op=ALU.add).then_inc(v.sem, v.step("cen"))
                dve.wait_ge(v.sem, v["cen"])
                nv.tensor_tensor(out=lsq, in0=lcen, in1=lcen, op=ALU.mult).then_inc(v.sem, v.step("sq"))
                dve.wait_ge(v.sem, v["sq"])
                nv.reduce_sum(lvar[:], tok(lsq), axis=AX.X).then_inc(v.sem, v.step("var"))
                dve.wait_ge(v.sem, v["var"])
                nv.tensor_scalar(var_eps[:], lvar[:], 1.0 / C, 1e-5, ALU.mult, ALU.add).then_inc(v.sem, v.step("eps"))
                dve.wait_ge(g0.sem, g0[pool_step])
                nv.tensor_tensor(out=tok(ln[:]), in0=tok(lcen), in1=rep(rstd[:], C), op=ALU.mult)\
                    .then_inc(v.sem, v.step("ln"))

            def moments_of(src, v):
                nv.bn_stats(stats[:], src).then_inc(v.sem, v.step("stats"))
                dve.wait_ge(v.sem, v["stats"])
                nv.bn_aggr(moments[:], stats[:]).then_inc(v.sem, v.step("moments"))
                dve.wait_ge(v.sem, v["moments"])
                nv.tensor_scalar(var_eps[:, 0:1], moments[:, 1:2], 1e-5, None, ALU.add).then_inc(v.sem, v.step("eps"))

            dve.wait_ge(d_cst, 16)
            nv.tensor_copy(identb[:], ident).then_inc(v0.sem, v0.step("identb"))
            nv.memset(neg1[:], -1.0).then_inc(v0.sem, v0.step("neg1"))
            nv.memset(pos1[:], 1.0).then_inc(v0.sem, v0.step("pos1"))
            nv.memset(aug[C:C + 1, :], 1.0).then_inc(v0.sem, v0.step("ones"))
            nv.tensor_tensor(out=base[:].rearrange("p (h n) -> p h n", h=NH),
                             in0=c["base"].rearrange("p (h n) -> p h n", h=NH),
                             in1=c["boff"][:, 0:2 * J].unsqueeze(1).broadcast_to([P, NH, 2 * J]), op=ALU.add)\
                .then_inc(v0.sem, v0.step("base"))
            dve.wait_ge(d_x, 16)
            moments_of(x[:], v0)
            dve.wait_ge(g0.sem, g0["rstd0"])
            nv.tensor_scalar(xg[:], x[:], moments[:, 0:1], rstd[:, 0:1], ALU.subtract, ALU.mult)\
                .then_inc(v0.sem, v0.step("xg"))

            def tap_step(j, t, dst, name):
                win = qkvp[:, j, t // 3:t // 3 + H, t % 3:t % 3 + W]
                w = f["wdw"][:, j * K2 + t:j * K2 + t + 1]
                if t == 0:
                    nv.tensor_scalar(dst, win, w, f["bdw"][:, j:j + 1], ALU.mult, ALU.add)\
                        .then_inc(v0.sem, v0.step(name))
                else:
                    nv.scalar_tensor_tensor(out=dst, in0=win, scalar=w, in1=dst, op0=ALU.mult, op1=ALU.add)\
                        .then_inc(v0.sem, v0.step(name))

            q_in = img(q_mid)
            dve.wait_ge(g0.sem, g0["kvpad"])
            dve.wait_ge(d_front, 16)
            dve.wait_ge(a0.sem, a0["q"])
            for t in range(K2):
                if t:
                    dve.wait_ge(v0.sem, v0[f"q{t - 1}"])
                tap_step(0, t, q_in, f"q{t}")
            dve.wait_ge(v0.sem, v0["q8"])
            for v, cols in ((0, slice(0, W - 1)), (2, slice(1, W))):
                nv.tensor_copy(img(qf[:, v, W + 1:W + 1 + N])[:, :, cols], q_in[:, :, cols])\
                    .then_inc(v0.sem, v0.step(f"shift{v}"))
            dve.wait_ge(a0.sem, a0["v"])
            for t in range(K2):
                for j, nm in ((1, "k"), (2, "v")):
                    if t:
                        dve.wait_ge(v0.sem, v0[f"{nm}{t - 1}"])
                    tap_step(j, t, img(kvv[:, j - 1, 0:N]), f"{nm}{t}")

            dve.wait_ge(t0.sem, t0["offsets"])
            off = ps[:, 2:6, 0:2 * NOFF].rearrange("p b (h n) -> p b h n", h=NH)
            nv.tensor_tensor(out=pos.rearrange("p (b h n) -> p b h n", b=B, h=NH), in0=off[:, :, :, 0:2 * J],
                             in1=base[:].rearrange("p (h n) -> p h n", h=NH).unsqueeze(1).broadcast_to([P, B, NH, 2 * J]),
                             op=ALU.add).then_inc(v0.sem, v0.step("pos"))
            dve.wait_ge(v0.sem, v0["pos"])
            nv.tensor_scalar(pos, pos, -2.0, H + 1.0, ALU.max, ALU.min).then_inc(v0.sem, v0.step("clamp"))
            dve.wait_ge(v0.sem, v0["clamp"])
            nv.tensor_scalar(near, pos, -0.5, ROUND, ALU.add, ALU.add).then_inc(v0.sem, v0.step("near0"))
            dve.wait_ge(v0.sem, v0["near0"])
            nv.tensor_scalar(near, near, -ROUND, 0.0, ALU.add, ALU.max).then_inc(v0.sem, v0.step("near1"))
            dve.wait_ge(v0.sem, v0["near1"])
            nv.tensor_scalar(near, near, H - 2.0, None, ALU.min).then_inc(v0.sem, v0.step("near"))
            dve.wait_ge(v0.sem, v0["near"])
            yx = near.rearrange("p (n a) -> p n a", a=2)
            nv.scalar_tensor_tensor(out=index[:], in0=yx[:, :, 0], scalar=float(W), in1=yx[:, :, 1],
                                    op0=ALU.mult, op1=ALU.add).then_inc(v0.sem, v0.step("index"))
            TB = (0, 1, 6, 7)
            rst = lambda i: rest[:, i * BANK:(i + 1) * BANK].rearrange("p (s k d) -> p s k d", s=B * G, k=4)
            tab = lambda i, part: tabv[:, i // 2, part, :, :, (i % 2) * HC:(i % 2 + 1) * HC]
            for i in range(4):
                dve.wait_ge(a0.sem, a0[f"high{i}"])
                nv.tensor_tensor(out=rst(i), in0=ps[:, TB[i], :].rearrange("p (k s d) -> p s k d", k=4, s=B * G),
                                 in1=tab(i, 0), op=ALU.subtract).then_inc(v0.sem, v0.step(f"rest{i}"))
            for i in range(4):
                dve.wait_ge(a0.sem, a0[f"mid{i}"])
                nv.tensor_tensor(out=tab(i, 2), in0=rst(i), in1=tab(i, 1), op=ALU.subtract)\
                    .then_inc(v0.sem, v0.step(f"low{i}"))
            nv.tensor_tensor(out=away, in0=pos, in1=near, op=ALU.subtract).then_inc(v0.sem, v0.step("away"))
            dve.wait_ge(v0.sem, v0["away"])
            nv.scalar_tensor_tensor(out=hat0, in0=away, scalar=-1.0, in1=away, op0=ALU.mult, op1=ALU.min).then_inc(v0.sem, v0.step("hat0a"))
            dve.wait_ge(v0.sem, v0["hat0a"])
            nv.tensor_scalar(hats.rearrange("p (n z) -> p n z", z=2)[:, :, 0], hat0, 1.0, 0.0, ALU.add, ALU.max)\
                .then_inc(v0.sem, v0.step("hat0"))
            nv.tensor_tensor(out=gate_m[:].rearrange("p (b h n) -> p b h n", b=B, h=NH), in0=off[:, :, :, 2 * J:],
                             in1=c["boff"][:, 2 * J:].unsqueeze(1).unsqueeze(1).broadcast_to([P, B, NH, K2]), op=ALU.add)\
                .then_inc(v0.sem, v0.step("gate"))
            dve.wait_ge(a0.sem, a0["sigexp"])
            nv.tensor_scalar(gate_m[:], gate_m[:], 1.0, None, ALU.add).then_inc(v0.sem, v0.step("gate1"))
            dve.wait_ge(v0.sem, v0["gate1"])
            nv.reciprocal(gate_m[:], gate_m[:]).then_inc(v0.sem, v0.step("sigmoid"))
            dve.wait_ge(v0.sem, v0["sigmoid"])
            nv.tensor_copy(mask_x[:].rearrange("p (t g k) -> p t g k", t=T, g=G),
                           gate_m[:].rearrange("p (t k) -> p t k", t=T).unsqueeze(2).broadcast_to([P, T, G, K2]))\
                .then_inc(v0.sem, v0.step("maskx"))
            dve.wait_ge(v0.sem, v0["maskx"])
            dve.wait_ge(a0.sem, a0["hat1"])
            hv = hats.rearrange("p (n a z) -> p n a z", a=2, z=2)
            nv.tensor_tensor(out=hv[:, :, 0, :], in0=hv[:, :, 0, :], in1=rep(mask_x[:], 2), op=ALU.mult)\
                .then_inc(v0.sem, v0.step("hatm"))
            dve.wait_ge(v0.sem, v0["hatm"])
            nv.tensor_tensor(out=w4[:].rearrange("p (n y z) -> p n y z", y=2, z=2), in0=rep(hv[:, :, 0, :], 2),
                             in1=hv[:, :, 1, :].unsqueeze(2).broadcast_to([P, T * J, 2, 2]), op=ALU.mult)\
                .then_inc(v0.sem, v0.step("w4"))

            nv.tensor_tensor(out=zsel[:], in0=c["logw"], in1=c["gumbel"], op=ALU.add).then_inc(vz.sem, vz.step("z"))
            dve.wait_ge(vz.sem, vz["z"])
            nv.reduce_max(zmax[:], zsel[:], axis=AX.X).then_inc(vz.sem, vz.step("zmax"))
            dve.wait_ge(vz.sem, vz["zmax"])
            nv.tensor_scalar(zmax[:], zmax[:], -1.0, None, ALU.mult).then_inc(vz.sem, vz.step("zneg"))

            def one_hots(u):
                for half in range(2):
                    js = slice(half * J // 2, (half + 1) * J // 2)
                    dve.wait_ge(s_bce, 9 * u + (5 if half == 0 else 9))
                    if u >= 2 and half == 0:
                        dve.wait_ge(s_un, u - 1)
                    for q in range(2):
                        ins = nv.tensor_scalar(ohv[:, u % 2, q, js, :], ixb[:, u % 2, js, :], c["pidx"][:, q:q + 1],
                                               None, ALU.is_equal)
                    ins.then_inc(s_oh, 1)

            def pair(b):
                r = b % 2
                w = slice(b * NH * J * 4, (b + 1) * NH * J * 4)
                gk = gv[:, r, :, :].rearrange("p (h s) (k d) -> p h (s k) d", h=NH * G, k=4)
                dve.wait_ge(s_ge, GRP * (b + 1))
                qv = q_tok[:, b * NH * C:(b + 1) * NH * C].rearrange("p (s d) -> p s d", d=HC)
                nv.tensor_tensor(out=prod.rearrange("p (s n d) -> p s n d", s=NH * G, n=4 * K2),
                                 in0=gk[:, :, :, 0:HC],
                                 in1=qv.unsqueeze(2).broadcast_to([P, NH * G, 4 * K2, HC]), op=ALU.mult)\
                    .then_inc(v1.sem, v1.step(f"prodk{b}"))
                dve.wait_ge(v1.sem, v1[f"prodk{b}"])
                nv.reduce_sum(dots[:], prod.rearrange("p (n d) -> p n d", d=HC), axis=AX.X)\
                    .then_inc(v1.sem, v1.step(f"dots{b}"))
                dve.wait_ge(v1.sem, v1[f"dots{b}"])
                nv.tensor_tensor(out=dots[:], in0=dots[:], in1=w4[:, w], op=ALU.mult).then_inc(v1.sem, v1.step(f"wdots{b}"))
                dve.wait_ge(v1.sem, v1[f"wdots{b}"])
                nv.reduce_sum(logit[:], dots[:].rearrange("p (n k) -> p n k", k=4), axis=AX.X)\
                    .then_inc(v1.sem, v1.step(f"logit{b}"))
                dve.wait_ge(v1.sem, v1[f"logit{b}"])
                lg = logit[:].rearrange("p (s k) -> p s k", k=K2)
                nv.reduce_max(peak[:], lg, axis=AX.X).then_inc(v1.sem, v1.step(f"peak{b}"))
                dve.wait_ge(v1.sem, v1[f"peak{b}"])
                nv.tensor_tensor(out=lg, in0=lg, in1=rep(peak[:], K2), op=ALU.subtract).then_inc(v1.sem, v1.step(f"sub{b}"))
                dve.wait_ge(s_px, b + 1)
                pv = pexp[:].rearrange("p (s k) -> p s k", k=K2)
                nv.reduce_sum(psum_[:], pv, axis=AX.X).then_inc(v1.sem, v1.step(f"expsum{b}"))
                dve.wait_ge(v1.sem, v1[f"expsum{b}"])
                nv.reciprocal(pinv[:], psum_[:]).then_inc(v1.sem, v1.step(f"inv{b}"))
                nv.tensor_tensor(out=w4p[:].rearrange("p (n k) -> p n k", k=4),
                                 in0=w4[:, w].rearrange("p (n k) -> p n k", k=4), in1=rep(pexp[:], 4), op=ALU.mult)\
                    .then_inc(v1.sem, v1.step(f"w4p{b}"))
                dve.wait_ge(v1.sem, v1[f"w4p{b}"])
                nv.tensor_tensor(out=prod.rearrange("p (s d n) -> p s d n", s=NH * G, d=HC),
                                 in0=gk[:, :, :, HC:KV].rearrange("p s n d -> p s d n"),
                                 in1=w4p[:].rearrange("p (s n) -> p s n", s=NH * G).unsqueeze(2)
                                 .broadcast_to([P, NH * G, HC, 4 * K2]), op=ALU.mult)\
                    .then_inc(v1.sem, v1.step(f"prodv{b}"))
                dve.wait_ge(v1.sem, v1[f"prodv{b}"])
                nv.reduce_sum(mixed[:], prod.rearrange("p (n k) -> p n k", k=4 * K2), axis=AX.X)\
                    .then_inc(v1.sem, v1.step(f"mixed{b}"))
                dve.wait_ge(v1.sem, v1[f"mixed{b}"])
                hgd = lambda ap: ap.rearrange("p (h g d) -> p h g d", h=NH, g=G)
                nv.tensor_tensor(out=tokhb(att[:])[:, :, b, :].rearrange("p h (g d) -> p h g d", g=G),
                                 in0=hgd(mixed[:]), in1=rep(pinv[:].rearrange("p (h g) -> p h g", h=NH), HC), op=ALU.mult)\
                    .then_inc(v1.sem, v1.step(f"att{b}"))

            for u in range(T):
                one_hots(u)
                if u == 0:
                    dve.wait_ge(az.sem, az["exp"])
                    nv.reciprocal(zsum[:], zsum[:]).then_inc(vz.sem, vz.step("zinv"))
                    dve.wait_ge(vz.sem, vz["zinv"])
                    nv.tensor_scalar(soft[:], soft[:], zsum[:], None, ALU.mult).then_inc(vz.sem, vz.step("soft"))
                    dve.wait_ge(vz.sem, vz["soft"])
                    sj = soft[:].unsqueeze(1).broadcast_to([P, NSC, NSC])
                    z44 = lambda ap: ap.rearrange("p (i j) -> p i j", i=NSC)
                    nv.tensor_tensor(out=z44(zgt[:]), in0=sj, in1=rep(soft[:], NSC), op=ALU.is_gt)\
                        .then_inc(vz.sem, vz.step("zgt"))
                    nv.tensor_tensor(out=z44(zeq[:]), in0=sj, in1=rep(soft[:], NSC), op=ALU.is_equal)\
                        .then_inc(vz.sem, vz.step("zeq"))
                    dve.wait_ge(vz.sem, vz["zeq"])
                    nv.tensor_tensor(out=zeq[:], in0=zeq[:], in1=c["lt4"], op=ALU.mult).then_inc(vz.sem, vz.step("zeqlt"))
                    dve.wait_ge(vz.sem, vz["zeqlt"])
                    nv.tensor_tensor(out=zgt[:], in0=zgt[:], in1=zeq[:], op=ALU.add).then_inc(vz.sem, vz.step("zadd"))
                    dve.wait_ge(vz.sem, vz["zadd"])
                    nv.reduce_sum(hard[:], z44(zgt[:]), axis=AX.X).then_inc(vz.sem, vz.step("rank"))
                    dve.wait_ge(vz.sem, vz["rank"])
                    nv.tensor_scalar(hard[:], hard[:], 0.0, None, ALU.is_equal).then_inc(vz.sem, vz.step("hard"))
                    dve.wait_ge(vz.sem, vz["hard"])
                    nv.tensor_tensor(out=wsel[:], in0=hard[:], in1=soft[:], op=ALU.subtract).then_inc(vz.sem, vz.step("diff"))
                    dve.wait_ge(vz.sem, vz["diff"])
                    nv.tensor_tensor(out=wsel[:], in0=wsel[:], in1=soft[:], op=ALU.add).then_inc(vz.sem, vz.step("w"))
                    nv.tensor_tensor(out=hard[:], in0=hard[:], in1=c["frac"], op=ALU.mult).then_inc(vz.sem, vz.step("lenp"))
                    dve.wait_ge(vz.sem, vz["lenp"])
                    nv.reduce_sum(length[:], hard[:], axis=AX.X).then_inc(vz.sem, vz.step("length"))
                    dve.wait_ge(vz.sem, vz["length"])
                    nv.tensor_scalar(window[:], c["tokidx"], length[:], None, ALU.is_lt).then_inc(vz.sem, vz.step("win"))
                    dve.wait_ge(vz.sem, vz["win"])
                    nv.tensor_scalar(winsgn[:], window[:], c["sgn"], None, ALU.mult).then_inc(vz.sem, vz.step("winsgn"))
                    dve.wait_ge(d_l3, 48)
                    nv.tensor_scalar(l3w[C:C + 1, 0:2 * NHEAD * D], l3w[C:C + 1, 0:2 * NHEAD * D], 1.0, None, ALU.add)\
                        .then_inc(vz.sem, vz.step("lbias"))
                if u >= 3 and u % 2:
                    pair((u - 3) // 2)
            pair(B - 1)

            dve.wait_ge(t2.sem, t2["proj"])
            nv.scalar_tensor_tensor(out=x1[:], in0=ps[:, 1, 0:N], scalar=p1["bproj"], in1=x[:], op0=ALU.add, op1=ALU.add)\
                .then_inc(v2.sem, v2.step("x1"))
            dve.wait_ge(v2.sem, v2["x1"])
            moments_of(x1[:], v2)
            dve.wait_ge(g0.sem, g0["rstd1"])
            nv.tensor_scalar(xp[:, 1:1 + H, 1:1 + W], img(x1[:]), moments[:, 0:1], rstd[:, 0:1], ALU.subtract, ALU.mult)\
                .then_inc(v2.sem, v2.step("xpad"))
            dve.wait_ge(v2.sem, v2["xpad"])
            nv.tensor_reduce(pool[:], xp[:, 1:1 + H, 1:1 + W], AX.XY, ALU.add).then_inc(v2.sem, v2.step("pool"))
            dve.wait_ge(v2.sem, v2["pool"])
            nv.tensor_scalar(pool_bd[:], c["bmask"], pool[:], 1.0 / N, ALU.mult, ALU.mult).then_inc(v2.sem, v2.step("poolbd"))
            dve.wait_ge(t2.sem, t2["katt"])
            nv.reduce_max(kmax[:], ps[:, 3, 0:4], axis=AX.X).then_inc(v2.sem, v2.step("kmax"))
            dve.wait_ge(v2.sem, v2["kmax"])
            nv.tensor_scalar(kmax[:], kmax[:], -1.0 / 30.0, None, ALU.mult).then_inc(v2.sem, v2.step("kneg"))
            dve.wait_ge(a2.sem, a2["kexp"])
            nv.reciprocal(kinv[:], ksum_[:]).then_inc(v2.sem, v2.step("kinv"))
            dve.wait_ge(v2.sem, v2["kinv"])
            nv.tensor_scalar(katt[:], kexp[:], kinv[:], None, ALU.mult).then_inc(v2.sem, v2.step("katt"))
            for k in range(4):
                ck = p1["convk"][:, k * K2 * C:(k + 1) * K2 * C]
                if k == 0:
                    dve.wait_ge(v2.sem, v2["katt"])
                    nv.tensor_scalar(wmix, ck, katt[:, 0:1], None, ALU.mult).then_inc(v2.sem, v2.step("mix0"))
                else:
                    dve.wait_ge(v2.sem, v2[f"mix{k - 1}"])
                    nv.scalar_tensor_tensor(out=wmix, in0=ck, scalar=katt[:, k:k + 1], in1=wmix,
                                            op0=ALU.mult, op1=ALU.add).then_inc(v2.sem, v2.step(f"mix{k}"))
            dve.wait_ge(v2.sem, v2["mix3"])
            nv.tensor_tensor(out=wmix_bd.rearrange("p (t b o) -> p t b o", t=K2, b=B),
                             in0=wmix.rearrange("p (t o) -> p t o", t=K2).unsqueeze(2).broadcast_to([P, K2, B, C]),
                             in1=rep(c["bmask"].unsqueeze(1).broadcast_to([P, K2, B]), C), op=ALU.mult)\
                .then_inc(v2.sem, v2.step("mixbd"))
            nv.tensor_tensor(out=bmix[:], in0=katt[:], in1=p1["kbias"], op=ALU.mult).then_inc(v2.sem, v2.step("bmix"))
            dve.wait_ge(v2.sem, v2["bmix"])
            nv.reduce_sum(bsum[:], bmix[:], axis=AX.X).then_inc(v2.sem, v2.step("bsum"))
            dve.wait_ge(g0.sem, g0["bninv"])
            dve.wait_ge(v2.sem, v2["bsum"])
            nv.tensor_scalar(bn_inv[:], bn_inv[:], p1["bnscale"], None, ALU.mult).then_inc(v2.sem, v2.step("binv"))
            dve.wait_ge(v2.sem, v2["binv"])
            nv.tensor_scalar(bshift[:], bsum[:], p1["bnmean"], bn_inv[:], ALU.subtract, ALU.mult)\
                .then_inc(v2.sem, v2.step("bcent"))
            dve.wait_ge(v2.sem, v2["bcent"])
            nv.tensor_tensor(out=bshift[:], in0=bshift[:], in1=p1["bnbias"], op=ALU.add).then_inc(v2.sem, v2.step("bshift"))
            dve.wait_ge(a2.sem, a2["y1"])
            nv.tensor_tensor(out=x2, in0=x1[:], in1=y1, op=ALU.add).then_inc(v2.sem, v2.step("x2"))
            dve.wait_ge(t2.sem, t2["x2T"])
            nv.tensor_copy(x2t[:], ps[:, 5, 0:N]).then_inc(v2.sem, v2.step("x2t"))
            dve.wait_ge(v2.sem, v2["x2t"])

            layernorm(x2t[:], v3, "rstd2")
            dve.wait_ge(t3.sem, t3["kc"])
            nv.tensor_copy(kc, ps[:, 2, 0:N]).then_inc(v3.sem, v3.step("kc"))
            sc = score.rearrange("p (b k) -> p b k", b=B)
            dve.wait_ge(d_l2, 16)
            dve.wait_ge(t3.sem, t3["score"])
            nv.scalar_tensor_tensor(out=sc, in0=ps[:, 4:8, 0:3 * P], scalar=float(N) ** -0.5,
                                    in1=p2["causal"].unsqueeze(1).broadcast_to([P, B, 3 * P]),
                                    op0=ALU.mult, op1=ALU.add).then_inc(v3.sem, v3.step("score"))
            dve.wait_ge(v3.sem, v3["score"])
            sx = smax[:].rearrange("p (h b) -> p h b", h=NH)
            nv.reduce_max(sx[:, 0, :], sc[:, :, 0:P], axis=AX.X).then_inc(v3.sem, v3.step("smax0"))
            nv.reduce_max(sx[:, 1, :], sc[:, :, P:3 * P], axis=AX.X).then_inc(v3.sem, v3.step("smax1"))
            dve.wait_ge(v3.sem, v3["smax1"])
            nv.tensor_scalar(smax[:], smax[:], -1.0, None, ALU.mult).then_inc(v3.sem, v3.step("sneg"))
            dve.wait_ge(a3.sem, a3[f"exp{T - 1}"])
            nv.reciprocal(sinv[:], ssum[:]).then_inc(v3.sem, v3.step("sinv"))
            for b in (1, 3):
                dve.wait_ge(t3.sem, t3[f"pt{b}"])
                nv.tensor_copy(prob_t[:, b * 3 * P:(b + 1) * 3 * P], ps[:, b, 0:3 * P])\
                    .then_inc(v3.sem, v3.step(f"pt{b}"))
            dve.wait_ge(t3.sem, t3["pv"])
            nv.tensor_tensor(out=tok(ctx_n), in0=tok(ps[:, 4, 0:N]), in1=rep(sinv[:], C), op=ALU.mult)\
                .then_inc(v3.sem, v3.step("ctx"))
            dve.wait_ge(v3.sem, v3["ctx"])
            nv.tensor_tensor(out=x3t, in0=x2t[:], in1=ctx_n, op=ALU.add).then_inc(v3.sem, v3.step("x3"))
            dve.wait_ge(v3.sem, v3["x3"])

            layernorm(x3t, v4, "rstd3")
            dve.wait_ge(t4.sem, t4["aug1"])
            nv.tensor_copy(aug[0:C, 4 * P:], ps[0:C, 1, :]).then_inc(v4.sem, v4.step("aug1"))
            dve.wait_ge(t4.sem, t4["router"])
            te = lambda ap: ap.rearrange("p (t e) -> p t e", e=E)
            tee = lambda ap: ap.rearrange("p (t i j) -> p t i j", i=E, j=E)
            nv.tensor_copy(rlog[:], ps[:, 2, 0:T * E]).then_inc(v4.sem, v4.step("rlog"))
            dve.wait_ge(v4.sem, v4["rlog"])
            lj = te(rlog[:]).unsqueeze(2).broadcast_to([P, T, E, E])
            li = rep(te(rlog[:]), E)
            nv.tensor_tensor(out=tee(rgt), in0=lj, in1=li, op=ALU.is_gt).then_inc(v4.sem, v4.step("rgt"))
            nv.tensor_tensor(out=tee(req), in0=lj, in1=li, op=ALU.is_equal).then_inc(v4.sem, v4.step("req"))
            dve.wait_ge(v4.sem, v4["req"])
            nv.tensor_tensor(out=req.rearrange("p (t n) -> p t n", t=T), in0=req.rearrange("p (t n) -> p t n", t=T),
                             in1=c["lt8"].unsqueeze(1).broadcast_to([P, T, E * E]), op=ALU.mult)\
                .then_inc(v4.sem, v4.step("reqlt"))
            dve.wait_ge(v4.sem, v4["reqlt"])
            nv.tensor_tensor(out=rgt, in0=rgt, in1=req, op=ALU.add).then_inc(v4.sem, v4.step("rsum"))
            dve.wait_ge(v4.sem, v4["rsum"])
            nv.reduce_sum(rank[:], rgt.rearrange("p (n j) -> p n j", j=E), axis=AX.X).then_inc(v4.sem, v4.step("rank"))
            nv.reduce_max(rmax[:], te(rlog[:]), axis=AX.X).then_inc(v4.sem, v4.step("rmax"))
            dve.wait_ge(v4.sem, v4["rmax"])
            nv.tensor_tensor(out=te(rexp[:]), in0=te(rlog[:]), in1=rep(rmax[:], E), op=ALU.subtract)\
                .then_inc(v4.sem, v4.step("rsub"))
            nv.tensor_scalar(chosen[:], rank[:], 2.0, None, ALU.is_lt).then_inc(v4.sem, v4.step("chosen"))
            dve.wait_ge(v4.sem, v4["chosen"])
            dve.wait_ge(a4.sem, a4["rexp"])
            nv.tensor_tensor(out=chosen[:], in0=chosen[:], in1=rexp[:], op=ALU.mult).then_inc(v4.sem, v4.step("esel"))
            dve.wait_ge(v4.sem, v4["esel"])
            nv.reduce_sum(rsum[:], te(chosen[:]), axis=AX.X).then_inc(v4.sem, v4.step("esum"))
            dve.wait_ge(v4.sem, v4["esum"])
            nv.reciprocal(rsum[:], rsum[:]).then_inc(v4.sem, v4.step("einv"))
            dve.wait_ge(v4.sem, v4["einv"])
            dve.wait_ge(t4.sem, t4["experts"])
            tce = lambda ap: ap.rearrange("p (t c e) -> p t c e", t=T, e=E)
            nv.tensor_tensor(out=tce(gated),
                             in0=ps[:, 4:8, :].rearrange("p k (u e c) -> p (k u) c e", u=2, e=E),
                             in1=te(chosen[:]).unsqueeze(2).broadcast_to([P, T, C, E]), op=ALU.mult)\
                .then_inc(v4.sem, v4.step("gated"))
            dve.wait_ge(v4.sem, v4["gated"])
            nv.reduce_sum(lsq, gated.rearrange("p (n e) -> p n e", e=E), axis=AX.X).then_inc(v4.sem, v4.step("y"))
            dve.wait_ge(v4.sem, v4["y"])
            nv.tensor_tensor(out=tok(lsq), in0=tok(lsq), in1=rep(rsum[:], C), op=ALU.mult)\
                .then_inc(v4.sem, v4.step("ynorm"))
            dve.wait_ge(v4.sem, v4["ynorm"])
            nv.tensor_tensor(out=x4t, in0=x3t, in1=lsq, op=ALU.add).then_inc(v4.sem, v4.step("x4"))
            dve.wait_ge(v4.sem, v4["x4"])

            layernorm(x4t, v5, "rstd4")
            dve.wait_ge(t5.sem, t5["aug1"])
            nv.tensor_copy(aug[0:C, 4 * P:], ps[0:C, 1, :]).then_inc(v5.sem, v5.step("aug1"))
            for t in range(T):
                blk = slice(t * BANK, (t + 1) * BANK)
                dve.wait_ge(a5.sem, a5[f"ek{t}"])
                nv.scalar_tensor_tensor(out=fk[:, blk], in0=fk[:, blk], scalar=1.0, in1=ps[:, 2 + 2 * (t % 2), :],
                                        op0=ALU.min, op1=ALU.max).then_inc(v5.sem, v5.step(f"fk{t}"))
            for i in range(8):
                blk = slice(i * BANK, (i + 1) * BANK)
                dve.wait_ge(a5.sem, a5[f"eq{i}"])
                nv.scalar_tensor_tensor(out=fq[:, blk], in0=fq[:, blk], scalar=1.0, in1=ps[:, 6 + i % 2, :],
                                        op0=ALU.min, op1=ALU.max).then_inc(v5.sem, v5.step(f"fq{i}"))
            for i in range(8):
                dve.wait_ge(t5.sem, t5[f"kv{i}"])
                nv.tensor_tensor(out=kv_t[:, i * BANK:(i + 1) * BANK].rearrange("p (r n) -> p r n", r=4),
                                 in0=ps[:, i % 2, :].rearrange("p (r n) -> p r n", r=4),
                                 in1=p3["blocks"].unsqueeze(1).broadcast_to([P, 4, P]), op=ALU.mult)\
                    .then_inc(v5.sem, v5.step(f"kvt{i}"))
            dve.wait_ge(a5.sem, a5["ks"])
            nv.tensor_tensor(out=ks_bd[:].rearrange("p (n h s) -> p n h s", n=16, h=4),
                             in0=ks_sb[:].rearrange("p (n s) -> p n s", n=16).unsqueeze(2).broadcast_to([P, 16, 4, 2]),
                             in1=rep(c["bmask"].unsqueeze(1).broadcast_to([P, 16, 4]), 2), op=ALU.mult)\
                .then_inc(v5.sem, v5.step("ksb"))
            dve.wait_ge(t5.sem, t5["den"])
            d2 = den2.rearrange("p (h n s) -> p h n s", h=NH, s=2)
            pd = ps[:, 5, 0:T * NHEAD * 2].rearrange("p (h n s) -> p h n s", h=NH, s=2)
            for h in range(NH):
                nv.tensor_tensor(out=d2[:, h, :, :], in0=pd[:, h, :, :],
                                 in1=c["cs"][:, 2 * h:2 * h + 2].unsqueeze(1).broadcast_to([P, B * NHEAD, 2]),
                                 op=ALU.mult).then_inc(v5.sem, v5.step(f"den2{h}"))
            dve.wait_ge(v5.sem, v5["den21"])
            nv.reduce_sum(den, den2.rearrange("p (n s) -> p n s", s=2), axis=AX.X).then_inc(v5.sem, v5.step("den"))
            dve.wait_ge(v5.sem, v5["den"])
            nv.tensor_scalar(den, den, 1e-5, None, ALU.add).then_inc(v5.sem, v5.step("deneps"))
            dve.wait_ge(v5.sem, v5["deneps"])
            nv.reciprocal(den, den).then_inc(v5.sem, v5.step("deninv"))
            for i in range(8):
                blk = slice(i * BANK, (i + 1) * BANK)
                dve.wait_ge(t5.sem, t5[f"qn{i}"])
                nv.tensor_tensor(out=fq[:, blk], in0=fq[:, blk], in1=ps[:, i % 2, :], op=ALU.mult)\
                    .then_inc(v5.sem, v5.step(f"qn{i}"))
            dve.wait_ge(t5.sem, t5["out"])
            fo = ps[:, 4, :].rearrange("p (h b s e) -> p h b s e", b=B, h=NH, s=2)
            x4v, x5v = tokhb(x4d), tokhb(x5t)
            for h in range(NH):
                nv.scalar_tensor_tensor(out=x4v[:, h, :, :], in0=fo[:, h, :, 0, :], scalar=c["cs"][:, 2 * h:2 * h + 1],
                                        in1=tokhb(x4t)[:, h, :, :], op0=ALU.mult, op1=ALU.add)\
                    .then_inc(v5.sem, v5.step(f"cos{h}"))
            dve.wait_ge(v5.sem, v5["cos1"])
            nv.tensor_tensor(out=tok(x4d), in0=tok(x4d), in1=p3["denseb"].unsqueeze(1).broadcast_to([P, T, D]),
                             op=ALU.add).then_inc(v5.sem, v5.step("bias"))
            dve.wait_ge(v5.sem, v5["bias"])
            for h, name in enumerate(("sin0", "x5")):
                nv.scalar_tensor_tensor(out=x5v[:, h, :, :], in0=fo[:, h, :, 1, :],
                                        scalar=c["cs"][:, 2 * h + 1:2 * h + 2], in1=x4v[:, h, :, :],
                                        op0=ALU.mult, op1=ALU.add).then_inc(v5.sem, v5.step(name))
            dve.wait_ge(v5.sem, v5["x5"])

            layernorm(x5t, v6, "rstd5")
            dve.wait_ge(t6.sem, t6["aug1"])
            nv.tensor_copy(sh[:, :, KU - 1 + P:], ps[0:D, 1, :].rearrange("p (b n) -> p b n", b=B))\
                .then_inc(v6.sem, v6.step("aug1"))
            for t in range(T):
                b, h = t % B, t // B
                dve.wait_ge(t6.sem, t6[f"v{t}"])
                nv.tensor_scalar(vv.rearrange("p (k h b m e) -> p k h b m e", k=NF, h=NH, b=B, m=2)[:, :, h, b, 1, :],
                                 ps[:, 3 + 2 * (t % 2), :].rearrange("p (k e) -> p k e", k=NF), c["sgn"], None, ALU.mult)\
                    .then_inc(v6.sem, v6.step(f"vm{t}"))
            dve.wait_ge(t6.sem, t6["out"])
            so = ps[:, 6, :].rearrange("p (h b m e) -> p h b m e", h=NH, b=B, m=2)
            sv, yv = tokhb(stu_m), tokhb(x6t)
            for h in range(NH):
                nv.tensor_scalar(sv[:, h, :, :], so[:, h, :, 1, :], winsgn[:, h:h + 1], None, ALU.mult)\
                    .then_inc(v6.sem, v6.step(f"m{h}"))
            dve.wait_ge(v6.sem, v6["m1"])
            for h in range(NH):
                nv.scalar_tensor_tensor(out=yv[:, h, :, :], in0=so[:, h, :, 0, :], scalar=window[:, h:h + 1],
                                        in1=sv[:, h, :, :], op0=ALU.mult, op1=ALU.add)\
                    .then_inc(v6.sem, v6.step(f"y{h}"))
            dve.wait_ge(v6.sem, v6["y1"])
            nv.tensor_tensor(out=x6t, in0=x6t, in1=x5t, op=ALU.add).then_inc(v6.sem, v6.step("x6"))

        @block.tensor
        def _(pe):
            def mm(out_ap, lhsT, rhs, start=True, stop=True):
                return nc.tensor.matmul(out_ap, lhsT, rhs, start=start, stop=stop)

            pe.wait_ge(d_front, 16)
            pe.wait_ge(v0.sem, v0["xg"])
            for j, (name, dst) in enumerate((("q", ps[:, 0, 0:N]), ("k", ps[:, 0, N:2 * N]), ("v", ps[:, 1, 0:N]))):
                mm(dst, f["wqkv"][:, j * P:(j + 1) * P], xg[:]).then_inc(t0.sem, t0.step(name))
            pe.wait_ge(d_pw, 16)
            pwv = pw[:, 0:5 * K2 * P].rearrange("p (s t c) -> p s t c", s=5, t=K2)
            wo = pw[:, 5 * K2 * P:]
            for t in range(K2):
                for s in range(5):
                    n0, n = s * 2 * K2, (2 * K2 if s < G else K2)
                    at = (t % 5) * NOFF + n0
                    ins = mm(ps[:, 6 + t // 5, at:at + n],
                             pwv[:, s, t, :], wo[:, n0:n0 + n])
            ins.then_inc(t0.sem, t0.step("comp"))
            pe.wait_ge(v0.sem, v0["q8"])
            pe.wait_ge(a0.sem, a0["v"])
            for h in range(NH):
                ins = nc.tensor.transpose(ps[:, 1, N + h * P:N + (h + 1) * P], q_mid[:, h * P:(h + 1) * P], ident)
            ins.then_inc(t0.sem, t0.step("qtok"))
            pe.wait_ge(v0.sem, v0["shift2"])
            pe.wait_ge(a0.sem, a0["comp1"])
            for b in range(B):
                rows = slice(b * C, (b + 1) * C)
                for h in range(NH):
                    for t in range(K2):
                        at = (t // 3) * W + t % 3 + h * P
                        ins = mm(ps[:, 2 + b, h * NOFF:(h + 1) * NOFF],
                                 qf[rows, t % 3, at:at + P], compv[rows, t, :],
                                 start=t == 0, stop=t == K2 - 1)
            ins.then_inc(t0.sem, t0.step("offsets"))
            pe.wait_ge(v0.sem, v0["v8"])
            pe.wait_ge(a0.sem, a0["qtok"])
            TB = (0, 1, 6, 7)
            for i in range(4):
                for k in range(4):
                    at = (i // 2) * P + (k // 2) * W + k % 2
                    ins = nc.tensor.transpose(ps[:, TB[i], k * P:(k + 1) * P], kvv[:, i % 2, at:at + P], ident)
                ins.then_inc(t0.sem, t0.step(f"table{i}"))

            def index_group(u, i):
                n = u * 9 + i
                if n >= 2:
                    pe.wait_ge(s_bce, n - 1)
                for q in range(4):
                    ins = mm(ps[:, n % 2, q * P:(q + 1) * P],
                             index[:, u * J + 4 * i + q:u * J + 4 * i + q + 1].broadcast_to([P, P]), identb[:])
                ins.then_inc(s_bc, 1)

            pe.wait_ge(v0.sem, v0["rest3"])
            for i in range(9):
                index_group(0, i)
            pe.wait_ge(v0.sem, v0["gate"])
            for u in range(T):
                b = u // NH
                for i in range(9):
                    if u + 1 < T:
                        index_group(u + 1, i)
                    for j in range(4 * i, 4 * i + 4):
                        n, slot = (u * J + j) // 8, (u * J + j) % 8
                        if j in (0, J // 2):
                            pe.wait_ge(s_oh, 2 * u + 1 + (j > 0))
                        if slot == 0 and n >= 4:
                            pe.wait_ge(s_ge, n - 3)
                        for q in range(2):
                            for part in range(3):
                                ins = mm(ps[:, 2 + n % 4, slot * SLOT:(slot + 1) * SLOT], ohv[:, u % 2, q, j, :],
                                         tabv[:, q, part, b * G + j // K2, :, :].rearrange("p k d -> p (k d)"),
                                         start=(q, part) == (0, 0), stop=(q, part) == (1, 2))
                        if slot == 7:
                            ins.then_inc(s_gp, 1)
                        if j == J - 1:
                            if slot == 7:
                                pe.wait_ge(s_gp, n + 1)
                                pe.sem_inc(s_un, 1)
                            else:
                                ins.then_inc(s_un, 1)

            pe.wait_ge(v1.sem, v1[f"att{B - 1}"])
            for h in range(NH):
                ins = nc.tensor.transpose(ps[:, 0, h * P:(h + 1) * P], att[:, h * P:(h + 1) * P], ident)
            ins.then_inc(t2.sem, t2.step("attT"))
            pe.wait_ge(d_l1, 32)
            pe.wait_ge(a2.sem, a2["attT"])
            mm(ps[:, 1, 0:N], p1["wproj"], att_ch).then_inc(t2.sem, t2.step("proj"))
            pe.wait_ge(v2.sem, v2["poolbd"])
            mm(ps[0:4, 2, 0:B], p1["red"], pool_bd[:]).then_inc(t2.sem, t2.step("poolred"))
            pe.wait_ge(a2.sem, a2["poolred"])
            mm(ps[:, 3, 0:4], pool_red[:], attk[:]).then_inc(t2.sem, t2.step("katt"))
            pe.wait_ge(v2.sem, v2["mixbd"])
            for t in range(K2):
                ins = mm(ps[:, 4, 0:N], wmix_bd[:, t * P:(t + 1) * P], xp[:, t // 3:t // 3 + H, t % 3:t % 3 + W],
                         start=t == 0, stop=t == K2 - 1)
            ins.then_inc(t2.sem, t2.step("conv"))
            pe.wait_ge(v2.sem, v2["x2"])
            for h in range(NH):
                ins = nc.tensor.transpose(ps[:, 5, h * P:(h + 1) * P], x2[:, h * P:(h + 1) * P], ident)
            ins.then_inc(t2.sem, t2.step("x2T"))

            pe.wait_ge(v3.sem, v3["ln"])
            for h in range(NH):
                ins = nc.tensor.transpose(ps[:, 0, h * P:(h + 1) * P], ln[:, h * P:(h + 1) * P], ident)
            ins.then_inc(t3.sem, t3.step("lnT"))
            pe.wait_ge(d_l2, 16)
            pe.wait_ge(a3.sem, a3["lnT"])
            mm(ps[:, 1, 0:N], p2["wq"], ln_ch).then_inc(t3.sem, t3.step("qc"))
            mm(ps[:, 2, 0:N], p2["wk"], ln_ch).then_inc(t3.sem, t3.step("kc"))
            for h in range(NH):
                ins = mm(ps[:, 3, h * P:(h + 1) * P], ln_ch[:, h * P:(h + 1) * P], p2["wv"])
            ins.then_inc(t3.sem, t3.step("vt"))
            pe.wait_ge(a3.sem, a3["qc"])
            pe.wait_ge(v3.sem, v3["kc"])
            for b in range(B):
                rows = slice(b * C, (b + 1) * C)
                mm(ps[:, 4 + b, 0:P], qc[rows, 0:P], kc[rows, 0:P])
                ins = mm(ps[:, 4 + b, P:3 * P], qc[rows, P:2 * P], kc[rows, :])
            ins.then_inc(t3.sem, t3.step("score"))
            pe.wait_ge(a3.sem, a3["vt"])
            for b in range(B):
                pe.wait_ge(a3.sem, a3[f"exp{B + b}"])
                for r in range(3):
                    ins = nc.tensor.transpose(ps[:, b, r * P:(r + 1) * P], prob[:, (b * 3 + r) * P:(b * 3 + r + 1) * P],
                                              ident)
                ins.then_inc(t3.sem, t3.step(f"pt{b}"))
            pe.wait_ge(a3.sem, a3["pt2"])
            pe.wait_ge(v3.sem, v3["pt3"])
            for b in range(B):
                def blk(r):
                    return prob_t[:, (b * 3 + r) * P:(b * 3 + r + 1) * P]

                def vals(h):
                    return vt[:, h * P + b * C:h * P + (b + 1) * C]
                first, second = (ps[:, 4, (h * B + b) * C:(h * B + b + 1) * C] for h in range(NH))
                mm(first, blk(0), vals(0))
                mm(second, blk(1), vals(0), stop=False)
                ins = mm(second, blk(2), vals(1), start=False)
            ins.then_inc(t3.sem, t3.step("pv"))

            def augmented(steps):
                for t in range(T):
                    ins = nc.tensor.transpose(ps[0:C, t // 4, (t % 4) * P:(t % 4 + 1) * P], ln[:, t * C:(t + 1) * C], ident)
                    if t % 4 == 3:
                        ins.then_inc(steps.sem, steps.step(f"aug{t // 4}"))

            pe.wait_ge(v4.sem, v4["ln"])
            augmented(t4)
            pe.wait_ge(d_moe, 16)
            pe.wait_ge(a4.sem, a4["aug0"])
            pe.wait_ge(v4.sem, v4["aug1"])
            for t in range(T):
                ins = mm(ps[:, 2, t * E:(t + 1) * E], augt[:, t, :], moe[:, E * C:])
            ins.then_inc(t4.sem, t4.step("router"))
            for t in range(T):
                ins = mm(ps[:, 4 + t // 2, (t % 2) * E * C:(t % 2 + 1) * E * C], augt[:, t, :], moe[:, 0:E * C])
            ins.then_inc(t4.sem, t4.step("experts"))

            pe.wait_ge(v5.sem, v5["ln"])
            augmented(t5)
            pe.wait_ge(vz.sem, vz["lbias"])
            pe.wait_ge(a5.sem, a5["aug0"])
            pe.wait_ge(v5.sem, v5["aug1"])
            DH = NHEAD * D
            for t in range(T):
                if t >= 2:
                    pe.wait_ge(v5.sem, v5[f"fk{t - 2}"])
                    pe.wait_ge(a5.sem, a5[f"vs{t - 2}"])
                mm(ps[:, 2 + 2 * (t % 2), :], augt[:, t, :], l3w[:, DH:2 * DH]).then_inc(t5.sem, t5.step(f"k{t}"))
                mm(ps[:, 3 + 2 * (t % 2), :], augt[:, t, :], l3w[:, 2 * DH:]).then_inc(t5.sem, t5.step(f"v{t}"))
            for i in range(8):
                if i >= 2:
                    pe.wait_ge(v5.sem, v5[f"fq{i - 2}"])
                mm(ps[:, 6 + i % 2, :], l3w[:, (i // 2) * P:(i // 2 + 1) * P],
                   augt[:, (i % 2) * 4:(i % 2) * 4 + 4, :]).then_inc(t5.sem, t5.step(f"q{i}"))
            pe.wait_ge(a5.sem, a5[f"vs{T - 1}"])
            pe.wait_ge(v5.sem, v5[f"fk{T - 1}"])

            def part(buf, t, hg):
                return buf[:, t * BANK + hg * P:t * BANK + (hg + 1) * P]

            for i in range(16):
                b, hg = i // HG, i % HG
                if i % 2 == 0 and i >= 4:
                    pe.wait_ge(v5.sem, v5[f"kvt{i // 2 - 2}"])
                for s, val in enumerate((vcos, vsin)):
                    at = (i % 2) * 2 * P + s * P
                    for h in range(NH):
                        ins = mm(ps[:, (i // 2) % 2, at:at + P], part(val, h * B + b, hg), part(fk, h * B + b, hg),
                                 start=h == 0, stop=h == NH - 1)
                if i % 2:
                    ins.then_inc(t5.sem, t5.step(f"kv{i // 2}"))
            for i in range(16):
                b, hg = i // HG, i % HG
                for h in range(NH):
                    ins = mm(ps[:, 4, 2 * i:2 * i + 2], part(fk, h * B + b, hg), c["cs"][:, 2 * h:2 * h + 2],
                             start=h == 0, stop=h == NH - 1)
            ins.then_inc(t5.sem, t5.step("ks"))
            pe.wait_ge(v5.sem, v5["kvt7"])
            for i in range(16):
                for s in range(2):
                    at = (i % 8) * 2 * D + s * D
                    ins = mm(ps[:, 2 + i // 8, at:at + D], kv_t[:, (2 * i + s) * P:(2 * i + s + 1) * P],
                             p3["dense"][:, (i % HG) * D:(i % HG + 1) * D])
            ins.then_inc(t5.sem, t5.step("mcs"))
            pe.wait_ge(v5.sem, v5["ksb"])
            for t in range(T):
                b = t % B
                for hg in range(HG):
                    i = b * HG + hg
                    ins = mm(ps[:, 5, (t * HG + hg) * 8:(t * HG + hg + 1) * 8],
                             fq[:, hg * T * P + t * P:hg * T * P + (t + 1) * P], ks_bd[:, i * 8:(i + 1) * 8])
            ins.then_inc(t5.sem, t5.step("den"))
            pe.wait_ge(v5.sem, v5["deninv"])
            for t in range(T):
                ins = nc.tensor.transpose(ps[0:NHEAD, 6 + t // 4, (t % 4) * P:(t % 4 + 1) * P],
                                          den[:, t * NHEAD:(t + 1) * NHEAD], ident)
            ins.then_inc(t5.sem, t5.step("denT"))
            pe.wait_ge(a5.sem, a5["denT1"])
            for i in range(8):
                if i >= 2:
                    pe.wait_ge(v5.sem, v5[f"qn{i - 2}"])
                mm(ps[:, i % 2, :], ex[:, (i // 2) * P:(i // 2 + 1) * P], den_t[:, (i % 2) * BANK:(i % 2 + 1) * BANK])\
                    .then_inc(t5.sem, t5.step(f"qn{i}"))
            pe.wait_ge(v5.sem, v5["qn7"])
            for t in range(T):
                b = t % B
                for hg in range(HG):
                    i = b * HG + hg
                    ins = mm(ps[:, 4, t * 2 * D:(t + 1) * 2 * D], fq[:, hg * T * P + t * P:hg * T * P + (t + 1) * P],
                             mcs[:, i * 2 * D:(i + 1) * 2 * D], start=hg == 0, stop=hg == HG - 1)
            ins.then_inc(t5.sem, t5.step("out"))

            pe.wait_ge(v6.sem, v6["ln"])
            augmented(t6)
            pe.wait_ge(g0.sem, g0["sm"])
            pe.wait_ge(a6.sem, a6["aug0"])
            pe.wait_ge(v6.sem, v6["aug1"])
            for t in range(T):
                b, h = t % B, t // B
                if t >= 2:
                    pe.wait_ge(a6.sem, a6[f"vp{t - 2}"])
                    pe.wait_ge(v6.sem, v6[f"vm{t - 2}"])
                u = sh[:, b, KU - 1 + h * P:KU - 1 + (h + 1) * P]
                mm(ps[:, 2 + 2 * (t % 2), :], u, sm[:, 0:NF * D])
                mm(ps[:, 3 + 2 * (t % 2), :], u, sm[:, NF * D:]).then_inc(t6.sem, t6.step(f"v{t}"))
            pe.wait_ge(d_toep, 16)
            pe.wait_ge(a6.sem, a6[f"vp{T - 1}"])
            pe.wait_ge(v6.sem, v6[f"vm{T - 1}"])
            for k in range(NF):
                mm(ps[:, 6, :], toep[:, k * N:k * N + P], vv[:, k * BANK:(k + 1) * BANK], start=k == 0, stop=False)
                mm(ps[:, 6, BANK // 2:], toep[:, k * N + P:(k + 1) * N], vv[:, k * BANK:k * BANK + BANK // 2],
                   start=False, stop=False)
            for t in range(T):
                b, h = t % B, t // B
                at = (h * B + b) * 2 * D
                for i in range(KU):
                    u = sh[:, b, KU - 1 - i + h * P:KU - 1 - i + (h + 1) * P]
                    ins = nc.tensor.matmul(ps[:, 6, at:at + D], u, msel[:, 2 * NF * D + i * D:2 * NF * D + (i + 1) * D],
                                           start=False, stop=(t, i) == (T - 1, KU - 1))
            ins.then_inc(t6.sem, t6.step("out"))


def kernel(**inputs):
    import numpy as np
    import concourse.bacc as bacc
    from concourse.bass_utils import run_bass_kernel_spmd

    a = {k: np.asarray(v) for k, v in inputs.items()}
    f32 = np.float32

    def pack(block, parts):
        return np.concatenate([np.asarray(parts[n], f32).reshape(-1, w) for n, w in block], axis=1)

    def rows(v, n=P):
        return np.broadcast_to(np.asarray(v, f32).reshape(1, -1), (n, np.size(v)))

    def images(v):
        v = np.asarray(v).reshape(C, -1)
        return np.concatenate([v] * B, axis=0)

    def diagonal(w):
        out = np.zeros((P, P), w.dtype)
        for b in range(B):
            out[b * C:(b + 1) * C, b * C:(b + 1) * C] = w
        return out

    p = np.arange(P)
    part = np.arange(2)[:, None]
    eye = np.eye(P, dtype=f32)
    grid = np.zeros((P, NH, G, K2, 2), f32)
    for g in range(G):
        dil = 2 * g + 1
        for t in range(K2):
            for h in range(NH):
                n = h * P + p
                grid[:, h, g, t, 0] = n // W + (t // 3 - 1) * dil
                grid[:, h, g, t, 1] = n % W + (t % 3 - 1) * dil
    turn = (1.57 * np.arange(N, dtype=f32) / N).astype(f32).reshape(NH, P).T
    cst = pack(CST, {
        "ident": eye, "bmask": (p[:, None] // C == np.arange(B)).astype(f32), "base": grid.reshape(P, -1),
        "boff": rows(np.concatenate([a["L0_conv_b_off"].reshape(-1), a["L0_conv_b_mask"]])),
        "pidx": np.stack([p, p + P], 1).astype(f32),
        "cs": np.stack([np.cos(turn), np.sin(turn)], 2).reshape(P, -1),
        "sgn": np.where(p % 2 == 0, 1.0, -1.0), "tokidx": np.stack([p, p + P], 1),
        "lt4": rows(np.tril(np.ones((4, 4)), -1)), "lt8": rows(np.tril(np.ones((8, 8)), -1)),
        "neghalf": np.full((P, 8), -0.5), "quarter": np.full((P, NF), 0.25),
        "frac": rows(np.array([N, N // 2, N // 4, N // 8])),
        "gumbel": rows(a["L3_ffn_gumbel"]), "logw": rows(a["L3_ffn_log_weights"])})
    w_dw = a["L0_conv_w_dw"].reshape(3, C, K2)
    front = pack(FRONT, {
        "wqkv": np.concatenate([diagonal(a["L0_conv_w_qkv"][:, j * C:(j + 1) * C]) for j in range(3)], 1),
        "wdw": images(w_dw.transpose(1, 0, 2)), "bqkv": images(a["L0_conv_b_qkv"].reshape(3, C).T),
        "bdw": images(a["L0_conv_b_dw"].reshape(3, C).T)})
    pw = np.zeros((C, 5, K2, C), f32)
    for s in range(5):
        w = a["L0_conv_pconv_off_w"][s] if s < G else a["L0_conv_pconv_mask_w"]
        pw[:HC, s, :, :HC] = w.reshape(HC, HC, K2).transpose(0, 2, 1)
        pw[HC:, s, K2 // 2, HC:] = eye[HC:C, HC:C]
    wo = np.concatenate([a["L0_conv_w_off"].reshape(G * 2 * K2, C), a["L0_conv_w_mask"]], 0).T
    pw = np.concatenate([np.tile(pw, (1, 1, 1, B)).reshape(C, -1), wo], 1)
    l1 = pack(L1, {
        "wproj": diagonal(a["L0_conv_w_proj"]), "bproj": images(a["L0_conv_b_proj"]),
        "red": images(a["L1_conv_reduction_kernel"]),
        "convk": images(a["L1_conv_conv_kernels"].reshape(4, K2, C, C).transpose(2, 0, 1, 3)),
        "kbias": images(a["L1_conv_bias"].T), "bnscale": images(a["L1_conv_bn_scale"]),
        "bnbias": images(a["L1_conv_bn_bias"]), "bnmean": images(a["L1_conv_bn_mean"]),
        "bnvar": images(a["L1_conv_bn_var"])})
    future = np.where(p[None, :] > p[:, None], -1e12, 0.0).astype(f32)
    l2 = pack(L2, {"wq": diagonal(a["L2_attn_Wq"]), "wk": diagonal(a["L2_attn_Wk"]), "wv": diagonal(a["L2_attn_Wv"]),
                   "causal": np.concatenate([future, np.zeros((P, P), f32), future], 1)})
    moe = np.concatenate([
        np.concatenate([a["L2_ffn_expert_w"].transpose(1, 0, 2).reshape(C, -1), a["L2_ffn_expert_b"].reshape(1, -1)], 0),
        np.concatenate([a["L2_ffn_router_w"], a["L2_ffn_router_b"].reshape(1, -1)], 0)], 1)
    l3w = np.concatenate([np.concatenate([a[f"L3_attn_w{n}_w"].T, a[f"L3_attn_w{n}_b"].reshape(1, -1)], 0)
                          for n in "qkv"], 1)
    l3 = pack(L3, {"dense": a["L3_attn_dense_w"].T.reshape(HG, P, D).transpose(1, 0, 2).reshape(P, -1),
                   "blocks": (p[:, None] // D == p[None, :] // D), "denseb": rows(a["L3_attn_dense_b"])})
    ex = (np.arange(NHEAD)[:, None] == np.arange(NHEAD * D)[None, :] // D).astype(f32)
    mphi = np.stack([a["L3_ffn_M_phi_plus"], a["L3_ffn_M_phi_minus"]], 1)
    stu = np.concatenate([mphi.transpose(3, 0, 1, 2, 4).reshape(D, NSC, -1),
                          a["L3_ffn_M_u"].transpose(2, 0, 1, 3).reshape(D, NSC, -1)], 2).reshape(D, -1)
    stu = np.concatenate([stu, rows(a["L3_ffn_sigma"], D)], 1)
    phi = np.concatenate([np.zeros((P - 1, NF), f32), a["L3_ffn_phi"][:N]], 0)
    toep = phi[(np.arange(N)[None, :] - p[:, None]) + P - 1].transpose(0, 2, 1).reshape(P, -1)
    x_ch = a["x"].reshape(B, N, C).transpose(0, 2, 1).reshape(P, N)

    host = dict(x_ch=x_ch, cst=cst, front=front, pw=pw, l1=l1, attk=a["L1_conv_attention_kernel"], l2=l2, moe=moe,
                l3w=l3w, l3=l3, ex=ex, stu=stu, toep=toep)
    nc = bacc.Bacc("TRN2", target_bir_lowering=False, num_devices=1)
    arrays, args = {}, []
    for name, v in host.items():
        v = np.ascontiguousarray(v, dtype=f32)
        arrays[f"in_{name}"] = v
        args.append(nc.dram_tensor(f"in_{name}", v.shape, F32, kind="ExternalInput").ap())
    args.append(nc.dram_tensor("out_x", (P, T * C), F32, kind="ExternalOutput").ap())
    hybrid(nc, *args)
    r = run_bass_kernel_spmd(nc, [arrays], core_ids=[0])
    got = r.results[0]["out_x"]
    return got.reshape(P, NH, B, C).transpose(2, 1, 0, 3).reshape(B, H, W, C)
```

```python
from contextlib import ExitStack

import concourse.bass as bass
from concourse import mybir

F32 = mybir.dt.float32
BF16 = mybir.dt.bfloat16
ALU = mybir.AluOpType
ACT = mybir.ActivationFunctionType
AX = mybir.AxisListType

P = 128
B, H, W, C = 4, 16, 16, 32
N = H * W
NH = N // P
T = B * NH
G, HC, K2 = 4, 8, 9
J = G * K2
NOFF = J * 2 + K2
KV = 2 * HC
SLOT = 4 * KV
HP, WP = H + 2, W + 2
E = 8
NHEAD, D = 16, 32
HG = NHEAD * D // P
NF = 16
KU = 3
NSC = 4
STU = 2 * NF * D + KU * D
DH = NHEAD * D
HCOLS = 2 * P + 2
ROUND = 1.5 * 2.0 ** 23
BANK = 512

CST = (("ident", P), ("bmask", B), ("base", NH * 2 * J), ("boff", NOFF), ("pidx", 2), ("cs", 2 * NH),
       ("sgn", 1), ("tokidx", NH), ("lt4", 16), ("lt8", 64), ("neghalf", 8), ("quarter", NF), ("frac", NSC),
       ("fold", C), ("headsel", 64),
       ("gumbel", NSC), ("logw", NSC))
FRONT = (("wqkv", 3 * P), ("wdw", 27), ("bqkv", 3), ("bdw", 3), ("select", P), ("bmask8", B))
AROUND = (0, 1, 2, 3, 5, 6, 7, 8)
PWK = 5 * HC + C
L1 = (("wproj", P), ("bproj", 1), ("red", 4), ("convk", 4 * K2 * C), ("kbias", 4), ("bnscale", 1),
      ("bnbias", 1), ("bnmean", 1), ("bnvar", 1))
L2 = (("wq", P), ("wk", P), ("wv", P), ("causal", 3 * P))
L3 = (("dense", HG * D), ("denseb", D), ("wv", HG * P), ("bv", 3 * HG))
TURN = (("cs_out", N), ("expand", NHEAD * D))
NPART = 3 * NHEAD


def width(block):
    return sum(n for _, n in block)


def columns(tensor, block):
    out, at = {}, 0
    for name, n in block:
        out[name] = tensor[:, at:at + n]
        at += n
    return out


class Steps:

    def __init__(self, semaphore, names):
        self.sem, self.names, self.said = semaphore, names.split(), 0
        assert len(set(self.names)) == len(self.names)

    def __getitem__(self, name):
        return self.names.index(name) + 1

    def step(self, name):
        assert self.names[self.said] == name, (self.names[self.said], name)
        self.said += 1
        return 1


def hybrid(nc, x_ch, cst_d, front_d, pw_d, l1_d, attk_d, l2_d, moe_d, moeb_d, l3w_d, l3b_d, l3_d, turn_d, stu_d, toep_d, out, DBG=()):
    with ExitStack() as ctx:
        def sb(name, shape, dt=F32):
            return ctx.enter_context(nc.sbuf_tensor(name, shape, dt))

        def sem(name):
            return ctx.enter_context(nc.semaphore(name))

        x = sb("x", [P, N])
        cst = sb("cst", [P, width(CST)])
        front = sb("front", [P, width(FRONT)])
        l1 = sb("l1", [P, width(L1)])
        attk = sb("attk", [4, 4])
        l2 = sb("l2", [P, width(L2)])
        moe = sb("moe", [P, E * C + E])
        moeb = sb("moeb", [P, E * C + E])
        moe_w1 = sb("moe_w1", [P, E * C + E], BF16)
        moe_w2 = sb("moe_w2", [P, E * C + E], BF16)
        l3w = sb("l3w", [P, 3 * DH])
        l3 = sb("l3", [P, width(L3)])
        stu_fq = sb("stu_fq", [P, NSC * STU + NF])
        stu, fq = stu_fq[:], stu_fq[:, 0:4096]
        biasb = stu_fq[:].bitcast(BF16)
        c, f, p1, p2, p3 = columns(cst, CST), columns(front, FRONT), columns(l1, L1), columns(l2, L2), columns(l3, L3)
        ident = c["ident"]
        identb = sb("identb", [P, P], BF16)
        neg1 = sb("neg1", [P, 1])
        pos1 = sb("pos1", [P, 1])

        stats = sb("stats", [P, 6])
        moments = sb("moments", [P, 2])
        var_eps = sb("var_eps", [P, T])
        rstd = sb("rstd", [P, T])
        bn_var_eps = sb("bn_var_eps", [P, 1])
        bn_inv = sb("bn_inv", [P, 1])
        xg = sb("xg", [P, N])
        qkv_pad = sb("qkv_pad", [P, 3 * HP * WP])
        q_flat = sb("q_flat", [P, N + 2 * (W + 1)])
        kv = sb("kv", [P, 2 * (N + WP)])
        comp = sb("comp", [P, 2 * T * C])
        q_tok = sb("q_tok", [P, T * C])
        base = sb("base_b", [P, NH * 2 * J])
        w4 = sb("w4", [P, T * J * 4])
        gate_m = sb("gate_m", [P, T * K2])
        mask_x = sb("mask_x", [P, T * J])
        index = sb("index", [P, T * J], BF16)
        table = sb("table", [P, 2 * 3 * B * G * SLOT], BF16)
        indexb = sb("indexb", [P, 2 * J * P], BF16)
        onehot = sb("onehot", [P, 2 * 2 * J * P], BF16)
        arena = sb("arena", [P, 15296])
        dots = sb("dots", [P, NH * J * 4])
        logit = sb("logit", [P, NH * J])
        peak = sb("peak", [P, NH * G])
        pexp = sb("pexp", [P, NH * J])
        psum_ = sb("psum_", [P, NH * G])
        pinv = sb("pinv", [P, NH * G])
        w4p = sb("w4p", [P, NH * J * 4])
        mixed = sb("mixed", [P, NH * C])
        att = sb("att", [P, T * C])
        x1 = sb("x1", [P, N])
        x1_pad = sb("x1_pad", [P, HP * WP])
        pool = sb("pool", [P, 1])
        pool_bd = sb("pool_bd", [P, B])
        pool_red = sb("pool_red", [4, P])
        kmax = sb("kmax", [P, 1])
        kexp = sb("kexp", [P, 4])
        ksum_ = sb("ksum_", [P, 1])
        kinv = sb("kinv", [P, 1])
        katt = sb("katt", [P, 4])
        bmix = sb("bmix", [P, 4])
        bsum = sb("bsum", [P, 1])
        bshift = sb("bshift", [P, 1])
        x2t = xg
        lsum = sb("lsum", [P, T])
        lneg = sb("lneg", [P, T])
        lvar = sb("lvar", [P, T])
        ln = sb("ln", [P, T * C])
        smax = sb("smax", [P, T])
        ssum = sb("ssum", [P, T])
        sinv = sb("sinv", [P, T])
        rlog = sb("rlog", [P, T * E])
        rank = sb("rank", [P, T * E])
        chosen = sb("chosen", [P, T * E])
        rmax = sb("rmax", [P, T])
        rexp = sb("rexp", [P, T * E])
        rsum = sb("rsum", [P, T])
        ks_sb = sb("ks_sb", [P, HG * B * 2])
        zsel = sb("zsel", [P, NSC])
        zmax = sb("zmax", [P, 1])
        zsum = sb("zsum", [P, 1])
        soft = sb("soft", [P, NSC])
        zgt = sb("zgt", [P, NSC * NSC])
        zeq = sb("zeq", [P, NSC * NSC])
        hard = sb("hard", [P, NSC])
        wsel = sb("wsel", [P, NSC])
        length = sb("length", [P, 1])
        window = sb("window", [P, NH])
        winsgn = sb("winsgn", [P, NH])
        sig4 = sb("sig4", [P, NF])
        msel = sb("msel", [P, STU])

        gath = arena[:, 0:2 * NH * J * SLOT]
        comp_bd, q_stack = arena[:, 0:3 * B * NOFF], arena[:, 1024:1024 + 2 * N]
        fk, vcs = arena[:, 0:4096], arena[:, 4096:4096 + T * HG * HCOLS]
        recip = arena[:, 4096:4096 + 2 * BANK]
        vv, ar_v, toep = arena[:, 0:NF * BANK], arena[:, 8192:8192 + KU * N], arena[:, 8960:8960 + (NF + KU - 1) * N]
        att_ch, y1, x2, ctx_n, qc, kc, vt, ln_ch, x4d, stu_m = (
            arena[:, 12416 + i * N:12416 + (i + 1) * N] for i in range(10))
        side = 2 * NH * J * SLOT
        pos, near, away, hat0, hat1 = (arena[:, side + i * T * 2 * J:side + (i + 1) * T * 2 * J] for i in range(5))
        prod = arena[:, side:side + NH * J * 4 * HC]
        side += 5 * T * 2 * J
        hats = arena[:, side:side + 2 * T * 2 * J]
        side += 2 * T * 2 * J
        rest = arena[:, side:side + 4 * BANK]
        mpart = arena[:, side:side + STU]
        late = onehot[:].bitcast(F32)
        pw = late[0:PWK, 0:3 * P + NOFF]
        gated, late_b = late[:, 4096:4096 + T * C * E], late.bitcast(BF16)
        l3b, w1, w2 = late[:, 0:3 * DH], late_b[:, 3072:3072 + 3 * DH], late_b[:, 4608:4608 + 3 * DH]
        turns = columns(late[:, 3072:3072 + width(TURN)], TURN)
        ks_bd = late[:, 5128:5640]
        prob, prob_t = late[:, 6144:6144 + B * 3 * P], late[:, 7680:7680 + B * 3 * P]
        expandb, den_parts = late_b[:, 12288:12288 + DH], late_b[:, 12800:12800 + T * P]
        den_ch, oc = late[0:32, 6912:6912 + T * P], late[0:2 * D, 7936:7936 + T * P]
        den, den_p = late[:, 4096:4096 + T * NHEAD], late_b[:, 2 * 4224:2 * 4224 + T * NPART]
        late3 = table[:].bitcast(F32)
        late3_b = table[:]
        stu_w1, stu_w2 = late3_b[:, 0:STU], late3_b[:, 4096:4096 + STU]
        x3t, x4t, x5t, x6t = (late3[:, 1024 + i * N:1024 + (i + 1) * N] for i in range(4))
        lcen, lsq = comp[:, 0:T * C], comp[:, T * C:2 * T * C]
        late2 = indexb[:].bitcast(F32)
        score, mcs, req, wmix = (late2[:, 0:1536], late2[:, 1536:2560], late2[:, 1536:1536 + T * E * E],
                                late2[:, 2048:2048 + K2 * C])
        parts, stack1, stack2 = indexb[:, 0:1024], indexb[:, 1024:2048], indexb[:, 2048:3072]
        wmix_bd, rgt = late2[:, 2816:2816 + K2 * P], late2[:, 3968:3968 + T * E * E]

        ps = ctx.enter_context(nc.psum_tensor("ps", [P, 8, BANK], F32))

        d_x, d_cst, d_front, d_pw, d_l1, d_l2, d_moe, d_l3, d_stu, d_toep, d_late, d_out = (
            sem("loaded_" + n) for n in ("x", "cst", "front", "pw", "l1", "l2", "moe", "l3", "stu", "toep", "late", "out"))

        v0 = Steps(sem("vector_front"), "identb neg1 pos1 base stats moments eps xg comp0 comp1 "
                   + " ".join(f"q{t}" for t in range(K2)) + " s20 s21 s30 s31 "
                   + " ".join(f"k{t} v{t}" for t in range(K2))
                   + " pos gate clamp near0 near1 near index rest0 rest1 rest2 rest3 low0 low1 low2 low3"
                   + " away hat0a hat0 gate1 sigmoid maskx hatm w4")
        a0 = Steps(sem("scalar_front"), "q k v s00 s01 s10 s11 qtok high0 high1 high2 high3 mid0 mid1 mid2 mid3"
                   " sigexp hat1a hat1")
        t0 = Steps(sem("tensor_front"), "comp q k v select offsets qtok table0 table1 table2 table3")
        g0 = Steps(sem("pool_steps"), "qkvpad qpad stackpad kvpad xpad rstd0 bnvar bninv sigma "
                   + " ".join(f"m{i} a{i}" for i in range(NSC)) + " sm"
                   + " rstd1 rstd2 ones rstd3 rstd4 "
                   "qn3 qn7 rstd5")
        s_bc = sem("index_spread")
        s_bce = sem("index_copied")
        s_oh = sem("onehot_ready")
        s_gp = sem("samples_in_psum")
        s_ge = sem("samples_copied")
        s_un = sem("unit_gathered")
        PAIR = ("prodk dots wdots logit peak sub expsum inv w4p prodv mixed att").split()
        v1 = Steps(sem("vector_pairs"), " ".join(f"{n}{b}" for b in range(B) for n in PAIR))
        s_px = sem("attention_exp")

        t2 = Steps(sem("tensor_conv"), "attT proj poolred katt conv x2T")
        a2 = Steps(sem("scalar_conv"), "attT poolred kexp y1")
        v2 = Steps(sem("vector_conv"), "x1 stats moments eps xpad pool poolbd kmax kneg kinv katt mix0 mix1 mix2 mix3"
                   " mixbd bmix bsum binv bcent bshift x2 x2t")
        LN = "sum cen sq var eps ln "
        STACK = "ph pr pl s1b s2b "
        v3 = Steps(sem("vector_attn"), LN + "kc score smax0 smax1 sneg sinv pt1 pt3 ctx x3")
        a3 = Steps(sem("scalar_attn"), "lnT qc vt " + " ".join(f"exp{t}" for t in range(T)) + " pt0 pt2")
        t3 = Steps(sem("tensor_attn"), "lnT qc kc vt score pt0 pt1 pt2 pt3 pv")
        v4 = Steps(sem("vector_moe"), LN + STACK + "rlog rgt req reqlt rsum rank rmax rsub chosen esel esum einv gated y ynorm x4")
        a4 = Steps(sem("scalar_moe"), "pm pd s1a s2a rexp")
        t4 = Steps(sem("tensor_moe"), "st0 st1 experts")
        v5 = Steps(sem("vector_linear"), LN + "cs0 cs1 " + STACK
                   + " ".join(f"fk{t} vs{t}" for t in range(T)) + " fq0 fq1 fq2 fq3 kv1 fq4 fq5 fq6 fq7 kv3 bias ksb"
                   + " dc1 cos0 cos1 den0 den1 deneps inv dh dr dm ds dl dp1 "
                   + " ".join(f"qn{i}" for i in range(8) if i % HG < 3) + " oc0 oc1 x5")
        a5 = Steps(sem("scalar_linear"), "pm pd s1a s2a expand " + " ".join(f"ek{t} vc{t}" for t in range(T))
                   + " eq0 eq1 kv0 eq2 eq3 eq4 eq5 kv2 eq6 eq7 dc0 dp0 rt3 rt7")
        t5 = Steps(sem("tensor_linear"), "st0 st1 " + " ".join(f"k{t} v{t}" for t in range(T))
                   + " q0 q1 kv0 q2 q3 kv1 q4 q5 kv2 q6 q7 kv3 den0 den1 denT dp0 dp1 " + " ".join(f"ex{i}" for i in range(8))
                   + " out0 out1 fold")
        tw = Steps(sem("tensor_weights"), "wd")
        aw = Steps(sem("scalar_weights"), "mhi mbh wdw0 wdb0 wdw1 wdb1 wdw2 wdb2 wdw3 wdb3 lhi lbh mmid mbm lmid lbm mw2m mw2h lw2m lw2h shi smid")
        gw = Steps(sem("pool_weights"), "lb1 mres mbres lres lbres mlow mblow llow lblow sres slow")
        vz = Steps(sem("vector_select"), "z zmax zneg zinv soft zgt zeq zeqlt zadd rank hard diff w lenp length win winsgn")
        az = Steps(sem("scalar_select"), "exp")
        v6 = Steps(sem("vector_stu"), LN + STACK + " ".join(f"vm{t}" for t in range(T)) + " ar1 m0 m1 y0 y1 x6")
        a6 = Steps(sem("scalar_stu"), "pm pd s1a s2a " + " ".join(f"vp{t}" for t in range(T)) + " ar0")
        t6 = Steps(sem("tensor_stu"), "st0 st1 " + " ".join(f"v{t}" for t in range(T)) + " out")

        block = ctx.enter_context(nc.Block())

        img = lambda ap: ap.rearrange("p (y x) -> p y x", y=H)
        qkvp = qkv_pad[:].rearrange("p (j y x) -> p j y x", j=3, y=HP)
        q_mid = q_flat[:, W + 1:W + 1 + N]
        q_st = q_stack.rearrange("p (s y x) -> p s y x", s=2, y=H)
        xp = x1_pad[:].rearrange("p (y x) -> p y x", y=HP)
        kvv = kv[:].rearrange("p (j n) -> p j n", j=2)
        tabv = table[:].rearrange("p (q r s k d) -> p q r s k d", q=2, r=3, s=B * G, k=4)
        ohv = onehot[:].rearrange("p (u q j n) -> p u q j n", u=2, q=2, j=J)
        ixb = indexb[:].rearrange("p (u j n) -> p u j n", u=2, j=J)
        gv = gath.rearrange("p (r s d) -> p r s d", r=2, s=NH * J)
        tok = lambda ap: ap.rearrange("p (t c) -> p t c", t=T)
        tokhb = lambda ap: ap.rearrange("p (h b c) -> p h b c", b=B, h=NH)
        vcv = vcs.rearrange("p (t g n) -> p t g n", t=T, g=HG)
        fqv = fq.rearrange("p (g h b n) -> p g h b n", g=HG, h=NH, b=B)
        mcv = mcs.rearrange("p (g b s e) -> p g b s e", g=HG, b=B, s=2)
        partv = parts.rearrange("p (t r c) -> p t r c", t=T, r=4)
        psb = [ps[:, i, :].bitcast(BF16) for i in range(2)]
        arv = ar_v.rearrange("p (i t e) -> p i t e", i=KU, t=T)
        WB = (0, 1, 6, 7)
        BROWS = slice(2 * C, 2 * C + 3)
        GRP = NH * J // 8

        def rep(ap, n):
            return ap.unsqueeze(len(ap.shape)).broadcast_to(list(ap.shape) + [n])

        TB = (4, 5, 6, 7)

        def shifted_queries(copy, r, s):
            tap = AROUND[4 * s + r]
            dy, dx = tap // 3 - 1, tap % 3 - 1
            rows, at = slice(r * C, (r + 1) * C), (dy + 1) * W + dx + 1
            cols = slice(max(0, -dx), W - max(0, dx))
            return copy(q_st[rows, s, :, cols], img(ps[rows, 7, at:at + N])[:, :, cols])

        def bias_hi(layer):
            return biasb[BROWS, 3072 * 2:3072 * 2 + 264] if layer == "m" else biasb[BROWS, 0:3 * DH]

        def bias_mid(layer):
            return biasb[BROWS, 3072 * 2 + 264:3072 * 2 + 528] if layer == "m" else biasb[BROWS, 3 * DH:6 * DH]

        def over_denominator(engine, n, inverse):
            half, hg = n // HG, n % HG
            q = fqv[:, hg, :, 2 * half:2 * half + 2, :].rearrange("p h b n -> p b h n")
            inv = inverse.rearrange("p (b h n) -> p b h n", b=2, h=NH)
            return engine.tensor_tensor(out=q, in0=q, in1=inv, op=ALU.mult)

        def heads_products(copy, hg):
            acc = ps[:, 4:8, 0:2 * P].rearrange("p b (s r e) -> p b s r e", s=2, r=4)
            for r in range(4):
                rows = slice(r * D, (r + 1) * D)
                copy(mcv[rows, hg], acc[rows, :, :, r, :])
            return copy(ks_sb[:, hg * 2 * B:(hg + 1) * 2 * B].rearrange("p (b s) -> p b s", b=B), ps[:, 4:8, 2 * P:HCOLS])

        @block.sync
        def _(sp):
            sp.dma_start(x[:], x_ch).then_inc(d_x, 16)
            sp.dma_start(front[:], front_d).then_inc(d_front, 16)
            sp.dma_start(pw, pw_d).then_inc(d_pw, 16)
            sp.dma_start(l1[:], l1_d).then_inc(d_l1, 16)
            sp.dma_start(attk[:], attk_d).then_inc(d_l1, 16)
            sp.dma_start(l2[:], l2_d).then_inc(d_l2, 16)
            sp.dma_start(moe[:], moe_d).then_inc(d_moe, 16)
            sp.dma_start(moeb[:], moeb_d).then_inc(d_moe, 16)
            sp.dma_start(l3w[:, 0:2 * DH], l3w_d).then_inc(d_l3, 16)
            sp.dma_start(l3[:], l3_d).then_inc(d_l3, 16)
            sp.dma_start(stu, stu_d).then_inc(d_stu, 16)
            sp.wait_ge(s_un, T)
            sp.dma_start(l3b[BROWS, 0:2 * DH], l3b_d).then_inc(d_late, 16)
            sp.dma_start(late[:, 3072:3072 + width(TURN)], turn_d).then_inc(d_late, 16)
            sp.wait_ge(t5.sem, t5["kv3"])
            sp.dma_start(toep, toep_d).then_inc(d_toep, 16)
            sp.wait_ge(v6.sem, v6["x6"])
            sp.dma_start(out, x6t).then_inc(d_out, 16)
            sp.wait_ge(d_out, 16)

        @block.gpsimd
        def _(pool_e):
            nc.gpsimd.memset(qkv_pad[:], 0.0).then_inc(g0.sem, g0.step("qkvpad"))
            nc.gpsimd.memset(q_flat[:], 0.0).then_inc(g0.sem, g0.step("qpad"))
            nc.gpsimd.memset(q_stack, 0.0).then_inc(g0.sem, g0.step("stackpad"))
            nc.gpsimd.memset(kv[:], 0.0).then_inc(g0.sem, g0.step("kvpad"))
            nc.gpsimd.memset(x1_pad[:], 0.0).then_inc(g0.sem, g0.step("xpad"))

            def power(out_ap, in_ap, exponent, name):
                nc.gpsimd.tensor_tensor(out=out_ap, in0=in_ap, in1=exponent, op=ALU.pow).then_inc(g0.sem, g0.step(name))

            pool_e.wait_ge(d_cst, 16)
            pool_e.wait_ge(v0.sem, v0["eps"])
            power(rstd[:, 0:1], var_eps[:, 0:1], c["neghalf"][:, 0:1], "rstd0")
            pool_e.wait_ge(d_l1, 32)
            nc.gpsimd.tensor_scalar(bn_var_eps[:], p1["bnvar"], 1e-5, None, ALU.add).then_inc(g0.sem, g0.step("bnvar"))
            pool_e.wait_ge(g0.sem, g0["bnvar"])
            power(bn_inv[:], bn_var_eps[:], c["neghalf"][:, 0:1], "bninv")
            pool_e.wait_ge(d_stu, 16)
            power(sig4[:], stu[:, NSC * STU:], c["quarter"], "sigma")
            pool_e.wait_ge(vz.sem, vz["w"])
            for i in range(NSC):
                dst = msel if i == 0 else mpart
                if i > 1:
                    pool_e.wait_ge(g0.sem, g0[f"a{i - 1}"])
                nc.gpsimd.tensor_scalar(dst[:], stu[:, i * STU:(i + 1) * STU], wsel[:, i:i + 1], None, ALU.mult)\
                    .then_inc(g0.sem, g0.step(f"m{i}"))
                pool_e.wait_ge(g0.sem, g0[f"m{i}"])
                if i == 0:
                    nc.gpsimd.memset(mpart, 0.0).then_inc(g0.sem, g0.step("a0"))
                    pool_e.wait_ge(g0.sem, g0["a0"])
                else:
                    nc.gpsimd.tensor_tensor(out=msel[:], in0=msel[:], in1=mpart, op=ALU.add)\
                        .then_inc(g0.sem, g0.step(f"a{i}"))
            pool_e.wait_ge(g0.sem, g0[f"a{NSC - 1}"])
            mk = msel[:, 0:2 * NF * D].rearrange("p (m k e) -> p m k e", m=2, k=NF)
            nc.gpsimd.tensor_tensor(out=mk, in0=mk, in1=rep(sig4[:].unsqueeze(1).broadcast_to([P, 2, NF]), D), op=ALU.mult)\
                .then_inc(g0.sem, g0.step("sm"))
            def minus(out_ap, in_ap, part, name, after):
                steps, before = after
                pool_e.wait_ge(steps.sem, steps[before])
                nc.gpsimd.tensor_tensor(out=out_ap, in0=in_ap, in1=part, op=ALU.subtract).then_inc(gw.sem, gw.step(name))

            LROWS = slice(3 * C, P)
            pool_e.wait_ge(d_late, 32)
            pool_e.wait_ge(g0.sem, g0["sm"])
            nc.gpsimd.tensor_scalar(l3b[BROWS, 0:2 * DH], l3b[BROWS, 0:2 * DH], 1.0, None, ALU.add)\
                .then_inc(gw.sem, gw.step("lb1"))
            pool_e.wait_ge(aw.sem, aw["mhi"])
            minus(moe[:], moe[:], moe_w1[:], "mres", (gw, "lb1"))
            pool_e.wait_ge(aw.sem, aw["mbh"])
            minus(moeb[BROWS, :], moeb[BROWS, :], bias_hi("m"), "mbres", (gw, "mres"))
            pool_e.wait_ge(aw.sem, aw["lhi"])
            minus(l3w[:], l3w[:], w1, "lres", (gw, "mbres"))
            pool_e.wait_ge(aw.sem, aw["lbh"])
            minus(l3b[BROWS, :], l3b[BROWS, :], bias_hi("l"), "lbres", (gw, "lres"))
            pool_e.wait_ge(gw.sem, gw["lbres"])
            pool_e.wait_ge(v2.sem, v2["eps"])
            power(rstd[:, 0:1], var_eps[:, 0:1], c["neghalf"][:, 0:1], "rstd1")
            pool_e.wait_ge(aw.sem, aw["mmid"])
            minus(moe_w1[LROWS, :], moe[LROWS, :], moe_w2[LROWS, :], "mlow", (g0, "rstd1"))
            pool_e.wait_ge(aw.sem, aw["mbm"])
            minus(moe_w2[BROWS, :], moeb[BROWS, :], bias_mid("m"), "mblow", (gw, "mlow"))
            pool_e.wait_ge(aw.sem, aw["lmid"])
            minus(w1[LROWS, :], l3w[LROWS, :], w2[LROWS, :], "llow", (gw, "mblow"))
            pool_e.wait_ge(aw.sem, aw["lbm"])
            minus(w2[BROWS, :], l3b[BROWS, :], bias_mid("l"), "lblow", (gw, "llow"))
            for i, v in enumerate((v3, v4, v5, v6)):
                pool_e.wait_ge(v.sem, v["eps"])
                if v is v3:
                    pool_e.wait_ge(gw.sem, gw["lblow"])
                if v is v4:
                    pool_e.wait_ge(g0.sem, g0["ones"])
                power(rstd[:], var_eps[:], c["neghalf"], f"rstd{i + 2}")
                if v is v3:
                    pool_e.wait_ge(aw.sem, aw["shi"])
                    minus(msel[:], msel[:], stu_w1, "sres", (g0, "rstd2"))
                    pool_e.wait_ge(aw.sem, aw["smid"])
                    minus(stu_w1[LROWS, :], msel[LROWS, :], stu_w2[LROWS, :], "slow", (gw, "sres"))
                    pool_e.wait_ge(t3.sem, t3["pv"])
                    pool_e.wait_ge(gw.sem, gw["slow"])
                    nc.gpsimd.memset(stack2[BROWS, :], 1.0).then_inc(g0.sem, g0.step("ones"))
                if v is v5:
                    for n in (3, 7):
                        pool_e.wait_ge(a5.sem, a5[f"rt{n}"])
                        over_denominator(nc.gpsimd, n, recip[:, n // HG * BANK:(n // HG + 1) * BANK])\
                            .then_inc(g0.sem, g0.step(f"qn{n}"))

        @block.scalar
        def _(act):
            act.dma_start(cst[:], cst_d).then_inc(d_cst, 16)

            def copy(out_ap, in_ap, steps, name, scale=1.0):
                nc.scalar.activation(out_ap, in_ap, ACT.Copy, scale=scale).then_inc(steps.sem, steps.step(name))

            act.wait_ge(g0.sem, g0["qkvpad"])
            act.wait_ge(d_front, 16)
            for j, (name, src) in enumerate((("q", ps[:, 0, 0:N]), ("k", ps[:, 0, N:2 * N]), ("v", ps[:, 1, 0:N]))):
                if j == 0:
                    act.wait_ge(t0.sem, t0["v"])
                nc.scalar.activation(qkvp[:, j, 1:1 + H, 1:1 + W], img(src), ACT.Identity, bias=f["bqkv"][:, j:j + 1])\
                    .then_inc(a0.sem, a0.step(name))
            act.wait_ge(g0.sem, g0["stackpad"])
            act.wait_ge(t0.sem, t0["select"])
            for r in (0, 1):
                for s in range(2):
                    shifted_queries(lambda o, i: nc.scalar.activation(o, i, ACT.Copy), r, s)\
                        .then_inc(a0.sem, a0.step(f"s{r}{s}"))
            act.wait_ge(t0.sem, t0["qtok"])
            copy(q_tok[:].rearrange("p (b h c) -> p h b c", b=B, h=NH),
                 ps[:, 1, N:2 * N].rearrange("p (h b c) -> p h b c", h=NH, b=B), a0, "qtok", HC ** -0.5)
            def tab(i, part):
                return tabv[:, i // 2, part, :, :, (i % 2) * HC:(i % 2 + 1) * HC]
            corner = lambda ap: ap.rearrange("p (k s d) -> p s k d", k=4, s=B * G)
            for i in range(4):
                act.wait_ge(t0.sem, t0[f"table{i}"])
                copy(tab(i, 0), corner(ps[:, TB[i], :]), a0, f"high{i}")
            for i in range(4):
                act.wait_ge(v0.sem, v0[f"rest{i}"])
                copy(tab(i, 1), rest[:, i * BANK:(i + 1) * BANK].rearrange("p (s k d) -> p s k d", s=B * G, k=4),
                     a0, f"mid{i}")
            def index_group(u, i):
                n = u * 9 + i
                act.wait_ge(s_bc, n + 1)
                if i == 0 and u >= 2:
                    act.wait_ge(s_oh, 2 * (u - 1))
                nc.scalar.activation(ixb[:, u % 2, 4 * i:4 * i + 4, :].rearrange("p j n -> p (j n)"),
                                     ps[:, n % 2, :], ACT.Copy).then_inc(s_bce, 1)

            def sample_group(n):
                b, i = n // GRP, n % GRP
                act.wait_ge(s_gp, n + 1)
                if i == 0 and b >= 2:
                    act.wait_ge(v1.sem, v1[f"prodv{b - 2}"])
                nc.scalar.activation(gv[:, b % 2, 8 * i:8 * i + 8, :].rearrange("p s d -> p (s d)"),
                                     ps[:, 2 + n % 4, :], ACT.Copy).then_inc(s_ge, 1)

            def pair_exp(b):
                act.wait_ge(v1.sem, v1[f"sub{b}"])
                nc.scalar.activation(pexp[:], logit[:], ACT.Exp).then_inc(s_px, 1)

            for i in range(9):
                index_group(0, i)
            nc.scalar.activation(gate_m[:], gate_m[:], ACT.Exp, scale=-1.0).then_inc(a0.sem, a0.step("sigexp"))
            act.wait_ge(v0.sem, v0["away"])
            nc.scalar.activation(hat1, away, ACT.Abs, bias=neg1[:]).then_inc(a0.sem, a0.step("hat1a"))
            act.wait_ge(a0.sem, a0["hat1a"])
            nc.scalar.activation(hats.rearrange("p (n z) -> p n z", z=2)[:, :, 1], hat1, ACT.Relu,
                                 bias=pos1[:], scale=-1.0).then_inc(a0.sem, a0.step("hat1"))
            done = 0
            for u in range(T):
                for i in range(9):
                    if u + 1 < T:
                        index_group(u + 1, i)
                    while 8 * (done + 1) <= u * J + 4 * i + 4:
                        sample_group(done)
                        done += 1
                    if i == 8 and u == 0:
                        act.wait_ge(vz.sem, vz["zneg"])
                        nc.scalar.activation(soft[:], zsel[:], ACT.Exp, bias=zmax[:], accum_out=zsum[:])\
                            .then_inc(az.sem, az.step("exp"))
                    if i == 6 and u in (3, 5, 7):
                        pair_exp((u - 3) // 2)
            act.wait_ge(d_moe, 32)
            copy(moe_w1[:], moe[:], aw, "mhi")
            act.wait_ge(g0.sem, g0["sm"])
            copy(bias_hi("m"), moeb[BROWS, :], aw, "mbh")
            act.wait_ge(tw.sem, tw["wd"])
            for r, bank in enumerate(WB):
                at = lambda ap: ap.rearrange("p (g r e) -> p g r e", g=HG, r=4)[:, :, r, :]
                grp = lambda ap: ap.rearrange("p (g e) -> p g e", g=HG)
                copy(at(l3w[:, 2 * DH:]), grp(ps[:, bank, 0:HG * D]), aw, f"wdw{r}")
                copy(at(l3b[BROWS, 2 * DH:]), grp(ps[0:3, bank, HG * D:2 * HG * D]), aw, f"wdb{r}")
            pair_exp(B - 1)
            act.wait_ge(d_l3, 32)
            act.wait_ge(aw.sem, aw["wdb3"])
            copy(w1, l3w[:], aw, "lhi")
            act.wait_ge(gw.sem, gw["lb1"])
            copy(bias_hi("l"), l3b[BROWS, :], aw, "lbh")
            act.wait_ge(gw.sem, gw["mres"])
            copy(moe_w2[:], moe[:], aw, "mmid")
            act.wait_ge(gw.sem, gw["mbres"])
            copy(bias_mid("m"), moeb[BROWS, :], aw, "mbm")

            act.wait_ge(t2.sem, t2["attT"])
            copy(att_ch, ps[:, 0, 0:N], a2, "attT")
            act.wait_ge(t2.sem, t2["poolred"])
            nc.scalar.activation(pool_red[:].rearrange("p (b c) -> p b c", b=B), rep(ps[0:4, 2, 0:B], C), ACT.Relu).then_inc(a2.sem, a2.step("poolred"))
            act.wait_ge(v2.sem, v2["kneg"])
            nc.scalar.activation(kexp[:], ps[:, 3, 0:4], ACT.Exp, scale=1.0 / 30.0, bias=kmax[:], accum_out=ksum_[:])\
                .then_inc(a2.sem, a2.step("kexp"))
            act.wait_ge(gw.sem, gw["lres"])
            copy(w2, l3w[:], aw, "lmid")
            act.wait_ge(gw.sem, gw["lbres"])
            copy(bias_mid("l"), l3b[BROWS, :], aw, "lbm")
            act.wait_ge(t2.sem, t2["conv"])
            act.wait_ge(v2.sem, v2["bshift"])
            nc.scalar.activation(y1, ps[:, 4, 0:N], ACT.Relu, bias=bshift[:], scale=bn_inv[:])\
                .then_inc(a2.sem, a2.step("y1"))
            for n, w in (("m", moe_w2[:]), ("l", w2)):
                act.wait_ge(gw.sem, gw[n + "blow"])
                two = slice(2 * C, 2 * C + 2)
                copy(w[two, :], (biasb[two, 6144 + 264:6144 + 528] if n == "m" else biasb[two, 3 * DH:6 * DH]), aw, n + "w2m")
                act.wait_ge(aw.sem, aw[n + "w2m"])
                one = slice(2 * C, 2 * C + 1)
                copy(w[one, :], (biasb[one, 6144:6144 + 264] if n == "m" else biasb[one, 0:3 * DH]), aw, n + "w2h")

            act.wait_ge(t3.sem, t3["lnT"])
            copy(ln_ch, ps[:, 0, 0:N], a3, "lnT")
            act.wait_ge(t3.sem, t3["qc"])
            copy(qc, ps[:, 1, 0:N], a3, "qc")
            act.wait_ge(t3.sem, t3["vt"])
            copy(vt, ps[:, 3, 0:N], a3, "vt")
            copy(stu_w1, msel[:], aw, "shi")
            sc = score.rearrange("p (b k) -> p b k", b=B)
            pr = prob.rearrange("p (b k) -> p b k", b=B)
            act.wait_ge(v3.sem, v3["sneg"])
            for t in range(T):
                b, h = t % B, t // B
                keys = slice(0, P) if h == 0 else slice(P, 3 * P)
                nc.scalar.activation(pr[:, b, keys], sc[:, b, keys], ACT.Exp, bias=smax[:, t:t + 1],
                                     accum_out=ssum[:, t:t + 1]).then_inc(a3.sem, a3.step(f"exp{t}"))
            for b in (0, 2):
                act.wait_ge(t3.sem, t3[f"pt{b}"])
                copy(prob_t[:, b * 3 * P:(b + 1) * 3 * P], ps[:, b, 0:3 * P], a3, f"pt{b}")
            act.wait_ge(gw.sem, gw["sres"])
            copy(stu_w2, msel[:], aw, "smid")

            def stacked(v, a, t):
                act.wait_ge(v.sem, v["pr"])
                copy(partv[:, :, 1, :], tok(lsq), a, "pm")
                copy(partv[:, :, 3, :], partv[:, :, 0, :], a, "pd")
                act.wait_ge(t.sem, t["st0"])
                copy(stack1[:, 0:BANK], psb[0][:, 0:BANK], a, "s1a")
                copy(stack2[0:2 * C, 0:BANK], psb[0][0:2 * C, 0:BANK], a, "s2a")

            stacked(v4, a4, t4)
            act.wait_ge(v4.sem, v4["rsub"])
            nc.scalar.activation(rexp[:], rexp[:], ACT.Exp).then_inc(a4.sem, a4.step("rexp"))

            stacked(v5, a5, t5)
            copy(expandb[0:NPART, :], turns["expand"][0:NPART, :], a5, "expand")
            for t in range(T):
                h = t // B
                act.wait_ge(t5.sem, t5[f"k{t}"])
                nc.scalar.activation(fk[:, t * BANK:(t + 1) * BANK], ps[:, 2 * t % 8, :], ACT.Exp, bias=neg1[:])\
                    .then_inc(a5.sem, a5.step(f"ek{t}"))
                act.wait_ge(t5.sem, t5[f"v{t}"])
                copy(vcv[:, t, :, 0:P], ps[:, (2 * t + 1) % 8, :].rearrange("p (g n) -> p g n", g=HG), a5, f"vc{t}",
                     c["cs"][:, 2 * h:2 * h + 1])

            def act_copy(out_ap, in_ap):
                return nc.scalar.activation(out_ap, in_ap, ACT.Copy)

            for i in range(8):
                act.wait_ge(t5.sem, t5[f"q{i}"])
                nc.scalar.activation(fq[:, i * BANK:(i + 1) * BANK], ps[:, i % 4, :], ACT.Exp, bias=neg1[:])\
                    .then_inc(a5.sem, a5.step(f"eq{i}"))
                if i in (1, 5):
                    act.wait_ge(t5.sem, t5[f"kv{i // 2}"])
                    heads_products(act_copy, i // 2).then_inc(a5.sem, a5.step(f"kv{i // 2}"))
            act.wait_ge(t5.sem, t5["den0"])
            copy(den_ch[:, 0:BANK], ps[0:32, 0, :], a5, "dc0")
            act.wait_ge(t5.sem, t5["dp0"])
            copy(den_parts[0:NPART, 0:BANK], psb[0][0:NPART, 0:BANK], a5, "dp0")
            for n in (3, 7):
                act.wait_ge(t5.sem, t5[f"ex{n}"])
                copy(recip[:, n // HG * BANK:(n // HG + 1) * BANK], ps[:, 3 + n % 4, :], a5, f"rt{n}")

            stacked(v6, a6, t6)
            for t in range(T):
                b, h = t % B, t // B
                act.wait_ge(t6.sem, t6[f"v{t}"])
                copy(vv.rearrange("p (k h b m e) -> p k h b m e", k=NF, h=NH, b=B, m=2)[:, :, h, b, 0, :],
                     ps[:, 2 * (t % 3), :].rearrange("p (k e) -> p k e", k=NF), a6, f"vp{t}")
            copy(arv[:, :, 0:B, :], ps[:, 6, 0:B * KU * D].rearrange("p (b i e) -> p i b e", b=B, i=KU), a6, "ar0")

        @block.vector
        def _(dve):
            nv = nc.vector

            def layernorm(src, v, pool_step):
                X = tok(src)
                nv.reduce_sum(lsum[:], X, axis=AX.X).then_inc(v.sem, v.step("sum"))
                dve.wait_ge(v.sem, v["sum"])
                nv.scalar_tensor_tensor(out=tok(lcen), in0=rep(lsum[:], C), scalar=-1.0 / C, in1=X,
                                        op0=ALU.mult, op1=ALU.add).then_inc(v.sem, v.step("cen"))
                dve.wait_ge(v.sem, v["cen"])
                nv.tensor_tensor(out=lsq, in0=lcen, in1=lcen, op=ALU.mult).then_inc(v.sem, v.step("sq"))
                dve.wait_ge(v.sem, v["sq"])
                nv.reduce_sum(lvar[:], tok(lsq), axis=AX.X).then_inc(v.sem, v.step("var"))
                dve.wait_ge(v.sem, v["var"])
                nv.tensor_scalar(var_eps[:], lvar[:], 1.0 / C, 1e-5, ALU.mult, ALU.add).then_inc(v.sem, v.step("eps"))
                dve.wait_ge(g0.sem, g0[pool_step])
                nv.tensor_tensor(out=tok(ln[:]), in0=tok(lcen), in1=rep(rstd[:], C), op=ALU.mult)\
                    .then_inc(v.sem, v.step("ln"))

            def stacked(v, a, t):
                dve.wait_ge(v.sem, v["ln"])
                nv.tensor_copy(partv[:, :, 0, :], tok(ln[:])).then_inc(v.sem, v.step("ph"))
                dve.wait_ge(v.sem, v["ph"])
                nv.tensor_tensor(out=tok(lsq), in0=tok(ln[:]), in1=partv[:, :, 0, :], op=ALU.subtract)\
                    .then_inc(v.sem, v.step("pr"))
                dve.wait_ge(a.sem, a["pm"])
                nv.tensor_tensor(out=partv[:, :, 2, :], in0=tok(lsq), in1=partv[:, :, 1, :], op=ALU.subtract)\
                    .then_inc(v.sem, v.step("pl"))
                dve.wait_ge(t.sem, t["st1"])
                nv.tensor_copy(stack1[:, BANK:], psb[1][:, 0:BANK]).then_inc(v.sem, v.step("s1b"))
                nv.tensor_copy(stack2[0:2 * C, BANK:], psb[1][0:2 * C, 0:BANK]).then_inc(v.sem, v.step("s2b"))

            def moments_of(src, v):
                nv.bn_stats(stats[:], src).then_inc(v.sem, v.step("stats"))
                dve.wait_ge(v.sem, v["stats"])
                nv.bn_aggr(moments[:], stats[:]).then_inc(v.sem, v.step("moments"))
                dve.wait_ge(v.sem, v["moments"])
                nv.tensor_scalar(var_eps[:, 0:1], moments[:, 1:2], 1e-5, None, ALU.add).then_inc(v.sem, v.step("eps"))

            dve.wait_ge(d_cst, 16)
            nv.tensor_copy(identb[:], ident).then_inc(v0.sem, v0.step("identb"))
            nv.memset(neg1[:], -1.0).then_inc(v0.sem, v0.step("neg1"))
            nv.memset(pos1[:], 1.0).then_inc(v0.sem, v0.step("pos1"))
            nv.tensor_tensor(out=base[:].rearrange("p (h n) -> p h n", h=NH),
                             in0=c["base"].rearrange("p (h n) -> p h n", h=NH),
                             in1=c["boff"][:, 0:2 * J].unsqueeze(1).broadcast_to([P, NH, 2 * J]), op=ALU.add)\
                .then_inc(v0.sem, v0.step("base"))
            dve.wait_ge(d_x, 16)
            moments_of(x[:], v0)
            dve.wait_ge(g0.sem, g0["rstd0"])
            nv.tensor_scalar(xg[:], x[:], moments[:, 0:1], rstd[:, 0:1], ALU.subtract, ALU.mult)\
                .then_inc(v0.sem, v0.step("xg"))

            dve.wait_ge(d_front, 16)
            dve.wait_ge(t0.sem, t0["comp"])
            cb = comp_bd.rearrange("p (s b n) -> p s b n", s=3, b=B)
            for i, (at, n, mask) in enumerate(((0, 2, f["bmask8"]), (2, 1, c["bmask"]))):
                nv.tensor_tensor(out=cb[:, at:at + n],
                                 in0=ps[:, 6, at * NOFF:(at + n) * NOFF].rearrange("p (s n) -> p s n", s=n)
                                 .unsqueeze(2).broadcast_to([P, n, B, NOFF]),
                                 in1=rep(mask, NOFF).unsqueeze(1).broadcast_to([P, n, B, NOFF]), op=ALU.mult)\
                    .then_inc(v0.sem, v0.step(f"comp{i}"))
            def tap_step(j, t, dst, name):
                win = qkvp[:, j, t // 3:t // 3 + H, t % 3:t % 3 + W]
                w = f["wdw"][:, j * K2 + t:j * K2 + t + 1]
                if t == 0:
                    nv.tensor_scalar(dst, win, w, f["bdw"][:, j:j + 1], ALU.mult, ALU.add)\
                        .then_inc(v0.sem, v0.step(name))
                else:
                    nv.scalar_tensor_tensor(out=dst, in0=win, scalar=w, in1=dst, op0=ALU.mult, op1=ALU.add)\
                        .then_inc(v0.sem, v0.step(name))

            q_in = img(q_mid)
            dve.wait_ge(g0.sem, g0["kvpad"])
            dve.wait_ge(a0.sem, a0["q"])
            for t in range(K2):
                if t:
                    dve.wait_ge(v0.sem, v0[f"q{t - 1}"])
                tap_step(0, t, q_in, f"q{t}")
            dve.wait_ge(t0.sem, t0["select"])
            for r in (2, 3):
                for s in range(2):
                    shifted_queries(nv.tensor_copy, r, s).then_inc(v0.sem, v0.step(f"s{r}{s}"))
            dve.wait_ge(a0.sem, a0["v"])
            for t in range(K2):
                for j, nm in ((1, "k"), (2, "v")):
                    if t:
                        dve.wait_ge(v0.sem, v0[f"{nm}{t - 1}"])
                    tap_step(j, t, img(kvv[:, j - 1, 0:N]), f"{nm}{t}")

            dve.wait_ge(t0.sem, t0["offsets"])
            off = ps[:, 2:2 + NH, 0:B * NOFF].rearrange("p h (b n) -> p h b n", b=B)
            hbn = lambda ap: ap.rearrange("p (b h n) -> p h b n", b=B, h=NH)
            nv.tensor_tensor(out=hbn(pos), in0=off[:, :, :, 0:2 * J],
                             in1=base[:].rearrange("p (h n) -> p h n", h=NH).unsqueeze(2).broadcast_to([P, NH, B, 2 * J]),
                             op=ALU.add).then_inc(v0.sem, v0.step("pos"))
            nv.tensor_tensor(out=hbn(gate_m[:]), in0=off[:, :, :, 2 * J:],
                             in1=c["boff"][:, 2 * J:].unsqueeze(1).unsqueeze(1).broadcast_to([P, NH, B, K2]), op=ALU.add)\
                .then_inc(v0.sem, v0.step("gate"))
            dve.wait_ge(v0.sem, v0["pos"])
            nv.tensor_scalar(pos, pos, -2.0, H + 1.0, ALU.max, ALU.min).then_inc(v0.sem, v0.step("clamp"))
            dve.wait_ge(v0.sem, v0["clamp"])
            nv.tensor_scalar(near, pos, -0.5, ROUND, ALU.add, ALU.add).then_inc(v0.sem, v0.step("near0"))
            dve.wait_ge(v0.sem, v0["near0"])
            nv.tensor_scalar(near, near, -ROUND, 0.0, ALU.add, ALU.max).then_inc(v0.sem, v0.step("near1"))
            dve.wait_ge(v0.sem, v0["near1"])
            nv.tensor_scalar(near, near, H - 2.0, None, ALU.min).then_inc(v0.sem, v0.step("near"))
            dve.wait_ge(v0.sem, v0["near"])
            yx = near.rearrange("p (n a) -> p n a", a=2)
            nv.scalar_tensor_tensor(out=index[:], in0=yx[:, :, 0], scalar=float(W), in1=yx[:, :, 1],
                                    op0=ALU.mult, op1=ALU.add).then_inc(v0.sem, v0.step("index"))
            rst = lambda i: rest[:, i * BANK:(i + 1) * BANK].rearrange("p (s k d) -> p s k d", s=B * G, k=4)
            tab = lambda i, part: tabv[:, i // 2, part, :, :, (i % 2) * HC:(i % 2 + 1) * HC]
            for i in range(4):
                dve.wait_ge(a0.sem, a0[f"high{i}"])
                nv.tensor_tensor(out=rst(i), in0=ps[:, TB[i], :].rearrange("p (k s d) -> p s k d", k=4, s=B * G),
                                 in1=tab(i, 0), op=ALU.subtract).then_inc(v0.sem, v0.step(f"rest{i}"))
            for i in range(4):
                dve.wait_ge(a0.sem, a0[f"mid{i}"])
                nv.tensor_tensor(out=tab(i, 2), in0=rst(i), in1=tab(i, 1), op=ALU.subtract)\
                    .then_inc(v0.sem, v0.step(f"low{i}"))
            def one_hots(u):
                for half in range(2):
                    js = slice(half * J // 2, (half + 1) * J // 2)
                    dve.wait_ge(s_bce, 9 * u + (5 if half == 0 else 9))
                    if u >= 2 and half == 0:
                        dve.wait_ge(s_un, u - 1)
                    for q in range(2):
                        ins = nv.tensor_scalar(ohv[:, u % 2, q, js, :], ixb[:, u % 2, js, :], c["pidx"][:, q:q + 1],
                                               None, ALU.is_equal)
                    ins.then_inc(s_oh, 1)

            def pair(b):
                r = b % 2
                w = slice(b * NH * J * 4, (b + 1) * NH * J * 4)
                gk = gv[:, r, :, :].rearrange("p (h s) (k d) -> p h (s k) d", h=NH * G, k=4)
                dve.wait_ge(s_ge, GRP * (b + 1))
                qv = q_tok[:, b * NH * C:(b + 1) * NH * C].rearrange("p (s d) -> p s d", d=HC)
                nv.tensor_tensor(out=prod.rearrange("p (s n d) -> p s n d", s=NH * G, n=4 * K2),
                                 in0=gk[:, :, :, 0:HC],
                                 in1=qv.unsqueeze(2).broadcast_to([P, NH * G, 4 * K2, HC]), op=ALU.mult)\
                    .then_inc(v1.sem, v1.step(f"prodk{b}"))
                dve.wait_ge(v1.sem, v1[f"prodk{b}"])
                nv.reduce_sum(dots[:], prod.rearrange("p (n d) -> p n d", d=HC), axis=AX.X)\
                    .then_inc(v1.sem, v1.step(f"dots{b}"))
                dve.wait_ge(v1.sem, v1[f"dots{b}"])
                nv.tensor_tensor(out=dots[:], in0=dots[:], in1=w4[:, w], op=ALU.mult).then_inc(v1.sem, v1.step(f"wdots{b}"))
                dve.wait_ge(v1.sem, v1[f"wdots{b}"])
                nv.reduce_sum(logit[:], dots[:].rearrange("p (n k) -> p n k", k=4), axis=AX.X)\
                    .then_inc(v1.sem, v1.step(f"logit{b}"))
                dve.wait_ge(v1.sem, v1[f"logit{b}"])
                lg = logit[:].rearrange("p (s k) -> p s k", k=K2)
                nv.reduce_max(peak[:], lg, axis=AX.X).then_inc(v1.sem, v1.step(f"peak{b}"))
                dve.wait_ge(v1.sem, v1[f"peak{b}"])
                nv.tensor_tensor(out=lg, in0=lg, in1=rep(peak[:], K2), op=ALU.subtract).then_inc(v1.sem, v1.step(f"sub{b}"))
                dve.wait_ge(s_px, b + 1)
                pv = pexp[:].rearrange("p (s k) -> p s k", k=K2)
                nv.reduce_sum(psum_[:], pv, axis=AX.X).then_inc(v1.sem, v1.step(f"expsum{b}"))
                dve.wait_ge(v1.sem, v1[f"expsum{b}"])
                nv.reciprocal(pinv[:], psum_[:]).then_inc(v1.sem, v1.step(f"inv{b}"))
                nv.tensor_tensor(out=w4p[:].rearrange("p (n k) -> p n k", k=4),
                                 in0=w4[:, w].rearrange("p (n k) -> p n k", k=4), in1=rep(pexp[:], 4), op=ALU.mult)\
                    .then_inc(v1.sem, v1.step(f"w4p{b}"))
                dve.wait_ge(v1.sem, v1[f"w4p{b}"])
                nv.tensor_tensor(out=prod.rearrange("p (s d n) -> p s d n", s=NH * G, d=HC),
                                 in0=gk[:, :, :, HC:KV].rearrange("p s n d -> p s d n"),
                                 in1=w4p[:].rearrange("p (s n) -> p s n", s=NH * G).unsqueeze(2)
                                 .broadcast_to([P, NH * G, HC, 4 * K2]), op=ALU.mult)\
                    .then_inc(v1.sem, v1.step(f"prodv{b}"))
                dve.wait_ge(v1.sem, v1[f"prodv{b}"])
                nv.reduce_sum(mixed[:], prod.rearrange("p (n k) -> p n k", k=4 * K2), axis=AX.X)\
                    .then_inc(v1.sem, v1.step(f"mixed{b}"))
                dve.wait_ge(v1.sem, v1[f"mixed{b}"])
                hgd = lambda ap: ap.rearrange("p (h g d) -> p h g d", h=NH, g=G)
                nv.tensor_tensor(out=tokhb(att[:])[:, :, b, :].rearrange("p h (g d) -> p h g d", g=G),
                                 in0=hgd(mixed[:]), in1=rep(pinv[:].rearrange("p (h g) -> p h g", h=NH), HC), op=ALU.mult)\
                    .then_inc(v1.sem, v1.step(f"att{b}"))

            for u in range(T):
                one_hots(u)
                if u == 0:
                    nv.tensor_tensor(out=away, in0=pos, in1=near, op=ALU.subtract).then_inc(v0.sem, v0.step("away"))
                    dve.wait_ge(v0.sem, v0["away"])
                    nv.scalar_tensor_tensor(out=hat0, in0=away, scalar=-1.0, in1=away, op0=ALU.mult, op1=ALU.min).then_inc(v0.sem, v0.step("hat0a"))
                    dve.wait_ge(v0.sem, v0["hat0a"])
                    nv.tensor_scalar(hats.rearrange("p (n z) -> p n z", z=2)[:, :, 0], hat0, 1.0, 0.0, ALU.add, ALU.max)\
                        .then_inc(v0.sem, v0.step("hat0"))
                    dve.wait_ge(a0.sem, a0["sigexp"])
                    nv.tensor_scalar(gate_m[:], gate_m[:], 1.0, None, ALU.add).then_inc(v0.sem, v0.step("gate1"))
                    dve.wait_ge(v0.sem, v0["gate1"])
                    nv.reciprocal(gate_m[:], gate_m[:]).then_inc(v0.sem, v0.step("sigmoid"))
                    dve.wait_ge(v0.sem, v0["sigmoid"])
                    nv.tensor_copy(mask_x[:].rearrange("p (t g k) -> p t g k", t=T, g=G),
                                   gate_m[:].rearrange("p (t k) -> p t k", t=T).unsqueeze(2).broadcast_to([P, T, G, K2]))\
                        .then_inc(v0.sem, v0.step("maskx"))
                    dve.wait_ge(v0.sem, v0["maskx"])
                    dve.wait_ge(a0.sem, a0["hat1"])
                    hv = hats.rearrange("p (n a z) -> p n a z", a=2, z=2)
                    nv.tensor_tensor(out=hv[:, :, 0, :], in0=hv[:, :, 0, :], in1=rep(mask_x[:], 2), op=ALU.mult)\
                        .then_inc(v0.sem, v0.step("hatm"))
                    dve.wait_ge(v0.sem, v0["hatm"])
                    nv.tensor_tensor(out=w4[:].rearrange("p (n y z) -> p n y z", y=2, z=2), in0=rep(hv[:, :, 0, :], 2),
                                     in1=hv[:, :, 1, :].unsqueeze(2).broadcast_to([P, T * J, 2, 2]), op=ALU.mult)\
                        .then_inc(v0.sem, v0.step("w4"))

                    nv.tensor_tensor(out=zsel[:], in0=c["logw"], in1=c["gumbel"], op=ALU.add).then_inc(vz.sem, vz.step("z"))
                    dve.wait_ge(vz.sem, vz["z"])
                    nv.reduce_max(zmax[:], zsel[:], axis=AX.X).then_inc(vz.sem, vz.step("zmax"))
                    dve.wait_ge(vz.sem, vz["zmax"])
                    nv.tensor_scalar(zmax[:], zmax[:], -1.0, None, ALU.mult).then_inc(vz.sem, vz.step("zneg"))

                if u == 1:
                    dve.wait_ge(az.sem, az["exp"])
                    nv.reciprocal(zsum[:], zsum[:]).then_inc(vz.sem, vz.step("zinv"))
                    dve.wait_ge(vz.sem, vz["zinv"])
                    nv.tensor_scalar(soft[:], soft[:], zsum[:], None, ALU.mult).then_inc(vz.sem, vz.step("soft"))
                    dve.wait_ge(vz.sem, vz["soft"])
                    sj = soft[:].unsqueeze(1).broadcast_to([P, NSC, NSC])
                    z44 = lambda ap: ap.rearrange("p (i j) -> p i j", i=NSC)
                    nv.tensor_tensor(out=z44(zgt[:]), in0=sj, in1=rep(soft[:], NSC), op=ALU.is_gt)\
                        .then_inc(vz.sem, vz.step("zgt"))
                    nv.tensor_tensor(out=z44(zeq[:]), in0=sj, in1=rep(soft[:], NSC), op=ALU.is_equal)\
                        .then_inc(vz.sem, vz.step("zeq"))
                    dve.wait_ge(vz.sem, vz["zeq"])
                    nv.tensor_tensor(out=zeq[:], in0=zeq[:], in1=c["lt4"], op=ALU.mult).then_inc(vz.sem, vz.step("zeqlt"))
                    dve.wait_ge(vz.sem, vz["zeqlt"])
                    nv.tensor_tensor(out=zgt[:], in0=zgt[:], in1=zeq[:], op=ALU.add).then_inc(vz.sem, vz.step("zadd"))
                    dve.wait_ge(vz.sem, vz["zadd"])
                    nv.reduce_sum(hard[:], z44(zgt[:]), axis=AX.X).then_inc(vz.sem, vz.step("rank"))
                    dve.wait_ge(vz.sem, vz["rank"])
                    nv.tensor_scalar(hard[:], hard[:], 0.0, None, ALU.is_equal).then_inc(vz.sem, vz.step("hard"))
                    dve.wait_ge(vz.sem, vz["hard"])
                    nv.tensor_tensor(out=wsel[:], in0=hard[:], in1=soft[:], op=ALU.subtract).then_inc(vz.sem, vz.step("diff"))
                    dve.wait_ge(vz.sem, vz["diff"])
                    nv.tensor_tensor(out=wsel[:], in0=wsel[:], in1=soft[:], op=ALU.add).then_inc(vz.sem, vz.step("w"))
                    nv.tensor_tensor(out=hard[:], in0=hard[:], in1=c["frac"], op=ALU.mult).then_inc(vz.sem, vz.step("lenp"))
                    dve.wait_ge(vz.sem, vz["lenp"])
                    nv.reduce_sum(length[:], hard[:], axis=AX.X).then_inc(vz.sem, vz.step("length"))
                    dve.wait_ge(vz.sem, vz["length"])
                    nv.tensor_scalar(window[:], c["tokidx"], length[:], None, ALU.is_lt).then_inc(vz.sem, vz.step("win"))
                    dve.wait_ge(vz.sem, vz["win"])
                    nv.tensor_scalar(winsgn[:], window[:], c["sgn"], None, ALU.mult).then_inc(vz.sem, vz.step("winsgn"))
                if u >= 3 and u % 2:
                    pair((u - 3) // 2)
            pair(B - 1)

            dve.wait_ge(t2.sem, t2["proj"])
            nv.scalar_tensor_tensor(out=x1[:], in0=ps[:, 1, 0:N], scalar=p1["bproj"], in1=x[:], op0=ALU.add, op1=ALU.add)\
                .then_inc(v2.sem, v2.step("x1"))
            dve.wait_ge(v2.sem, v2["x1"])
            moments_of(x1[:], v2)
            dve.wait_ge(g0.sem, g0["rstd1"])
            nv.tensor_scalar(xp[:, 1:1 + H, 1:1 + W], img(x1[:]), moments[:, 0:1], rstd[:, 0:1], ALU.subtract, ALU.mult)\
                .then_inc(v2.sem, v2.step("xpad"))
            dve.wait_ge(v2.sem, v2["xpad"])
            nv.tensor_reduce(pool[:], xp[:, 1:1 + H, 1:1 + W], AX.XY, ALU.add).then_inc(v2.sem, v2.step("pool"))
            dve.wait_ge(v2.sem, v2["pool"])
            nv.tensor_scalar(pool_bd[:], c["bmask"], pool[:], 1.0 / N, ALU.mult, ALU.mult).then_inc(v2.sem, v2.step("poolbd"))
            dve.wait_ge(t2.sem, t2["katt"])
            nv.reduce_max(kmax[:], ps[:, 3, 0:4], axis=AX.X).then_inc(v2.sem, v2.step("kmax"))
            dve.wait_ge(v2.sem, v2["kmax"])
            nv.tensor_scalar(kmax[:], kmax[:], -1.0 / 30.0, None, ALU.mult).then_inc(v2.sem, v2.step("kneg"))
            dve.wait_ge(a2.sem, a2["kexp"])
            nv.reciprocal(kinv[:], ksum_[:]).then_inc(v2.sem, v2.step("kinv"))
            dve.wait_ge(v2.sem, v2["kinv"])
            nv.tensor_scalar(katt[:], kexp[:], kinv[:], None, ALU.mult).then_inc(v2.sem, v2.step("katt"))
            for k in range(4):
                ck = p1["convk"][:, k * K2 * C:(k + 1) * K2 * C]
                if k == 0:
                    dve.wait_ge(v2.sem, v2["katt"])
                    nv.tensor_scalar(wmix, ck, katt[:, 0:1], None, ALU.mult).then_inc(v2.sem, v2.step("mix0"))
                else:
                    dve.wait_ge(v2.sem, v2[f"mix{k - 1}"])
                    nv.scalar_tensor_tensor(out=wmix, in0=ck, scalar=katt[:, k:k + 1], in1=wmix,
                                            op0=ALU.mult, op1=ALU.add).then_inc(v2.sem, v2.step(f"mix{k}"))
            dve.wait_ge(v2.sem, v2["mix3"])
            nv.tensor_tensor(out=wmix_bd.rearrange("p (t b o) -> p t b o", t=K2, b=B),
                             in0=wmix.rearrange("p (t o) -> p t o", t=K2).unsqueeze(2).broadcast_to([P, K2, B, C]),
                             in1=rep(c["bmask"].unsqueeze(1).broadcast_to([P, K2, B]), C), op=ALU.mult)\
                .then_inc(v2.sem, v2.step("mixbd"))
            nv.tensor_tensor(out=bmix[:], in0=katt[:], in1=p1["kbias"], op=ALU.mult).then_inc(v2.sem, v2.step("bmix"))
            dve.wait_ge(v2.sem, v2["bmix"])
            nv.reduce_sum(bsum[:], bmix[:], axis=AX.X).then_inc(v2.sem, v2.step("bsum"))
            dve.wait_ge(g0.sem, g0["bninv"])
            dve.wait_ge(v2.sem, v2["bsum"])
            nv.tensor_scalar(bn_inv[:], bn_inv[:], p1["bnscale"], None, ALU.mult).then_inc(v2.sem, v2.step("binv"))
            dve.wait_ge(v2.sem, v2["binv"])
            nv.tensor_scalar(bshift[:], bsum[:], p1["bnmean"], bn_inv[:], ALU.subtract, ALU.mult)\
                .then_inc(v2.sem, v2.step("bcent"))
            dve.wait_ge(v2.sem, v2["bcent"])
            nv.tensor_tensor(out=bshift[:], in0=bshift[:], in1=p1["bnbias"], op=ALU.add).then_inc(v2.sem, v2.step("bshift"))
            dve.wait_ge(a2.sem, a2["y1"])
            nv.tensor_tensor(out=x2, in0=x1[:], in1=y1, op=ALU.add).then_inc(v2.sem, v2.step("x2"))
            dve.wait_ge(t2.sem, t2["x2T"])
            nv.tensor_copy(x2t[:], ps[:, 5, 0:N]).then_inc(v2.sem, v2.step("x2t"))
            dve.wait_ge(v2.sem, v2["x2t"])

            layernorm(x2t[:], v3, "rstd2")
            dve.wait_ge(t3.sem, t3["kc"])
            nv.tensor_copy(kc, ps[:, 2, 0:N]).then_inc(v3.sem, v3.step("kc"))
            sc = score.rearrange("p (b k) -> p b k", b=B)
            dve.wait_ge(d_l2, 16)
            dve.wait_ge(t3.sem, t3["score"])
            nv.scalar_tensor_tensor(out=sc, in0=ps[:, 4:8, 0:3 * P], scalar=float(N) ** -0.5,
                                    in1=p2["causal"].unsqueeze(1).broadcast_to([P, B, 3 * P]),
                                    op0=ALU.mult, op1=ALU.add).then_inc(v3.sem, v3.step("score"))
            dve.wait_ge(v3.sem, v3["score"])
            sx = smax[:].rearrange("p (h b) -> p h b", h=NH)
            nv.reduce_max(sx[:, 0, :], sc[:, :, 0:P], axis=AX.X).then_inc(v3.sem, v3.step("smax0"))
            nv.reduce_max(sx[:, 1, :], sc[:, :, P:3 * P], axis=AX.X).then_inc(v3.sem, v3.step("smax1"))
            dve.wait_ge(v3.sem, v3["smax1"])
            nv.tensor_scalar(smax[:], smax[:], -1.0, None, ALU.mult).then_inc(v3.sem, v3.step("sneg"))
            dve.wait_ge(a3.sem, a3[f"exp{T - 1}"])
            nv.reciprocal(sinv[:], ssum[:]).then_inc(v3.sem, v3.step("sinv"))
            for b in (1, 3):
                dve.wait_ge(t3.sem, t3[f"pt{b}"])
                nv.tensor_copy(prob_t[:, b * 3 * P:(b + 1) * 3 * P], ps[:, b, 0:3 * P])\
                    .then_inc(v3.sem, v3.step(f"pt{b}"))
            dve.wait_ge(t3.sem, t3["pv"])
            nv.tensor_tensor(out=tok(ctx_n), in0=tok(ps[:, 4, 0:N]), in1=rep(sinv[:], C), op=ALU.mult)\
                .then_inc(v3.sem, v3.step("ctx"))
            dve.wait_ge(v3.sem, v3["ctx"])
            nv.tensor_tensor(out=x3t, in0=x2t[:], in1=ctx_n, op=ALU.add).then_inc(v3.sem, v3.step("x3"))
            dve.wait_ge(v3.sem, v3["x3"])

            layernorm(x3t, v4, "rstd3")
            stacked(v4, a4, t4)
            dve.wait_ge(t4.sem, t4["experts"])
            te = lambda ap: ap.rearrange("p (t e) -> p t e", e=E)
            tee = lambda ap: ap.rearrange("p (t i j) -> p t i j", i=E, j=E)
            nv.tensor_copy(te(rlog[:]), ps[:, :, E * C:E * C + E]).then_inc(v4.sem, v4.step("rlog"))
            dve.wait_ge(v4.sem, v4["rlog"])
            lj = te(rlog[:]).unsqueeze(2).broadcast_to([P, T, E, E])
            li = rep(te(rlog[:]), E)
            nv.tensor_tensor(out=tee(rgt), in0=lj, in1=li, op=ALU.is_gt).then_inc(v4.sem, v4.step("rgt"))
            nv.tensor_tensor(out=tee(req), in0=lj, in1=li, op=ALU.is_equal).then_inc(v4.sem, v4.step("req"))
            dve.wait_ge(v4.sem, v4["req"])
            nv.tensor_tensor(out=req.rearrange("p (t n) -> p t n", t=T), in0=req.rearrange("p (t n) -> p t n", t=T),
                             in1=c["lt8"].unsqueeze(1).broadcast_to([P, T, E * E]), op=ALU.mult)\
                .then_inc(v4.sem, v4.step("reqlt"))
            dve.wait_ge(v4.sem, v4["reqlt"])
            nv.tensor_tensor(out=rgt, in0=rgt, in1=req, op=ALU.add).then_inc(v4.sem, v4.step("rsum"))
            dve.wait_ge(v4.sem, v4["rsum"])
            nv.reduce_sum(rank[:], rgt.rearrange("p (n j) -> p n j", j=E), axis=AX.X).then_inc(v4.sem, v4.step("rank"))
            nv.reduce_max(rmax[:], te(rlog[:]), axis=AX.X).then_inc(v4.sem, v4.step("rmax"))
            dve.wait_ge(v4.sem, v4["rmax"])
            nv.tensor_tensor(out=te(rexp[:]), in0=te(rlog[:]), in1=rep(rmax[:], E), op=ALU.subtract)\
                .then_inc(v4.sem, v4.step("rsub"))
            nv.tensor_scalar(chosen[:], rank[:], 2.0, None, ALU.is_lt).then_inc(v4.sem, v4.step("chosen"))
            dve.wait_ge(v4.sem, v4["chosen"])
            dve.wait_ge(a4.sem, a4["rexp"])
            nv.tensor_tensor(out=chosen[:], in0=chosen[:], in1=rexp[:], op=ALU.mult).then_inc(v4.sem, v4.step("esel"))
            dve.wait_ge(v4.sem, v4["esel"])
            nv.reduce_sum(rsum[:], te(chosen[:]), axis=AX.X).then_inc(v4.sem, v4.step("esum"))
            dve.wait_ge(v4.sem, v4["esum"])
            nv.reciprocal(rsum[:], rsum[:]).then_inc(v4.sem, v4.step("einv"))
            dve.wait_ge(v4.sem, v4["einv"])
            tce = lambda ap: ap.rearrange("p (t c e) -> p t c e", t=T, e=E)
            nv.tensor_tensor(out=tce(gated),
                             in0=ps[:, :, 0:E * C].rearrange("p t (e c) -> p t c e", e=E),
                             in1=te(chosen[:]).unsqueeze(2).broadcast_to([P, T, C, E]), op=ALU.mult)\
                .then_inc(v4.sem, v4.step("gated"))
            dve.wait_ge(v4.sem, v4["gated"])
            nv.reduce_sum(lsq, gated.rearrange("p (n e) -> p n e", e=E), axis=AX.X).then_inc(v4.sem, v4.step("y"))
            dve.wait_ge(v4.sem, v4["y"])
            nv.tensor_tensor(out=tok(lsq), in0=tok(lsq), in1=rep(rsum[:], C), op=ALU.mult)\
                .then_inc(v4.sem, v4.step("ynorm"))
            dve.wait_ge(v4.sem, v4["ynorm"])
            nv.tensor_tensor(out=x4t, in0=x3t, in1=lsq, op=ALU.add).then_inc(v4.sem, v4.step("x4"))
            dve.wait_ge(v4.sem, v4["x4"])

            layernorm(x4t, v5, "rstd4")
            for h in range(NH):
                nv.tensor_copy(vcs.rearrange("p (h n k) -> p h n k", h=NH, k=HCOLS)[:, h, :, 2 * P:],
                               c["cs"][:, 2 * h:2 * h + 2].unsqueeze(1).broadcast_to([P, B * HG, 2]))\
                    .then_inc(v5.sem, v5.step(f"cs{h}"))
            stacked(v5, a5, t5)
            for t in range(T):
                h = t // B
                blk = slice(t * BANK, (t + 1) * BANK)
                dve.wait_ge(a5.sem, a5[f"ek{t}"])
                nv.scalar_tensor_tensor(out=fk[:, blk], in0=fk[:, blk], scalar=1.0, in1=ps[:, 2 * t % 8, :],
                                        op0=ALU.min, op1=ALU.max).then_inc(v5.sem, v5.step(f"fk{t}"))
                dve.wait_ge(a5.sem, a5[f"vc{t}"])
                nv.tensor_scalar(vcv[:, t, :, P:2 * P], ps[:, (2 * t + 1) % 8, :].rearrange("p (g n) -> p g n", g=HG),
                                 c["cs"][:, 2 * h + 1:2 * h + 2], None, ALU.mult).then_inc(v5.sem, v5.step(f"vs{t}"))
            for i in range(8):
                blk = slice(i * BANK, (i + 1) * BANK)
                dve.wait_ge(a5.sem, a5[f"eq{i}"])
                nv.scalar_tensor_tensor(out=fq[:, blk], in0=fq[:, blk], scalar=1.0, in1=ps[:, i % 4, :],
                                        op0=ALU.min, op1=ALU.max).then_inc(v5.sem, v5.step(f"fq{i}"))
                if i in (3, 7):
                    dve.wait_ge(t5.sem, t5[f"kv{i // 2}"])
                    heads_products(nv.tensor_copy, i // 2).then_inc(v5.sem, v5.step(f"kv{i // 2}"))
            nv.tensor_tensor(out=tok(x4d), in0=tok(x4t), in1=p3["denseb"].unsqueeze(1).broadcast_to([P, T, D]),
                             op=ALU.add).then_inc(v5.sem, v5.step("bias"))
            dve.wait_ge(v5.sem, v5["kv3"])
            dve.wait_ge(a5.sem, a5["kv2"])
            nv.tensor_tensor(out=ks_bd.rearrange("p (g n h) -> p g n h", g=HG, h=NHEAD),
                             in0=rep(ks_sb[:].rearrange("p (g n) -> p g n", g=HG), NHEAD),
                             in1=c["headsel"].rearrange("p (g h) -> p g h", g=HG).unsqueeze(2)
                             .broadcast_to([P, HG, 2 * B, NHEAD]), op=ALU.mult).then_inc(v5.sem, v5.step("ksb"))
            dve.wait_ge(t5.sem, t5["den1"])
            nv.tensor_copy(den_ch[:, BANK:], ps[0:32, 1, :]).then_inc(v5.sem, v5.step("dc1"))
            dve.wait_ge(t5.sem, t5["denT"])
            dt = ps[:, 2, 0:T * 32].rearrange("p (h b s n) -> p h b s n", h=NH, b=B, s=2)
            dn = den.rearrange("p (h b n) -> p h b n", h=NH, b=B)
            for h in range(NH):
                nv.tensor_scalar(dn[:, h], dt[:, h, :, 0, :], c["cs"][:, 2 * h:2 * h + 1], None, ALU.mult)\
                    .then_inc(v5.sem, v5.step(f"cos{h}"))
            for h in range(NH):
                dve.wait_ge(v5.sem, v5[f"cos{h}"])
                nv.scalar_tensor_tensor(out=dn[:, h], in0=dt[:, h, :, 1, :], scalar=c["cs"][:, 2 * h + 1:2 * h + 2],
                                        in1=dn[:, h], op0=ALU.mult, op1=ALU.add).then_inc(v5.sem, v5.step(f"den{h}"))
            dve.wait_ge(v5.sem, v5["den1"])
            nv.tensor_scalar(den, den, 1e-5, None, ALU.add).then_inc(v5.sem, v5.step("deneps"))
            dve.wait_ge(v5.sem, v5["deneps"])
            nv.reciprocal(den, den).then_inc(v5.sem, v5.step("inv"))
            dve.wait_ge(v5.sem, v5["inv"])
            dv = den.rearrange("p (t n) -> p t n", t=T)
            dp = den_p.rearrange("p (t r n) -> p t r n", t=T, r=3)
            for part, name, less in ((0, "dh", "dr"), (1, "dm", "ds")):
                nv.tensor_copy(dp[:, :, part, :], dv).then_inc(v5.sem, v5.step(name))
                dve.wait_ge(v5.sem, v5[name])
                nv.tensor_tensor(out=dv, in0=dv, in1=dp[:, :, part, :], op=ALU.subtract).then_inc(v5.sem, v5.step(less))
                dve.wait_ge(v5.sem, v5[less])
            nv.tensor_copy(dp[:, :, 2, :], dv).then_inc(v5.sem, v5.step("dl"))
            dve.wait_ge(t5.sem, t5["dp1"])
            nv.tensor_copy(den_parts[0:NPART, BANK:], psb[1][0:NPART, 0:BANK]).then_inc(v5.sem, v5.step("dp1"))
            for i in range(8):
                if i % HG < 3:
                    dve.wait_ge(t5.sem, t5[f"ex{i}"])
                    over_denominator(nv, i, ps[:, 3 + i % 4, :]).then_inc(v5.sem, v5.step(f"qn{i}"))
            halves = [slice(i * BANK, (i + 1) * BANK) for i in range(2)]
            dve.wait_ge(d_late, 32)
            for i, hs in enumerate(halves):
                dve.wait_ge(t5.sem, t5[f"out{i}"])
                nv.tensor_tensor(out=oc[:, hs].rearrange("p (b n) -> p b n", b=2),
                                 in0=ps[0:2 * D, 1 + i, :].rearrange("p (b n) -> p b n", b=2),
                                 in1=turns["cs_out"][0:2 * D, :].unsqueeze(1).broadcast_to([2 * D, 2, N]), op=ALU.mult)\
                    .then_inc(v5.sem, v5.step(f"oc{i}"))
            dve.wait_ge(t5.sem, t5["fold"])
            nv.tensor_tensor(out=x5t, in0=x4d, in1=ps[:, 0, 0:N], op=ALU.add).then_inc(v5.sem, v5.step("x5"))
            dve.wait_ge(v5.sem, v5["x5"])

            layernorm(x5t, v6, "rstd5")
            stacked(v6, a6, t6)
            for t in range(T):
                b, h = t % B, t // B
                dve.wait_ge(t6.sem, t6[f"v{t}"])
                nv.tensor_scalar(vv.rearrange("p (k h b m e) -> p k h b m e", k=NF, h=NH, b=B, m=2)[:, :, h, b, 1, :],
                                 ps[:, 2 * (t % 3) + 1, :].rearrange("p (k e) -> p k e", k=NF), c["sgn"], None, ALU.mult)\
                    .then_inc(v6.sem, v6.step(f"vm{t}"))
            nv.tensor_copy(arv[:, :, B:, :], ps[:, 7, 0:B * KU * D].rearrange("p (b i e) -> p i b e", b=B, i=KU))\
                .then_inc(v6.sem, v6.step("ar1"))
            dve.wait_ge(t6.sem, t6["out"])
            so = ps[:, 4, :].rearrange("p (h b m e) -> p h b m e", h=NH, b=B, m=2)
            sv, yv = tokhb(stu_m), tokhb(x6t)
            for h in range(NH):
                nv.tensor_scalar(sv[:, h, :, :], so[:, h, :, 1, :], winsgn[:, h:h + 1], None, ALU.mult)\
                    .then_inc(v6.sem, v6.step(f"m{h}"))
            dve.wait_ge(v6.sem, v6["m1"])
            for h in range(NH):
                nv.scalar_tensor_tensor(out=yv[:, h, :, :], in0=so[:, h, :, 0, :], scalar=window[:, h:h + 1],
                                        in1=sv[:, h, :, :], op0=ALU.mult, op1=ALU.add)\
                    .then_inc(v6.sem, v6.step(f"y{h}"))
            dve.wait_ge(v6.sem, v6["y1"])
            nv.tensor_tensor(out=x6t, in0=x6t, in1=x5t, op=ALU.add).then_inc(v6.sem, v6.step("x6"))

        @block.tensor
        def _(pe):
            def mm(out_ap, lhsT, rhs, start=True, stop=True):
                return nc.tensor.matmul(out_ap, lhsT, rhs, start=start, stop=stop)

            pe.wait_ge(d_pw, 16)
            for i in range(3):
                ins = mm(ps[:, 6, i * NOFF:(i + 1) * NOFF], pw[:, i * P:(i + 1) * P], pw[:, 3 * P:])
            ins.then_inc(t0.sem, t0.step("comp"))
            pe.wait_ge(d_front, 16)
            pe.wait_ge(v0.sem, v0["xg"])
            for j, (name, dst) in enumerate((("q", ps[:, 0, 0:N]), ("k", ps[:, 0, N:2 * N]), ("v", ps[:, 1, 0:N]))):
                mm(dst, f["wqkv"][:, j * P:(j + 1) * P], xg[:]).then_inc(t0.sem, t0.step(name))
            pe.wait_ge(v0.sem, v0["q8"])
            mm(ps[:, 7, 0:N + 2 * (W + 1)], f["select"], q_flat[:]).then_inc(t0.sem, t0.step("select"))
            pe.wait_ge(a0.sem, a0["s11"])
            pe.wait_ge(v0.sem, v0["s31"])
            for h in range(NH):
                hs = slice(h * P, (h + 1) * P)
                for i, q in enumerate((q_stack[:, 0:N][:, hs], q_stack[:, N:][:, hs], q_mid[:, hs])):
                    ins = mm(ps[:, 2 + h, 0:B * NOFF], q, comp_bd[:, i * B * NOFF:(i + 1) * B * NOFF],
                             start=i == 0, stop=i == 2)
            ins.then_inc(t0.sem, t0.step("offsets"))
            for h in range(NH):
                ins = nc.tensor.transpose(ps[:, 1, N + h * P:N + (h + 1) * P], q_mid[:, h * P:(h + 1) * P], ident)
            ins.then_inc(t0.sem, t0.step("qtok"))
            pe.wait_ge(v0.sem, v0["v8"])
            for i in range(4):
                for k in range(4):
                    at = (i // 2) * P + (k // 2) * W + k % 2
                    ins = nc.tensor.transpose(ps[:, TB[i], k * P:(k + 1) * P], kvv[:, i % 2, at:at + P], ident)
                ins.then_inc(t0.sem, t0.step(f"table{i}"))

            def index_group(u, i):
                n = u * 9 + i
                if n >= 2:
                    pe.wait_ge(s_bce, n - 1)
                for q in range(4):
                    ins = mm(ps[:, n % 2, q * P:(q + 1) * P],
                             index[:, u * J + 4 * i + q:u * J + 4 * i + q + 1].broadcast_to([P, P]), identb[:])
                ins.then_inc(s_bc, 1)

            pe.wait_ge(v0.sem, v0["index"])
            pe.wait_ge(a0.sem, a0["qtok"])
            for i in range(9):
                index_group(0, i)
            pe.wait_ge(v0.sem, v0["low3"])
            for u in range(T):
                b = u // NH
                for i in range(9):
                    if u + 1 < T:
                        index_group(u + 1, i)
                    for j in range(4 * i, 4 * i + 4):
                        n, slot = (u * J + j) // 8, (u * J + j) % 8
                        if j in (0, J // 2):
                            pe.wait_ge(s_oh, 2 * u + 1 + (j > 0))
                        if slot == 0 and n >= 4:
                            pe.wait_ge(s_ge, n - 3)
                        for q in range(2):
                            for part in range(3):
                                ins = mm(ps[:, 2 + n % 4, slot * SLOT:(slot + 1) * SLOT], ohv[:, u % 2, q, j, :],
                                         tabv[:, q, part, b * G + j // K2, :, :].rearrange("p k d -> p (k d)"),
                                         start=(q, part) == (0, 0), stop=(q, part) == (1, 2))
                        if slot == 7:
                            ins.then_inc(s_gp, 1)
                        if j == J - 1:
                            if slot == 7:
                                pe.wait_ge(s_gp, n + 1)
                                pe.sem_inc(s_un, 1)
                            else:
                                ins.then_inc(s_un, 1)

            pe.wait_ge(d_l3, 32)
            for h in range(NHEAD):
                hg, rows = h // 4, slice(h % 4 * D, (h % 4 + 1) * D)
                dense = p3["dense"][rows, hg * D:(hg + 1) * D]
                bank = WB[h % 4]
                mm(ps[:, bank, hg * D:(hg + 1) * D], p3["wv"][rows, hg * P:(hg + 1) * P], dense)
                ins = mm(ps[0:3, bank, (HG + hg) * D:(HG + hg + 1) * D], p3["bv"][rows, 3 * hg:3 * hg + 3], dense)
            ins.then_inc(tw.sem, tw.step("wd"))

            pe.wait_ge(v1.sem, v1[f"att{B - 1}"])
            pe.wait_ge(aw.sem, aw["wdb3"])
            for h in range(NH):
                ins = nc.tensor.transpose(ps[:, 0, h * P:(h + 1) * P], att[:, h * P:(h + 1) * P], ident)
            ins.then_inc(t2.sem, t2.step("attT"))
            pe.wait_ge(d_l1, 32)
            pe.wait_ge(a2.sem, a2["attT"])
            mm(ps[:, 1, 0:N], p1["wproj"], att_ch).then_inc(t2.sem, t2.step("proj"))
            pe.wait_ge(v2.sem, v2["poolbd"])
            mm(ps[0:4, 2, 0:B], p1["red"], pool_bd[:]).then_inc(t2.sem, t2.step("poolred"))
            pe.wait_ge(a2.sem, a2["poolred"])
            mm(ps[:, 3, 0:4], pool_red[:], attk[:]).then_inc(t2.sem, t2.step("katt"))
            pe.wait_ge(v2.sem, v2["mixbd"])
            for t in range(K2):
                ins = mm(ps[:, 4, 0:N], wmix_bd[:, t * P:(t + 1) * P], xp[:, t // 3:t // 3 + H, t % 3:t % 3 + W],
                         start=t == 0, stop=t == K2 - 1)
            ins.then_inc(t2.sem, t2.step("conv"))
            pe.wait_ge(v2.sem, v2["x2"])
            for h in range(NH):
                ins = nc.tensor.transpose(ps[:, 5, h * P:(h + 1) * P], x2[:, h * P:(h + 1) * P], ident)
            ins.then_inc(t2.sem, t2.step("x2T"))

            pe.wait_ge(v3.sem, v3["ln"])
            for h in range(NH):
                ins = nc.tensor.transpose(ps[:, 0, h * P:(h + 1) * P], ln[:, h * P:(h + 1) * P], ident)
            ins.then_inc(t3.sem, t3.step("lnT"))
            pe.wait_ge(d_l2, 16)
            pe.wait_ge(a3.sem, a3["lnT"])
            mm(ps[:, 1, 0:N], p2["wq"], ln_ch).then_inc(t3.sem, t3.step("qc"))
            mm(ps[:, 2, 0:N], p2["wk"], ln_ch).then_inc(t3.sem, t3.step("kc"))
            for h in range(NH):
                ins = mm(ps[:, 3, h * P:(h + 1) * P], ln_ch[:, h * P:(h + 1) * P], p2["wv"])
            ins.then_inc(t3.sem, t3.step("vt"))
            pe.wait_ge(a3.sem, a3["qc"])
            pe.wait_ge(v3.sem, v3["kc"])
            for b in range(B):
                rows = slice(b * C, (b + 1) * C)
                mm(ps[:, 4 + b, 0:P], qc[rows, 0:P], kc[rows, 0:P])
                ins = mm(ps[:, 4 + b, P:3 * P], qc[rows, P:2 * P], kc[rows, :])
            ins.then_inc(t3.sem, t3.step("score"))
            pe.wait_ge(a3.sem, a3["vt"])
            for b in range(B):
                pe.wait_ge(a3.sem, a3[f"exp{B + b}"])
                for r in range(3):
                    ins = nc.tensor.transpose(ps[:, b, r * P:(r + 1) * P], prob[:, (b * 3 + r) * P:(b * 3 + r + 1) * P],
                                              ident)
                ins.then_inc(t3.sem, t3.step(f"pt{b}"))
            pe.wait_ge(a3.sem, a3["pt2"])
            pe.wait_ge(v3.sem, v3["pt3"])
            for b in range(B):
                def blk(r):
                    return prob_t[:, (b * 3 + r) * P:(b * 3 + r + 1) * P]

                def vals(h):
                    return vt[:, h * P + b * C:h * P + (b + 1) * C]
                first, second = (ps[:, 4, (h * B + b) * C:(h * B + b + 1) * C] for h in range(NH))
                mm(first, blk(0), vals(0))
                mm(second, blk(1), vals(0), stop=False)
                ins = mm(second, blk(2), vals(1), start=False)
            ins.then_inc(t3.sem, t3.step("pv"))

            def stacked(v, a, t):
                pe.wait_ge(v.sem, v["pl"])
                pe.wait_ge(a.sem, a["pd"])
                for i in range(T):
                    ins = nc.tensor.transpose(psb[i // 4][:, i % 4 * P:(i % 4 + 1) * P], parts[:, i * P:(i + 1) * P], identb[:])
                    if i % 4 == 3:
                        ins.then_inc(t.sem, t.step(f"st{i // 4}"))
                pe.wait_ge(a.sem, a["s2a"])
                pe.wait_ge(v.sem, v["s2b"])

            def two_passes(out_ap, first, second, tokens_first=True):
                (l0, r0), (l1_, r1) = first, second
                nc.tensor.matmul(out_ap, l0, r0, start=True, stop=False)
                return nc.tensor.matmul(out_ap, l1_, r1, start=False, stop=True)

            BK = 2 * C + 3

            stacked(v4, a4, t4)
            pe.wait_ge(g0.sem, g0["ones"])
            pe.wait_ge(aw.sem, aw["mw2h"])
            pe.wait_ge(gw.sem, gw["mlow"])
            for t in range(T):
                ts = slice(t * P, (t + 1) * P)
                ins = two_passes(ps[:, t, 0:E * C + E], (stack1[:, ts], moe_w1[:]), (stack2[0:BK, ts], moe_w2[0:BK, :]))
            ins.then_inc(t4.sem, t4.step("experts"))

            stacked(v5, a5, t5)
            pe.wait_ge(aw.sem, aw["lw2h"])
            pe.wait_ge(gw.sem, gw["llow"])
            for t in range(T):
                ts = slice(t * P, (t + 1) * P)
                if t >= 4:
                    pe.wait_ge(v5.sem, v5[f"vs{t - 4}"])
                for j, name, bank in ((1, "k", 2 * t % 8), (2, "v", (2 * t + 1) % 8)):
                    w = slice(j * DH, (j + 1) * DH)
                    two_passes(ps[:, bank, :], (stack1[:, ts], w1[:, w]), (stack2[0:BK, ts], w2[0:BK, w]))\
                        .then_inc(t5.sem, t5.step(f"{name}{t}"))
            for hg in range(HG):
                w = slice(hg * P, (hg + 1) * P)
                for half in range(2):
                    i, ts = 2 * hg + half, slice(half * BANK, (half + 1) * BANK)
                    if i >= 4:
                        pe.wait_ge(v5.sem, v5[f"fq{i - 4}"])
                    elif half == 0:
                        pe.wait_ge(v5.sem, v5[f"vs{4 + hg}"])
                    two_passes(ps[:, i % 4, :], (w1[:, w], stack1[:, ts]), (w2[0:BK, w], stack2[0:BK, ts]))\
                        .then_inc(t5.sem, t5.step(f"q{i}"))
                if hg == 0:
                    pe.wait_ge(v5.sem, v5[f"vs{T - 1}"])
                elif hg % 2:
                    pe.wait_ge(a5.sem, a5[f"kv{hg - 1}"])
                else:
                    pe.wait_ge(v5.sem, v5[f"kv{hg - 1}"])
                for b in range(B):
                    for h in range(NH):
                        t = h * B + b
                        ins = mm(ps[:, 4 + b, 0:HCOLS], fk[:, t * BANK + hg * P:t * BANK + (hg + 1) * P], vcv[:, t, hg, :],
                                 start=h == 0, stop=h == NH - 1)
                ins.then_inc(t5.sem, t5.step(f"kv{hg}"))
            pe.wait_ge(v5.sem, v5["ksb"])
            for b in range(B):
                for hg in range(HG):
                    ins = mm(ps[0:32, b // 2, b % 2 * N:(b % 2 + 1) * N], ks_bd[:, (hg * B + b) * 32:(hg * B + b + 1) * 32],
                             fqv[:, hg, :, b, :], start=hg == 0, stop=hg == HG - 1)
                if b % 2:
                    ins.then_inc(t5.sem, t5.step(f"den{b // 2}"))
            pe.wait_ge(a5.sem, a5["dc0"])
            pe.wait_ge(v5.sem, v5["dc1"])
            for b in range(B):
                for h in range(NH):
                    at, t = (b * NH + h) * P, h * B + b
                    ins = nc.tensor.transpose(ps[:, 2, t * 32:(t + 1) * 32], den_ch[:, at:at + P], ident[0:32, 0:32])
            ins.then_inc(t5.sem, t5.step("denT"))
            pe.wait_ge(v5.sem, v5["dl"])
            for i in range(T):
                t = i % NH * B + i // NH
                ins = nc.tensor.transpose(psb[i // 4][0:NPART, i % 4 * P:(i % 4 + 1) * P],
                                          den_p[:, t * NPART:(t + 1) * NPART], identb[:])
                if i % 4 == 3:
                    ins.then_inc(t5.sem, t5.step(f"dp{i // 4}"))
            pe.wait_ge(a5.sem, a5["expand"])
            for i in range(8):
                half, hg = i // HG, i % HG
                if hg == 0:
                    pe.wait_ge(*((a5.sem, a5["dp0"]) if half == 0 else (v5.sem, v5["dp1"])))
                if i == 7:
                    pe.wait_ge(a5.sem, a5["rt3"])
                elif i >= 4:
                    pe.wait_ge(v5.sem, v5[f"qn{i - 4}"])
                mm(ps[:, 3 + i % 4, :], expandb[0:NPART, hg * P:(hg + 1) * P],
                   den_parts[0:NPART, half * BANK:(half + 1) * BANK]).then_inc(t5.sem, t5.step(f"ex{i}"))
            for b in range(B):
                if b % 2 == 0:
                    pe.wait_ge(v5.sem, v5[f"qn{2 * b + 2}"])
                    pe.wait_ge(g0.sem, g0[f"qn{2 * b + 3}"])
                for hg in range(HG):
                    i = hg * B + b
                    ins = mm(ps[0:2 * D, 1 + b // 2, b % 2 * N:(b % 2 + 1) * N], mcs[:, i * 2 * D:(i + 1) * 2 * D],
                             fqv[:, hg, :, b, :], start=hg == 0, stop=hg == HG - 1)
                if b % 2:
                    ins.then_inc(t5.sem, t5.step(f"out{b // 2}"))
            for b in range(B):
                if b % 2 == 0:
                    pe.wait_ge(v5.sem, v5[f"oc{b // 2}"])
                for h in range(NH):
                    ins = mm(ps[:, 0, (h * B + b) * D:(h * B + b + 1) * D], oc[:, (b * NH + h) * P:(b * NH + h + 1) * P],
                             c["fold"][0:2 * D, :])
            ins.then_inc(t5.sem, t5.step("fold"))

            stacked(v6, a6, t6)
            pe.wait_ge(gw.sem, gw["slow"])
            for t in range(T):
                ts, two = slice(t * P, (t + 1) * P), 2 * C
                if t >= 3:
                    pe.wait_ge(a6.sem, a6[f"vp{t - 3}"])
                    pe.wait_ge(v6.sem, v6[f"vm{t - 3}"])
                for out_ap, w in ((ps[:, 6 + t // B, t % B * KU * D:(t % B + 1) * KU * D], slice(2 * NF * D, STU)),
                                  (ps[:, 2 * (t % 3), :], slice(0, NF * D)), (ps[:, 2 * (t % 3) + 1, :], slice(NF * D, 2 * NF * D))):
                    ins = two_passes(out_ap, (stack1[:, ts], stu_w1[:, w]), (stack2[0:two, ts], stu_w2[0:two, w]))
                ins.then_inc(t6.sem, t6.step(f"v{t}"))
            pe.wait_ge(d_toep, 16)
            pe.wait_ge(a6.sem, a6["ar0"])
            pe.wait_ge(v6.sem, v6["ar1"])
            for k in range(NF):
                mm(ps[:, 4, :], toep[:, k * N:k * N + P], vv[:, k * BANK:(k + 1) * BANK], start=k == 0, stop=False)
                mm(ps[:, 4, BANK // 2:], toep[:, k * N + P:(k + 1) * N], vv[:, k * BANK:k * BANK + BANK // 2],
                   start=False, stop=False)
            plus = ps[:, 4, :].rearrange("p (t m e) -> p t m e", t=T, m=2)[:, :, 0, :]
            mm(plus, ident, arv[:, 0], start=False, stop=False)
            for i in range(1, KU):
                k = NF + i - 1
                mm(plus, toep[:, k * N:k * N + P], arv[:, i], start=False, stop=False)
                ins = mm(plus[:, B:], toep[:, k * N + P:(k + 1) * N], arv[:, i, 0:B, :], start=False, stop=i == KU - 1)
            ins.then_inc(t6.sem, t6.step("out"))


def kernel(**inputs):
    import numpy as np
    import concourse.bacc as bacc
    from concourse.bass_utils import run_bass_kernel_spmd

    a = {k: np.asarray(v) for k, v in inputs.items()}
    f32 = np.float32

    def pack(block, parts):
        return np.concatenate([np.asarray(parts[n], f32).reshape(-1, w) for n, w in block], axis=1)

    def rows(v, n=P):
        return np.broadcast_to(np.asarray(v, f32).reshape(1, -1), (n, np.size(v)))

    def images(v):
        v = np.asarray(v).reshape(C, -1)
        return np.concatenate([v] * B, axis=0)

    def diagonal(w):
        out = np.zeros((P, P), w.dtype)
        for b in range(B):
            out[b * C:(b + 1) * C, b * C:(b + 1) * C] = w
        return out

    p = np.arange(P)
    eye = np.eye(P, dtype=f32)
    grid = np.zeros((P, NH, G, K2, 2), f32)
    for g in range(G):
        dil = 2 * g + 1
        for t in range(K2):
            for h in range(NH):
                n = h * P + p
                grid[:, h, g, t, 0] = n // W + (t // 3 - 1) * dil
                grid[:, h, g, t, 1] = n % W + (t % 3 - 1) * dil
    turn = (1.57 * np.arange(N, dtype=f32) / N).astype(f32).reshape(NH, P).T
    cst = pack(CST, {
        "ident": eye, "bmask": (p[:, None] // C == np.arange(B)).astype(f32), "base": grid.reshape(P, -1),
        "boff": rows(np.concatenate([a["L0_conv_b_off"].reshape(-1), a["L0_conv_b_mask"]])),
        "pidx": np.stack([p, p + P], 1).astype(f32),
        "cs": np.stack([np.cos(turn), np.sin(turn)], 2).reshape(P, -1),
        "sgn": np.where(p % 2 == 0, 1.0, -1.0), "tokidx": np.stack([p, p + P], 1),
        "lt4": rows(np.tril(np.ones((4, 4)), -1)), "lt8": rows(np.tril(np.ones((8, 8)), -1)),
        "neghalf": np.full((P, 8), -0.5), "quarter": np.full((P, NF), 0.25),
        "frac": rows(np.array([N, N // 2, N // 4, N // 8])),
        "fold": p[:, None] % C == np.arange(C),
        "headsel": (np.arange(NHEAD)[None, None] == np.arange(HG)[None, :, None] * 4 + p[:, None, None] // D).reshape(P, -1),
        "gumbel": rows(a["L3_ffn_gumbel"]), "logw": rows(a["L3_ffn_log_weights"])})
    q8_image, q8_channel = p % C // HC, p % HC
    w_dw = a["L0_conv_w_dw"].reshape(3, C, K2)
    front = pack(FRONT, {
        "wqkv": np.concatenate([diagonal(a["L0_conv_w_qkv"][:, j * C:(j + 1) * C]) for j in range(3)], 1),
        "wdw": images(w_dw.transpose(1, 0, 2)), "bqkv": images(a["L0_conv_b_qkv"].reshape(3, C).T),
        "bdw": images(a["L0_conv_b_dw"].reshape(3, C).T),
        "select": (q8_image * C + q8_channel)[None, :] == p[:, None], "bmask8": q8_image[:, None] == np.arange(B)})
    wo = np.concatenate([a["L0_conv_w_off"].reshape(G * 2 * K2, C), a["L0_conv_w_mask"]], 0).T
    pw = np.zeros((PWK, 3, P), f32)
    pwo = np.zeros((PWK, NOFF), f32)
    for s in range(5):
        w = a["L0_conv_pconv_off_w"][s] if s < G else a["L0_conv_pconv_mask_w"]
        w = w.reshape(HC, HC, K2)
        rows_s, cols_s = slice(s * HC, (s + 1) * HC), slice(s * 2 * K2, (s + 1) * 2 * K2 if s < G else NOFF)
        for i in range(2):
            pw[rows_s, i] = np.repeat(w[:, :, list(AROUND[4 * i:4 * i + 4])].transpose(0, 2, 1)[:, :, None], B, 2).reshape(HC, P)
        pw[rows_s, 2].reshape(HC, B, C)[:, :, 0:HC] = w[:, None, :, K2 // 2]
        pwo[rows_s, cols_s] = wo[0:HC, cols_s]
    pw[5 * HC:, 2] = (np.arange(C)[:, None] == p % C) * (p % C >= HC)
    pwo[5 * HC:] = wo
    pw = np.concatenate([pw.reshape(PWK, -1), pwo], 1)
    l1 = pack(L1, {
        "wproj": diagonal(a["L0_conv_w_proj"]), "bproj": images(a["L0_conv_b_proj"]),
        "red": images(a["L1_conv_reduction_kernel"]),
        "convk": images(a["L1_conv_conv_kernels"].reshape(4, K2, C, C).transpose(2, 0, 1, 3)),
        "kbias": images(a["L1_conv_bias"].T), "bnscale": images(a["L1_conv_bn_scale"]),
        "bnbias": images(a["L1_conv_bn_bias"]), "bnmean": images(a["L1_conv_bn_mean"]),
        "bnvar": images(a["L1_conv_bn_var"])})
    future = np.where(p[None, :] > p[:, None], -1e12, 0.0).astype(f32)
    l2 = pack(L2, {"wq": diagonal(a["L2_attn_Wq"]), "wk": diagonal(a["L2_attn_Wk"]), "wv": diagonal(a["L2_attn_Wv"]),
                   "causal": np.concatenate([future, np.zeros((P, P), f32), future], 1)})
    def stack(v):
        return np.concatenate([v] * 4, 0)

    moe = stack(np.concatenate([a["L2_ffn_expert_w"].transpose(1, 0, 2).reshape(C, -1), a["L2_ffn_router_w"]], 1))
    moeb = rows(np.concatenate([a["L2_ffn_expert_b"].reshape(-1), a["L2_ffn_router_b"]]))
    l3w = stack(np.concatenate([a["L3_attn_wq_w"].T, a["L3_attn_wk_w"].T], 1))
    l3b = rows(np.concatenate([a["L3_attn_wq_b"], a["L3_attn_wk_b"]]), 3)
    l3 = pack(L3, {"dense": a["L3_attn_dense_w"].T.reshape(HG, P, D).transpose(1, 0, 2).reshape(P, -1),
                   "denseb": rows(a["L3_attn_dense_b"]),
                   "wv": np.tile(a["L3_attn_wv_w"].reshape(HG, P, 1, C).transpose(1, 0, 2, 3), (1, 1, 4, 1)).reshape(P, -1),
                   "bv": np.repeat(a["L3_attn_wv_b"].reshape(HG, P).T, 3, 1)})
    angle = (1.57 * np.arange(N, dtype=f32) / N).astype(f32)
    turn_rows = lambda n: np.concatenate([np.tile(np.cos(angle), (n, 1)), np.tile(np.sin(angle), (n, 1)),
                                          np.zeros((P - 2 * n, N), f32)], 0)
    ex = np.zeros((P, DH), f32)
    ex[0:NPART] = np.arange(NPART)[:, None] % NHEAD == np.arange(DH)[None, :] // D
    turn = pack(TURN, {"cs_out": turn_rows(D), "expand": ex})
    mphi = np.stack([a["L3_ffn_M_phi_plus"], a["L3_ffn_M_phi_minus"]], 1)
    stu = np.concatenate([mphi.transpose(3, 0, 1, 2, 4).reshape(D, NSC, -1),
                          a["L3_ffn_M_u"].transpose(2, 0, 1, 3).reshape(D, NSC, -1)], 2).reshape(D, -1)
    stu = stack(np.concatenate([stu, rows(a["L3_ffn_sigma"], D)], 1))
    shifts = (np.arange(N)[:, None] == np.arange(1, KU)).astype(f32)
    phi = np.concatenate([np.zeros((P - 1, NF + KU - 1), f32),
                          np.concatenate([a["L3_ffn_phi"][:N], shifts], 1)], 0)
    toep = phi[(np.arange(N)[None, :] - p[:, None]) + P - 1].transpose(0, 2, 1).reshape(P, -1)
    x_ch = a["x"].reshape(B, N, C).transpose(0, 2, 1).reshape(P, N)

    host = dict(x_ch=x_ch, cst=cst, front=front, pw=pw, l1=l1, attk=a["L1_conv_attention_kernel"], l2=l2, moe=moe,
                moeb=moeb, l3w=l3w, l3b=l3b, l3=l3, turn=turn, stu=stu, toep=toep)
    nc = bacc.Bacc("TRN2", target_bir_lowering=False, num_devices=1)
    arrays, args = {}, []
    for name, v in host.items():
        v = np.ascontiguousarray(v, dtype=f32)
        arrays[f"in_{name}"] = v
        args.append(nc.dram_tensor(f"in_{name}", v.shape, F32, kind="ExternalInput").ap())
    args.append(nc.dram_tensor("out_x", (P, T * C), F32, kind="ExternalOutput").ap())
    hybrid(nc, *args)
    r = run_bass_kernel_spmd(nc, [arrays], core_ids=[0])
    got = r.results[0]["out_x"]
    return got.reshape(P, NH, B, C).transpose(2, 1, 0, 3).reshape(B, H, W, C)
```

```python
from contextlib import ExitStack

import concourse.bass as bass
from concourse import mybir

F32 = mybir.dt.float32
BF16 = mybir.dt.bfloat16
ALU = mybir.AluOpType
ACT = mybir.ActivationFunctionType
AX = mybir.AxisListType

P = 128
B, H, W, C = 4, 16, 16, 32
N = H * W
NH = N // P
T = B * NH
G, HC, K2 = 4, 8, 9
J = G * K2
NOFF = J * 2 + K2
KV = 2 * HC
SLOT = 4 * KV
HP, WP = H + 2, W + 2
E = 8
NHEAD, D = 16, 32
HG = NHEAD * D // P
NF = 16
KU = 3
NSC = 4
STU = 2 * NF * D + KU * D
DH = NHEAD * D
HCOLS = 2 * P + 2
ROUND = 1.5 * 2.0 ** 23
BANK = 512

CST = (("ident", P), ("bmask", B), ("base", NH * 2 * J), ("boff", NOFF), ("pidx", 2), ("cs", 2 * NH),
       ("tokidx", 2), ("lt4", 16), ("lt8", 64), ("neghalf", 8), ("quarter", NF), ("frac", NSC),
       ("fold", C), ("headsel", 64),
       ("gumbel", NSC), ("logw", NSC))
FRONT = (("wqkv", 3 * P), ("wdw", 27), ("bqkv", 3), ("bdw", 3), ("select", P), ("bmask8", B))
AROUND = (0, 1, 2, 3, 5, 6, 7, 8)
PWK = 5 * HC + C
L1 = (("wproj", P), ("bproj", 1), ("red", 4), ("convk", 4 * K2 * C), ("kbias", 4), ("bnscale", 1),
      ("bnbias", 1), ("bnmean", 1), ("bnvar", 1))
L2 = (("wq", P), ("wk", P), ("wv", P), ("causal", 3 * P))
L3 = (("dense", HG * D), ("denseb", D), ("wv", HG * P), ("bv", 3 * HG))
XT = P + 1
LAGS = P + XT
PARITY = 2 * 3 * (P // 2)
TURN = (("cs_out", N), ("expand", NHEAD * D))
NPART = 3 * NHEAD


def width(block):
    return sum(n for _, n in block)


def columns(tensor, block):
    out, at = {}, 0
    for name, n in block:
        out[name] = tensor[:, at:at + n]
        at += n
    return out


class Steps:

    def __init__(self, semaphore, names):
        self.sem, self.names, self.said = semaphore, names.split(), 0
        assert len(set(self.names)) == len(self.names)

    def __getitem__(self, name):
        return self.names.index(name) + 1

    def step(self, name):
        assert self.names[self.said] == name, (self.names[self.said], name)
        self.said += 1
        return 1


def hybrid(nc, x_ch, cst_d, front_d, pw_d, l1_d, attk_d, l2_d, moe_d, moeb_d, l3w_d, l3b_d, l3_d, turn_d, sigma_d, stu_d, toep_d, parity_d, out, DBG=()):
    with ExitStack() as ctx:
        def sb(name, shape, dt=F32):
            return ctx.enter_context(nc.sbuf_tensor(name, shape, dt))

        def sem(name):
            return ctx.enter_context(nc.semaphore(name))

        x = sb("x", [P, N])
        cst = sb("cst", [P, width(CST)])
        front = sb("front", [P, width(FRONT)])
        l1 = sb("l1", [P, width(L1)])
        attk = sb("attk", [4, 4])
        l2 = sb("l2", [P, width(L2)])
        moe = sb("moe", [P, E * C + E])
        moeb = sb("moeb", [P, E * C + E])
        moe_w1 = sb("moe_w1", [P, E * C + E], BF16)
        moe_w2 = sb("moe_w2", [P, E * C + E], BF16)
        l3w = sb("l3w", [P, 3 * DH])
        l3 = sb("l3", [P, width(L3)])
        stu_fq = sb("stu_fq", [P, 4096])
        stu_sig = sb("stu_sig", [P, NF])
        wscale = sb("wscale", [P, NSC])
        wcol = sb("wcol", [P, 1])
        wpick = sb("wpick", [P, P])
        nwpick = sb("nwpick", [P, P])
        stu, fq = stu_fq[:, 0:STU], stu_fq[:]
        biasb = stu_fq[:].bitcast(BF16)
        c, f, p1, p2, p3 = columns(cst, CST), columns(front, FRONT), columns(l1, L1), columns(l2, L2), columns(l3, L3)
        ident = c["ident"]
        identb = sb("identb", [P, P], BF16)
        neg1 = sb("neg1", [P, 1])
        pos1 = sb("pos1", [P, 1])

        stats = sb("stats", [P, 6])
        moments = sb("moments", [P, 2])
        var_eps = sb("var_eps", [P, T])
        rstd = sb("rstd", [P, T])
        bn_var_eps = sb("bn_var_eps", [P, 1])
        bn_inv = sb("bn_inv", [P, 1])
        xg = sb("xg", [P, N])
        qkv_pad = sb("qkv_pad", [P, 3 * HP * WP])
        q_flat = sb("q_flat", [P, N + 2 * (W + 1)])
        kv = sb("kv", [P, 2 * (N + WP)])
        comp = sb("comp", [P, 2 * T * C])
        q_tok = sb("q_tok", [P, T * C])
        base = sb("base_b", [P, NH * 2 * J])
        w4 = sb("w4", [P, T * J * 4])
        gate_m = sb("gate_m", [P, T * K2])
        mask_x = sb("mask_x", [P, T * J])
        index = sb("index", [P, T * J], BF16)
        table = sb("table", [P, 2 * 3 * B * G * SLOT], BF16)
        indexb = sb("indexb", [P, 2 * J * P], BF16)
        onehot = sb("onehot", [P, 2 * 2 * J * P], BF16)
        arena = sb("arena", [P, 15296])
        dots = sb("dots", [P, J * 4])
        logit = sb("logit", [P, J])
        peak = sb("peak", [P, G])
        pexp = sb("pexp", [P, J])
        psum_ = sb("psum_", [P, T * G])
        pinv = sb("pinv", [P, T * G])
        w4p = sb("w4p", [P, J * 4])
        att = sb("att", [P, T * C])
        x1 = sb("x1", [P, N])
        x1_pad = sb("x1_pad", [P, HP * WP])
        pool = sb("pool", [P, 1])
        pool_bd = sb("pool_bd", [P, B])
        pool_red = sb("pool_red", [4, P])
        kmax = sb("kmax", [P, 1])
        kexp = sb("kexp", [P, 4])
        ksum_ = sb("ksum_", [P, 1])
        kinv = sb("kinv", [P, 1])
        katt = sb("katt", [P, 4])
        bmix = sb("bmix", [P, 4])
        bsum = sb("bsum", [P, 1])
        bshift = sb("bshift", [P, 1])
        x2t = xg
        lsum = sb("lsum", [P, T])
        lvar = sb("lvar", [P, T])
        ln = sb("ln", [P, T * C])
        smax = sb("smax", [P, T])
        ssum = sb("ssum", [P, T])
        sinv = sb("sinv", [P, T])
        rlog = sb("rlog", [P, T * E])
        rank = sb("rank", [P, T * E])
        chosen = sb("chosen", [P, T * E])
        rmax = sb("rmax", [P, T])
        rexp = sb("rexp", [P, T * E])
        rsum = sb("rsum", [P, T])
        ks_sb = sb("ks_sb", [P, HG * B * 2])
        zsel = sb("zsel", [P, NSC])
        zmax = sb("zmax", [P, 1])
        zsum = sb("zsum", [P, 1])
        soft = sb("soft", [P, NSC])
        zgt = sb("zgt", [P, NSC * NSC])
        zeq = sb("zeq", [P, NSC * NSC])
        hard = sb("hard", [P, NSC])
        wsel = sb("wsel", [P, NSC])
        length = sb("length", [P, 1])
        window = sb("window", [P, 2])
        sig4 = sb("sig4", [P, NF])
        msel = sb("msel", [P, STU])

        gath = arena[:, 0:2 * NH * J * SLOT]
        comp_bd, q_stack = arena[:, 0:3 * B * NOFF], arena[:, 1024:1024 + 2 * N]
        fk, vcs = arena[:, 0:4096], arena[:, 4096:4096 + T * HG * HCOLS]
        v_sum, v_diff = arena[:, 0:NF * N], arena[:, NF * N:2 * NF * N]
        ar_v, toep = arena[:, 8192:8192 + KU * N], arena[:, 8960:8960 + NF * LAGS + XT]
        att_ch, y1, x2, ctx_n, qc, kc, vt, ln_ch, x4d, x5p = (
            arena[:, 12416 + i * N:12416 + (i + 1) * N] for i in range(10))
        side = 2 * NH * J * SLOT
        pos, near, away, hat0, hat1 = (arena[:, side + i * T * 2 * J:side + (i + 1) * T * 2 * J] for i in range(5))
        prod_k, prod_v = (arena[:, side + i * J * 4 * HC:side + (i + 1) * J * 4 * HC] for i in range(2))
        side += 5 * T * 2 * J
        hats = arena[:, side:side + 2 * T * 2 * J]
        side += 2 * T * 2 * J
        rest = arena[:, side:side + 4 * BANK]
        late = onehot[:].bitcast(F32)
        pw = late[0:PWK, 0:3 * P + NOFF]
        gated, late_b = late[:, 4096:4096 + T * C * E], late.bitcast(BF16)
        l3b, w1, w2 = late[:, 0:3 * DH], late_b[:, 3072:3072 + 3 * DH], late_b[:, 4608:4608 + 3 * DH]
        turns = columns(late[:, 3072:3072 + width(TURN)], TURN)
        experts = late[:, 6912:6912 + T // 2 * E * C]
        ks_bd = late[:, 5128:5640]
        prob, prob_t = late[:, 6144:6144 + B * 3 * P], late[:, 7680:7680 + B * 3 * P]
        expandb, den_parts = late_b[:, 12288:12288 + DH], late_b[:, 12800:12800 + T * P]
        den_ch, oc = late[0:32, 6912:6912 + T * P], late[0:2 * D, 7936:7936 + T * P]
        den, den_p = late[:, 4096:4096 + T * NHEAD], late_b[:, 2 * 4224:2 * 4224 + T * NPART]
        late3 = table[:].bitcast(F32)
        late3_b = table[:]
        stu_w1, stu_w2 = late3_b[:, 0:STU], late3_b[:, 4096:4096 + STU]
        parity = late3[:, 2608:2608 + PARITY]
        x3t, x4t, x5t, x6t = (late3[:, 1024 + i * N:1024 + (i + 1) * N] for i in range(4))
        lcen, lsq = comp[:, 0:T * C], comp[:, T * C:2 * T * C]
        late2 = indexb[:].bitcast(F32)
        score, mcs, req, wmix = (late2[:, 0:1536], late2[:, 1536:2560], late2[:, 1536:1536 + T * E * E],
                                late2[:, 2048:2048 + K2 * C])
        parts, stack1, stack2 = indexb[:, 0:1024], indexb[:, 1024:2048], indexb[:, 2048:3072]
        wmix_bd, rgt = late2[:, 2816:2816 + K2 * P], late2[:, 3968:3968 + T * E * E]

        ps = ctx.enter_context(nc.psum_tensor("ps", [P, 8, BANK], F32))

        d_x, d_cst, d_front, d_pw, d_l1, d_l2, d_moe, d_l3, d_stu, d_toep, d_parity, d_late, d_out = (
            sem("loaded_" + n) for n in ("x", "cst", "front", "pw", "l1", "l2", "moe", "l3", "stu", "toep", "parity", "late", "out"))

        v0 = Steps(sem("vector_front"), "identb neg1 pos1 base stats moments eps xg comp0 comp1 "
                   + " ".join(f"q{t}" for t in range(K2)) + " s20 s21 s30 s31 "
                   + " ".join(f"k{t} v{t}" for t in range(K2))
                   + " pos gate clamp near0 near1 near index rest0 rest1 rest2 rest3 low0 low1 low2 low3"
                   + " away hat0a hat0 gate1 sigmoid maskx hatm w4")
        a0 = Steps(sem("scalar_front"), "q k v s00 s01 s10 s11 qtok high0 high1 high2 high3 mid0 mid1 mid2 mid3"
                   " sigexp hat1a hat1")
        t0 = Steps(sem("tensor_front"), "comp q k v select offsets qtok table0 table1 table2 table3")
        g0 = Steps(sem("pool_steps"), "qkvpad qpad stackpad kvpad xpad rstd0 bnvar bninv sigma "
                   + ""
                   + " rstd1 rstd2 sm ones rstd30 rstd31 gated rstd40 rstd41 "
                   "rstd50 rstd51")
        s_bc = sem("index_spread")
        s_bce = sem("index_copied")
        s_oh = sem("onehot_ready")
        s_gp = sem("samples_in_psum")
        s_ge = sem("samples_copied")
        s_un = sem("unit_gathered")
        s_pk = sem("keys_product")
        s_pv = sem("values_product")
        s_px = sem("attention_exp")

        def unit_steps(u):
            names = []
            if 4 <= u <= T:
                names += [f"mixed{u - 4}"]
            if u >= 3:
                names += [f"w4p{u - 3}"]
            if 2 <= u < T + 2:
                names += [f"{n}{u - 2}" for n in ("dots", "wdots", "logit", "peak")]
            if u >= T:
                names += [f"mixed{u - 3}"]
            return names

        v1 = Steps(sem("vector_units"), " ".join(n for u in range(T + 3) for n in unit_steps(u)) + " inv att")

        t2 = Steps(sem("tensor_conv"), "attT proj poolred katt conv x2T")
        a2 = Steps(sem("scalar_conv"), "attT poolred kexp y1")
        v2 = Steps(sem("vector_conv"), "x1 stats moments eps xpad pool poolbd kmax kneg kinv katt mix0 mix1 mix2 mix3"
                   " mixbd0 mixbd1 mixbd2 bmix bsum binv bcent bshift x2 x2t")
        LN = "sum cen sq var eps ln "
        v3 = Steps(sem("vector_attn"), LN + "kc score0 " + " ".join(f"score{b + 1} first{b} second{b} neg{b}" for b in range(B - 1))
                   + f" first{B - 1} second{B - 1} neg{B - 1} sinv pt1 pt3 ctx x3")
        a3 = Steps(sem("scalar_attn"), "lnT qc vt " + " ".join(f"exp{b} exp{B + b}" for b in range(B)) + " pt0 pt2")
        t3 = Steps(sem("tensor_attn"), "lnT qc kc vt score0 score1 score2 score3 pt0 pt1 pt2 pt3 pv")
        v4 = Steps(sem("vector_moe"), "sum0 cen0 sq0 var0 eps0 sum1 cen1 sq1 var1 eps1 ln0 ph0 pr0 pl0 ln1 ph1 pr1 pl1 s1b s2b "
                   + "rlog0 rgt0 req0 reqlt0 rsum0 rank0 rlog1 rgt1 req1 reqlt1 rsum1 rank1 rmax rsub chosen esel esum einv gated y0 ynorm0 x40 y1 ynorm1 x41")
        a4 = Steps(sem("scalar_moe"), "pm0 pd0 pm1 pd1 s1a s2a experts rexp")
        t4 = Steps(sem("tensor_moe"), "st0 st1 experts0 experts1")
        v5 = Steps(sem("vector_linear"), "sum0 cen0 sq0 var0 eps0 ln0 ph0 pr0 sum1 cen1 pl0 sq1 var1 eps1 cs0 cs1 ln1 ph1 pr1 pl1 s1b s2b "
                   + " ".join(f"fk{t} vs{t}" for t in range(T)) + " fq0 fq1 fq2 fq3 ks1 kv1 fq4 fq5 fq6 fq7 ks3 ksb kv3 bias"
                   + " "
                   + " ".join(f"cos{i}0 cos{i}1 den{i}0 den{i}1 inv{i} dh{i} dr{i} dm{i} ds{i} dl{i}" for i in range(2)) + " "
                   + " ".join(f"qn{i}" for i in range(8)) + " oc0 x50 oc1 x51")
        a5 = Steps(sem("scalar_linear"), "pm0 pd0 s1a s2a pm1 pd1 expand " + " ".join(f"ek{t} vc{t}" for t in range(T))
                   + " eq0 eq1 kv0 eq2 eq3 eq4 eq5 kv2 eq6 eq7 dc0 dc1 dp0 dp1")
        t5 = Steps(sem("tensor_linear"), "st0 k0 v0 k1 v1 st1 " + " ".join(f"k{t} v{t}" for t in range(2, T))
                   + " q0 q1 kv0 q2 q3 kv1 q4 q5 kv2 q6 q7 kv3 den0 denT0 den1 denT1 dp0 "
                   + "ex0 ex1 ex2 ex3 dp1 ex4 ex5 ex6 out0 ex7 fold0 out1 fold1")
        tw = Steps(sem("tensor_weights"), "wd sel")
        aw = Steps(sem("scalar_weights"), "mhi sel0 sel1 sel2 mbh wdw0 wdb0 wdw1 wdb1 wdw2 wdb2 wdw3 wdb3 lhi lb1 lbh mmid mbm lmid lbm mw2m mw2h lw2m lw2h shi smid")
        gw = Steps(sem("pool_weights"), "mres mbres lres lbres mlow mblow llow lblow sres slow")
        vz = Steps(sem("vector_select"), "z zmax zneg zinv soft zgt zeq zeqlt zadd rank hard diff w lenp length win wrow wcol wpick nwpick")
        az = Steps(sem("scalar_select"), "exp")
        v6 = Steps(sem("vector_stu"), "sum0 cen0 sq0 var0 eps0 ln0 ph0 pr0 sum1 cen1 pl0 sq1 var1 eps1 ln1 ph1 pr1 pl1 s1b "
                   + " ".join(f"vm{t}" for t in range(T)) + " ar1 x5p1 x6a x6")
        a6 = Steps(sem("scalar_stu"), "pm0 pd0 s1a pm1 pd1 vp0 vp1 vp2 vp3 ar0 x5p0 vp4 vp5 vp6 vp7")
        t6 = Steps(sem("tensor_stu"), "st0 v0 v1 st1 " + " ".join(f"v{t}" for t in range(2, T)) + " out")

        block = ctx.enter_context(nc.Block())

        img = lambda ap: ap.rearrange("p (y x) -> p y x", y=H)
        qkvp = qkv_pad[:].rearrange("p (j y x) -> p j y x", j=3, y=HP)
        q_mid = q_flat[:, W + 1:W + 1 + N]
        q_st = q_stack.rearrange("p (s y x) -> p s y x", s=2, y=H)
        xp = x1_pad[:].rearrange("p (y x) -> p y x", y=HP)
        kvv = kv[:].rearrange("p (j n) -> p j n", j=2)
        tabv = table[:].rearrange("p (q r s k d) -> p q r s k d", q=2, r=3, s=B * G, k=4)
        ohv = onehot[:].rearrange("p (u q j n) -> p u q j n", u=2, q=2, j=J)
        ixb = indexb[:].rearrange("p (u j n) -> p u j n", u=2, j=J)
        gv = gath.rearrange("p (r s d) -> p r s d", r=2, s=NH * J)
        tok = lambda ap: ap.rearrange("p (t c) -> p t c", t=T)
        tokhb = lambda ap: ap.rearrange("p (h b c) -> p h b c", b=B, h=NH)
        vcv = vcs.rearrange("p (t g n) -> p t g n", t=T, g=HG)
        fqv = fq.rearrange("p (g h b n) -> p g h b n", g=HG, h=NH, b=B)
        mcv = mcs.rearrange("p (g b s e) -> p g b s e", g=HG, b=B, s=2)
        NV = T // 2
        tce = lambda ap: ap.rearrange("p (t c e) -> p t c e", e=E, c=C)
        def half_of(ap, q):
            return ap.rearrange("p (q n) -> p q n", q=2)[:, q, :]

        def parts_of(q):
            return half_of(parts, q).rearrange("p (t r c) -> p t r c", r=4, c=C)

        def stacked_half(q):
            return ps[:, 6 + q, :].bitcast(BF16)[:, 0:BANK]

        tiles4 = lambda ap: ap.rearrange("p (t c) -> p t c", c=C)


        def small(q):
            return ps[:, 6 + q, 0:KU * BANK // 4], ps[:, 6 + q, KU * BANK // 4:]

        TILES = [(r * B + b, r, b) for q in range(2) for r in range(2) for b in (2 * q, 2 * q + 1)]
        arp = ar_v.rearrange("p (i r q n) -> p i r q n", i=KU, r=2, q=2)
        x5pv = x5p.rearrange("p (r q n) -> p r q n", r=2, q=2)
        DB = (2, 7)
        EB = (3, 4, 5, 6, 7, 0)
        psb = [ps[:, i, :].bitcast(BF16) for i in range(2)]
        AR_BANK = 4
        SELECTED = ((2, 0, NF * D), (3, NF * D, NF * D), (AR_BANK, 2 * NF * D, KU * D))
        WB = (0, 1, 6, 7)
        BROWS = slice(2 * C, 2 * C + 3)
        GRP = NH * J // 8

        def rep(ap, n):
            return ap.unsqueeze(len(ap.shape)).broadcast_to(list(ap.shape) + [n])

        groups = lambda u: ((u + 1) * J + 7) // 8

        EXP_AT = 6
        POOL_K, POOL_V = 6, 7

        def samples(u):
            return gv[:, u // NH % 2, u % NH * J:(u % NH + 1) * J, :].rearrange("p (g s) (k d) -> p g (s k) d", g=G, k=4)

        def keys_product(engine, u):
            q = q_tok[:, u * C:(u + 1) * C].rearrange("p (g d) -> p g d", g=G)
            return engine.tensor_tensor(out=prod_k.rearrange("p (g n d) -> p g n d", g=G, d=HC), in0=samples(u)[:, :, :, 0:HC],
                                        in1=q.unsqueeze(2).broadcast_to([P, G, 4 * K2, HC]), op=ALU.mult)

        def values_product(engine, u):
            w = w4p[:].rearrange("p (g n) -> p g n", g=G)
            return engine.tensor_tensor(out=prod_v.rearrange("p (g d n) -> p g d n", g=G, d=HC),
                                        in0=samples(u)[:, :, :, HC:KV].rearrange("p g n d -> p g d n"),
                                        in1=w.unsqueeze(2).broadcast_to([P, G, HC, 4 * K2]), op=ALU.mult)

        TB = (4, 5, 2, 3)
        IB = (0, 1, 6, 7)

        def shifted_queries(copy, r, s):
            tap = AROUND[4 * s + r]
            dy, dx = tap // 3 - 1, tap % 3 - 1
            rows, at = slice(r * C, (r + 1) * C), (dy + 1) * W + dx + 1
            cols = slice(max(0, -dx), W - max(0, dx))
            return copy(q_st[rows, s, :, cols], img(ps[rows, 7, at:at + N])[:, :, cols])

        def bias_hi(layer):
            return biasb[BROWS, 3072 * 2:3072 * 2 + 264] if layer == "m" else biasb[BROWS, 0:3 * DH]

        def bias_mid(layer):
            return biasb[BROWS, 3072 * 2 + 264:3072 * 2 + 528] if layer == "m" else biasb[BROWS, 3 * DH:6 * DH]

        def keys_sums(copy, hg):
            return copy(ks_sb[:, hg * 2 * B:(hg + 1) * 2 * B].rearrange("p (b s) -> p b s", b=B), ps[:, 4:8, 2 * P:HCOLS])

        def heads_products(copy, hg):
            acc = ps[:, 4:8, 0:2 * P].rearrange("p b (s r e) -> p b s r e", s=2, r=4)
            for r in range(4):
                rows = slice(r * D, (r + 1) * D)
                ins = copy(mcv[rows, hg], acc[rows, :, :, r, :])
            return ins

        @block.sync
        def _(sp):
            sp.dma_start(x[:], x_ch).then_inc(d_x, 16)
            sp.dma_start(front[:], front_d).then_inc(d_front, 16)
            sp.dma_start(pw, pw_d).then_inc(d_pw, 16)
            sp.dma_start(l1[:], l1_d).then_inc(d_l1, 16)
            sp.dma_start(attk[:], attk_d).then_inc(d_l1, 16)
            sp.dma_start(l2[:], l2_d).then_inc(d_l2, 16)
            sp.dma_start(moe[:], moe_d).then_inc(d_moe, 16)
            sp.dma_start(moeb[:], moeb_d).then_inc(d_moe, 16)
            sp.dma_start(l3w[:, 0:2 * DH], l3w_d).then_inc(d_l3, 16)
            sp.dma_start(l3[:], l3_d).then_inc(d_l3, 16)
            sp.dma_start(stu_sig[:], sigma_d).then_inc(d_stu, 16)
            sp.dma_start(stu, stu_d).then_inc(d_stu, 16)
            sp.wait_ge(s_un, T)
            sp.dma_start(l3b[BROWS, 0:2 * DH], l3b_d).then_inc(d_late, 16)
            sp.dma_start(late[:, 3072:3072 + width(TURN)], turn_d).then_inc(d_late, 16)
            sp.dma_start(parity, parity_d).then_inc(d_parity, 16)
            sp.wait_ge(t5.sem, t5["kv3"])
            sp.dma_start(toep, toep_d).then_inc(d_toep, 16)
            sp.wait_ge(v6.sem, v6["x6"])
            sp.dma_start(out, x6t).then_inc(d_out, 16)
            sp.wait_ge(d_out, 16)

        @block.gpsimd
        def _(pool_e):
            nc.gpsimd.memset(qkv_pad[:], 0.0).then_inc(g0.sem, g0.step("qkvpad"))
            nc.gpsimd.memset(q_flat[:], 0.0).then_inc(g0.sem, g0.step("qpad"))
            nc.gpsimd.memset(q_stack, 0.0).then_inc(g0.sem, g0.step("stackpad"))
            nc.gpsimd.memset(kv[:], 0.0).then_inc(g0.sem, g0.step("kvpad"))
            nc.gpsimd.memset(x1_pad[:], 0.0).then_inc(g0.sem, g0.step("xpad"))

            def power(out_ap, in_ap, exponent, name):
                nc.gpsimd.tensor_tensor(out=out_ap, in0=in_ap, in1=exponent, op=ALU.pow).then_inc(g0.sem, g0.step(name))

            pool_e.wait_ge(d_cst, 16)
            pool_e.wait_ge(v0.sem, v0["eps"])
            power(rstd[:, 0:1], var_eps[:, 0:1], c["neghalf"][:, 0:1], "rstd0")
            pool_e.wait_ge(d_l1, 32)
            nc.gpsimd.tensor_scalar(bn_var_eps[:], p1["bnvar"], 1e-5, None, ALU.add).then_inc(g0.sem, g0.step("bnvar"))
            pool_e.wait_ge(g0.sem, g0["bnvar"])
            power(bn_inv[:], bn_var_eps[:], c["neghalf"][:, 0:1], "bninv")
            pool_e.wait_ge(d_stu, 32)
            power(sig4[:], stu_sig[:], c["quarter"], "sigma")
            pool_e.wait_ge(v0.sem, v0["w4"])
            pool_e.wait_ge(a0.sem, a0["hat1"])
            for u in range(max(POOL_K, POOL_V + 1)):
                if u < POOL_K:
                    pool_e.wait_ge(s_ge, groups(u))
                    if u:
                        pool_e.wait_ge(v1.sem, v1[f"dots{u - 1}"])
                    keys_product(nc.gpsimd, u).then_inc(s_pk, 1)
                if 1 <= u <= POOL_V:
                    pool_e.wait_ge(v1.sem, v1[f"w4p{u - 1}"])
                    values_product(nc.gpsimd, u - 1).then_inc(s_pv, 1)
            def minus(out_ap, in_ap, part, name, after):
                steps, before = after
                pool_e.wait_ge(steps.sem, steps[before])
                nc.gpsimd.tensor_tensor(out=out_ap, in0=in_ap, in1=part, op=ALU.subtract).then_inc(gw.sem, gw.step(name))

            LROWS = slice(3 * C, P)
            pool_e.wait_ge(v2.sem, v2["eps"])
            power(rstd[:, 0:1], var_eps[:, 0:1], c["neghalf"][:, 0:1], "rstd1")
            pool_e.wait_ge(aw.sem, aw["mhi"])
            minus(moe[:], moe[:], moe_w1[:], "mres", (g0, "rstd1"))
            pool_e.wait_ge(aw.sem, aw["mbh"])
            minus(moeb[BROWS, :], moeb[BROWS, :], bias_hi("m"), "mbres", (gw, "mres"))
            pool_e.wait_ge(aw.sem, aw["lhi"])
            minus(l3w[:], l3w[:], w1, "lres", (gw, "mbres"))
            pool_e.wait_ge(aw.sem, aw["lbh"])
            minus(l3b[BROWS, :], l3b[BROWS, :], bias_hi("l"), "lbres", (gw, "lres"))
            pool_e.wait_ge(aw.sem, aw["mmid"])
            minus(moe_w1[LROWS, :], moe[LROWS, :], moe_w2[LROWS, :], "mlow", (gw, "lbres"))
            pool_e.wait_ge(aw.sem, aw["mbm"])
            minus(moe_w2[BROWS, :], moeb[BROWS, :], bias_mid("m"), "mblow", (gw, "mlow"))
            pool_e.wait_ge(aw.sem, aw["lmid"])
            minus(w1[LROWS, :], l3w[LROWS, :], w2[LROWS, :], "llow", (gw, "mblow"))
            pool_e.wait_ge(aw.sem, aw["lbm"])
            minus(w2[BROWS, :], l3b[BROWS, :], bias_mid("l"), "lblow", (gw, "llow"))
            pool_e.wait_ge(v3.sem, v3["eps"])
            pool_e.wait_ge(gw.sem, gw["lblow"])
            power(rstd[:], var_eps[:], c["neghalf"], "rstd2")
            pool_e.wait_ge(aw.sem, aw["sel2"])
            mk = msel[:, 0:2 * NF * D].rearrange("p (m k e) -> p m k e", m=2, k=NF)
            nc.gpsimd.tensor_tensor(out=mk, in0=mk, in1=rep(sig4[:].unsqueeze(1).broadcast_to([P, 2, NF]), D),
                                    op=ALU.mult).then_inc(g0.sem, g0.step("sm"))
            pool_e.wait_ge(t3.sem, t3["pv"])
            pool_e.wait_ge(g0.sem, g0["sm"])
            nc.gpsimd.memset(stack2[BROWS, :], 1.0).then_inc(g0.sem, g0.step("ones"))
            for name, v, before in (("rstd3", v4, (g0, "ones")), ("rstd4", v5, (gw, "sres")), ("rstd5", v6, (gw, "slow"))):
                for half in range(2):
                    cols = slice(half * T // 2, (half + 1) * T // 2)
                    pool_e.wait_ge(v.sem, v[f"eps{half}"])
                    pool_e.wait_ge(before[0].sem, before[0][before[1]])
                    power(rstd[:, cols], var_eps[:, cols], c["neghalf"][:, cols], f"{name}{half}")
                    before = (g0, f"{name}{half}")
                if v is v4:
                    pool_e.wait_ge(a4.sem, a4["experts"])
                    pool_e.wait_ge(v4.sem, v4["esel"])
                    nc.gpsimd.tensor_tensor(out=tce(gated[:, NV * E * C:]),
                                            in0=experts.rearrange("p (t e c) -> p t c e", e=E, c=C),
                                            in1=chosen[:].rearrange("p (t e) -> p t e", e=E)[:, NV:].unsqueeze(2)
                                            .broadcast_to([P, T - NV, C, E]), op=ALU.mult).then_inc(g0.sem, g0.step("gated"))
                    pool_e.wait_ge(aw.sem, aw["shi"])
                    minus(msel[:], msel[:], stu_w1, "sres", (g0, "gated"))
                if v is v5:
                    pool_e.wait_ge(aw.sem, aw["smid"])
                    minus(stu_w1[LROWS, :], msel[LROWS, :], stu_w2[LROWS, :], "slow", (g0, "rstd41"))

        @block.scalar
        def _(act):
            act.dma_start(cst[:], cst_d).then_inc(d_cst, 16)

            def copy(out_ap, in_ap, steps, name, scale=1.0):
                nc.scalar.activation(out_ap, in_ap, ACT.Copy, scale=scale).then_inc(steps.sem, steps.step(name))

            act.wait_ge(g0.sem, g0["qkvpad"])
            act.wait_ge(d_front, 16)
            for j, (name, src) in enumerate((("q", ps[:, 0, 0:N]), ("k", ps[:, 0, N:2 * N]), ("v", ps[:, 1, 0:N]))):
                if j == 0:
                    act.wait_ge(t0.sem, t0["v"])
                nc.scalar.activation(qkvp[:, j, 1:1 + H, 1:1 + W], img(src), ACT.Identity, bias=f["bqkv"][:, j:j + 1])\
                    .then_inc(a0.sem, a0.step(name))
            act.wait_ge(g0.sem, g0["stackpad"])
            act.wait_ge(t0.sem, t0["select"])
            for r in (0, 1):
                for s in range(2):
                    shifted_queries(lambda o, i: nc.scalar.activation(o, i, ACT.Copy), r, s)\
                        .then_inc(a0.sem, a0.step(f"s{r}{s}"))
            act.wait_ge(t0.sem, t0["qtok"])
            copy(q_tok[:].rearrange("p (b h c) -> p h b c", b=B, h=NH),
                 ps[:, 1, N:2 * N].rearrange("p (h b c) -> p h b c", h=NH, b=B), a0, "qtok", -HC ** -0.5)
            def tab(i, part):
                return tabv[:, i // 2, part, :, :, (i % 2) * HC:(i % 2 + 1) * HC]
            corner = lambda ap: ap.rearrange("p (k s d) -> p s k d", k=4, s=B * G)
            for i in range(4):
                act.wait_ge(t0.sem, t0[f"table{i}"])
                copy(tab(i, 0), corner(ps[:, TB[i], :]), a0, f"high{i}")
            for i in range(4):
                act.wait_ge(v0.sem, v0[f"rest{i}"])
                copy(tab(i, 1), rest[:, i * BANK:(i + 1) * BANK].rearrange("p (s k d) -> p s k d", s=B * G, k=4),
                     a0, f"mid{i}")
            def index_group(u, i):
                n = u * 9 + i
                act.wait_ge(s_bc, n + 1)
                if i == 0 and u >= 2:
                    act.wait_ge(s_oh, 2 * (u - 1))
                nc.scalar.activation(ixb[:, u % 2, 4 * i:4 * i + 4, :].rearrange("p j n -> p (j n)"),
                                     ps[:, IB[n % 4], :], ACT.Copy).then_inc(s_bce, 1)

            def sample_group(n):
                b, i = n // GRP, n % GRP
                act.wait_ge(s_gp, n + 1)
                if i in (0, 4) and b >= 2:
                    act.wait_ge(s_pv, (b - 2) * NH + 1 + (i > 0))
                nc.scalar.activation(gv[:, b % 2, 8 * i:8 * i + 8, :].rearrange("p s d -> p (s d)"),
                                     ps[:, 2 + n % 4, :], ACT.Copy).then_inc(s_ge, 1)

            def unit_exp(u):
                act.wait_ge(v1.sem, v1[f"peak{u}"])
                at = (u % NH * B + u // NH) * G
                for g in range(G):
                    ins = nc.scalar.activation(pexp[:, g * K2:(g + 1) * K2], logit[:, g * K2:(g + 1) * K2], ACT.Exp,
                                               scale=-1.0, bias=peak[:, g:g + 1], accum_out=psum_[:, at + g:at + g + 1])
                ins.then_inc(s_px, 1)

            for i in range(9):
                index_group(0, i)
            nc.scalar.activation(gate_m[:], gate_m[:], ACT.Exp, scale=-1.0).then_inc(a0.sem, a0.step("sigexp"))
            act.wait_ge(v0.sem, v0["away"])
            nc.scalar.activation(hat1, away, ACT.Abs, bias=neg1[:]).then_inc(a0.sem, a0.step("hat1a"))
            act.wait_ge(a0.sem, a0["hat1a"])
            nc.scalar.activation(hats.rearrange("p (n z) -> p n z", z=2)[:, :, 1], hat1, ACT.Relu,
                                 bias=pos1[:], scale=-1.0).then_inc(a0.sem, a0.step("hat1"))
            done = 0
            for u in range(T):
                for i in range(9):
                    if u + 1 < T:
                        index_group(u + 1, i)
                    while 8 * (done + 1) <= u * J + 4 * i + 4:
                        sample_group(done)
                        done += 1
                    if i == 8 and u == 0:
                        act.wait_ge(vz.sem, vz["zneg"])
                        nc.scalar.activation(soft[:], zsel[:], ACT.Exp, bias=zmax[:], accum_out=zsum[:])\
                            .then_inc(az.sem, az.step("exp"))
                    if i == EXP_AT and u >= 2:
                        unit_exp(u - 2)
            unit_exp(T - 2)
            act.wait_ge(d_moe, 32)
            copy(moe_w1[:], moe[:], aw, "mhi")
            unit_exp(T - 1)
            act.wait_ge(tw.sem, tw["sel"])
            for i, (bank, at, n) in enumerate(SELECTED):
                copy(msel[:, at:at + n], ps[:, bank, 0:n], aw, f"sel{i}")
            copy(bias_hi("m"), moeb[BROWS, :], aw, "mbh")
            act.wait_ge(tw.sem, tw["wd"])
            for r, bank in enumerate(WB):
                at = lambda ap: ap.rearrange("p (g r e) -> p g r e", g=HG, r=4)[:, :, r, :]
                grp = lambda ap: ap.rearrange("p (g e) -> p g e", g=HG)
                copy(at(l3w[:, 2 * DH:]), grp(ps[:, bank, 0:HG * D]), aw, f"wdw{r}")
                copy(at(l3b[BROWS, 2 * DH:]), grp(ps[0:3, bank, HG * D:2 * HG * D]), aw, f"wdb{r}")
            act.wait_ge(d_l3, 32)
            act.wait_ge(aw.sem, aw["wdb3"])
            copy(w1, l3w[:], aw, "lhi")
            act.wait_ge(t2.sem, t2["attT"])
            copy(att_ch, ps[:, 0, 0:N], a2, "attT")
            act.wait_ge(d_late, 32)
            nc.scalar.activation(l3b[BROWS, 0:2 * DH], l3b[BROWS, 0:2 * DH], ACT.Identity, bias=pos1[BROWS, :])\
                .then_inc(aw.sem, aw.step("lb1"))
            act.wait_ge(aw.sem, aw["lb1"])
            copy(bias_hi("l"), l3b[BROWS, :], aw, "lbh")
            act.wait_ge(t2.sem, t2["poolred"])
            nc.scalar.activation(pool_red[:].rearrange("p (b c) -> p b c", b=B), rep(ps[0:4, 2, 0:B], C), ACT.Relu).then_inc(a2.sem, a2.step("poolred"))
            act.wait_ge(v2.sem, v2["kneg"])
            nc.scalar.activation(kexp[:], ps[:, 3, 0:4], ACT.Exp, scale=1.0 / 30.0, bias=kmax[:], accum_out=ksum_[:])\
                .then_inc(a2.sem, a2.step("kexp"))
            act.wait_ge(gw.sem, gw["mres"])
            copy(moe_w2[:], moe[:], aw, "mmid")
            act.wait_ge(gw.sem, gw["mbres"])
            copy(bias_mid("m"), moeb[BROWS, :], aw, "mbm")
            act.wait_ge(gw.sem, gw["lres"])
            copy(w2, l3w[:], aw, "lmid")
            act.wait_ge(gw.sem, gw["lbres"])
            copy(bias_mid("l"), l3b[BROWS, :], aw, "lbm")
            act.wait_ge(t2.sem, t2["conv"])
            act.wait_ge(v2.sem, v2["bshift"])
            nc.scalar.activation(y1, ps[:, 4, 0:N], ACT.Relu, bias=bshift[:], scale=bn_inv[:])\
                .then_inc(a2.sem, a2.step("y1"))
            for n, w in (("m", moe_w2[:]), ("l", w2)):
                act.wait_ge(gw.sem, gw[n + "blow"])
                two = slice(2 * C, 2 * C + 2)
                copy(w[two, :], (biasb[two, 6144 + 264:6144 + 528] if n == "m" else biasb[two, 3 * DH:6 * DH]), aw, n + "w2m")
                act.wait_ge(aw.sem, aw[n + "w2m"])
                one = slice(2 * C, 2 * C + 1)
                copy(w[one, :], (biasb[one, 6144:6144 + 264] if n == "m" else biasb[one, 0:3 * DH]), aw, n + "w2h")

            act.wait_ge(t3.sem, t3["lnT"])
            copy(ln_ch, ps[:, 0, 0:N], a3, "lnT")
            act.wait_ge(t3.sem, t3["qc"])
            copy(qc, ps[:, 1, 0:N], a3, "qc")
            act.wait_ge(t3.sem, t3["vt"])
            copy(vt, ps[:, 3, 0:N], a3, "vt")
            sc = score.rearrange("p (b k) -> p b k", b=B)
            pr = prob.rearrange("p (b k) -> p b k", b=B)
            for b, h in ((b, h) for b in range(B) for h in range(NH)):
                t = h * B + b
                if h == 0:
                    act.wait_ge(v3.sem, v3[f"neg{b}"])
                keys = slice(0, P) if h == 0 else slice(P, 3 * P)
                nc.scalar.activation(pr[:, b, keys], sc[:, b, keys], ACT.Exp, bias=smax[:, t:t + 1],
                                     accum_out=ssum[:, t:t + 1]).then_inc(a3.sem, a3.step(f"exp{t}"))
            for b in (0, 2):
                act.wait_ge(t3.sem, t3[f"pt{b}"])
                copy(prob_t[:, b * 3 * P:(b + 1) * 3 * P], ps[:, b, 0:3 * P], a3, f"pt{b}")

            def middle(v, a, q):
                act.wait_ge(v.sem, v[f"pr{q}"])
                copy(parts_of(q)[:, :, 1, :], tiles4(half_of(lsq, q)), a, f"pm{q}")
                copy(parts_of(q)[:, :, 3, :], parts_of(q)[:, :, 0, :], a, f"pd{q}")

            middle(v4, a4, 0)
            middle(v4, a4, 1)
            act.wait_ge(t4.sem, t4["st0"])
            copy(stack1[:, 0:BANK], stacked_half(0), a4, "s1a")
            copy(stack2[0:2 * C, 0:BANK], stacked_half(0)[0:2 * C, :], a4, "s2a")
            act.wait_ge(v4.sem, v4["rlog1"])
            copy(experts.rearrange("p (t n) -> p t n", t=T - NV), ps[:, NV:, 0:E * C], a4, "experts")
            act.wait_ge(v4.sem, v4["rsub"])
            nc.scalar.activation(rexp[:], rexp[:], ACT.Exp).then_inc(a4.sem, a4.step("rexp"))
            act.wait_ge(g0.sem, g0["sm"])
            copy(stu_w1, msel[:], aw, "shi")

            middle(v5, a5, 0)
            act.wait_ge(t5.sem, t5["st0"])
            copy(stack1[:, 0:BANK], stacked_half(0), a5, "s1a")
            copy(stack2[0:2 * C, 0:BANK], stacked_half(0)[0:2 * C, :], a5, "s2a")
            middle(v5, a5, 1)
            copy(expandb[0:NPART, :], turns["expand"][0:NPART, :], a5, "expand")
            for t in range(T):
                h = t // B
                act.wait_ge(t5.sem, t5[f"k{t}"])
                nc.scalar.activation(fk[:, t * BANK:(t + 1) * BANK], ps[:, 2 * t % 8, :], ACT.Exp, bias=neg1[:])\
                    .then_inc(a5.sem, a5.step(f"ek{t}"))
                act.wait_ge(t5.sem, t5[f"v{t}"])
                copy(vcv[:, t, :, 0:P], ps[:, (2 * t + 1) % 8, :].rearrange("p (g n) -> p g n", g=HG), a5, f"vc{t}",
                     c["cs"][:, 2 * h:2 * h + 1])

            def act_copy(out_ap, in_ap):
                return nc.scalar.activation(out_ap, in_ap, ACT.Copy)

            for i in range(8):
                act.wait_ge(t5.sem, t5[f"q{i}"])
                nc.scalar.activation(fq[:, i * BANK:(i + 1) * BANK], ps[:, i % 4, :], ACT.Exp, bias=neg1[:])\
                    .then_inc(a5.sem, a5.step(f"eq{i}"))
                if i in (1, 5):
                    act.wait_ge(t5.sem, t5[f"kv{i // 2}"])
                    keys_sums(act_copy, i // 2)
                    heads_products(act_copy, i // 2).then_inc(a5.sem, a5.step(f"kv{i // 2}"))
            act.wait_ge(gw.sem, gw["sres"])
            copy(stu_w2, msel[:], aw, "smid")
            for half in range(2):
                act.wait_ge(t5.sem, t5[f"den{half}"])
                copy(den_ch[:, half * BANK:(half + 1) * BANK], ps[0:32, half, :], a5, f"dc{half}")
            for half in range(2):
                act.wait_ge(t5.sem, t5[f"dp{half}"])
                copy(den_parts[0:NPART, half * BANK:(half + 1) * BANK], psb[0][0:NPART, 0:BANK], a5, f"dp{half}")

            middle(v6, a6, 0)
            act.wait_ge(t6.sem, t6["st0"])
            copy(stack1[:, 0:BANK], stacked_half(0), a6, "s1a")
            middle(v6, a6, 1)
            for i, (t, _, _) in enumerate(TILES):
                act.wait_ge(t6.sem, t6[f"v{i}"])
                copy(v_sum.rearrange("p (k t e) -> p k t e", k=NF, t=T)[:, :, t, :],
                     ps[:, 2 * (i % 3), :].rearrange("p (k e) -> p k e", k=NF), a6, f"vp{i}")
                if i == 3:
                    taps, by_parity = small(0)
                    copy(arp[:, :, :, 0, :], taps.rearrange("p (i r n) -> p i r n", i=KU, r=2), a6, "ar0")
                    copy(x5pv[:, :, 0, :], by_parity.rearrange("p (r n) -> p r n", r=2), a6, "x5p0")

        @block.vector
        def _(dve):
            nv = nc.vector

            def layernorm(src, v, pool_step):
                X = tok(src)
                nv.reduce_sum(lsum[:], X, axis=AX.X).then_inc(v.sem, v.step("sum"))
                dve.wait_ge(v.sem, v["sum"])
                nv.scalar_tensor_tensor(out=tok(lcen), in0=rep(lsum[:], C), scalar=-1.0 / C, in1=X,
                                        op0=ALU.mult, op1=ALU.add).then_inc(v.sem, v.step("cen"))
                dve.wait_ge(v.sem, v["cen"])
                nv.tensor_tensor(out=lsq, in0=lcen, in1=lcen, op=ALU.mult).then_inc(v.sem, v.step("sq"))
                dve.wait_ge(v.sem, v["sq"])
                nv.reduce_sum(lvar[:], tok(lsq), axis=AX.X).then_inc(v.sem, v.step("var"))
                dve.wait_ge(v.sem, v["var"])
                nv.tensor_scalar(var_eps[:], lvar[:], 1.0 / C, 1e-5, ALU.mult, ALU.add).then_inc(v.sem, v.step("eps"))
                dve.wait_ge(g0.sem, g0[pool_step])
                nv.tensor_tensor(out=tok(ln[:]), in0=tok(lcen), in1=rep(rstd[:], C), op=ALU.mult)\
                    .then_inc(v.sem, v.step("ln"))

            def less_mean(src, v, q):
                xq = tiles4(half_of(src, q))
                nv.reduce_sum(half_of(lsum[:], q), xq, axis=AX.X).then_inc(v.sem, v.step(f"sum{q}"))
                dve.wait_ge(v.sem, v[f"sum{q}"])
                nv.scalar_tensor_tensor(out=tiles4(half_of(lcen, q)), in0=rep(half_of(lsum[:], q), C), scalar=-1.0 / C,
                                        in1=xq, op0=ALU.mult, op1=ALU.add).then_inc(v.sem, v.step(f"cen{q}"))

            def variance(v, q):
                cen, sq = half_of(lcen, q), half_of(lsq, q)
                dve.wait_ge(v.sem, v[f"cen{q}"])
                nv.tensor_tensor(out=sq, in0=cen, in1=cen, op=ALU.mult).then_inc(v.sem, v.step(f"sq{q}"))
                dve.wait_ge(v.sem, v[f"sq{q}"])
                nv.reduce_sum(half_of(lvar[:], q), tiles4(sq), axis=AX.X).then_inc(v.sem, v.step(f"var{q}"))
                dve.wait_ge(v.sem, v[f"var{q}"])
                nv.tensor_scalar(half_of(var_eps[:], q), half_of(lvar[:], q), 1.0 / C, 1e-5, ALU.mult, ALU.add)\
                    .then_inc(v.sem, v.step(f"eps{q}"))

            def normalised(v, q, power_step):
                lnq = tiles4(half_of(ln[:], q))
                dve.wait_ge(g0.sem, g0[f"{power_step}{q}"])
                nv.tensor_tensor(out=lnq, in0=tiles4(half_of(lcen, q)), in1=rep(half_of(rstd[:], q), C), op=ALU.mult)\
                    .then_inc(v.sem, v.step(f"ln{q}"))
                dve.wait_ge(v.sem, v[f"ln{q}"])
                nv.tensor_copy(parts_of(q)[:, :, 0, :], lnq).then_inc(v.sem, v.step(f"ph{q}"))
                dve.wait_ge(v.sem, v[f"ph{q}"])
                nv.tensor_tensor(out=tiles4(half_of(lsq, q)), in0=lnq, in1=parts_of(q)[:, :, 0, :], op=ALU.subtract)\
                    .then_inc(v.sem, v.step(f"pr{q}"))

            def low(v, a, q):
                dve.wait_ge(a.sem, a[f"pm{q}"])
                nv.tensor_tensor(out=parts_of(q)[:, :, 2, :], in0=tiles4(half_of(lsq, q)), in1=parts_of(q)[:, :, 1, :],
                                 op=ALU.subtract).then_inc(v.sem, v.step(f"pl{q}"))

            def moments_of(src, v):
                nv.bn_stats(stats[:], src).then_inc(v.sem, v.step("stats"))
                dve.wait_ge(v.sem, v["stats"])
                nv.bn_aggr(moments[:], stats[:]).then_inc(v.sem, v.step("moments"))
                dve.wait_ge(v.sem, v["moments"])
                nv.tensor_scalar(var_eps[:, 0:1], moments[:, 1:2], 1e-5, None, ALU.add).then_inc(v.sem, v.step("eps"))

            dve.wait_ge(d_cst, 16)
            nv.tensor_copy(identb[:], ident).then_inc(v0.sem, v0.step("identb"))
            nv.memset(neg1[:], -1.0).then_inc(v0.sem, v0.step("neg1"))
            nv.memset(pos1[:], 1.0).then_inc(v0.sem, v0.step("pos1"))
            nv.tensor_tensor(out=base[:].rearrange("p (h n) -> p h n", h=NH),
                             in0=c["base"].rearrange("p (h n) -> p h n", h=NH),
                             in1=c["boff"][:, 0:2 * J].unsqueeze(1).broadcast_to([P, NH, 2 * J]), op=ALU.add)\
                .then_inc(v0.sem, v0.step("base"))
            dve.wait_ge(d_x, 16)
            moments_of(x[:], v0)
            dve.wait_ge(g0.sem, g0["rstd0"])
            nv.tensor_scalar(xg[:], x[:], moments[:, 0:1], rstd[:, 0:1], ALU.subtract, ALU.mult)\
                .then_inc(v0.sem, v0.step("xg"))

            dve.wait_ge(d_front, 16)
            dve.wait_ge(t0.sem, t0["comp"])
            cb = comp_bd.rearrange("p (s b n) -> p s b n", s=3, b=B)
            for i, (at, n, mask) in enumerate(((0, 2, f["bmask8"]), (2, 1, c["bmask"]))):
                nv.tensor_tensor(out=cb[:, at:at + n],
                                 in0=ps[:, 6, at * NOFF:(at + n) * NOFF].rearrange("p (s n) -> p s n", s=n)
                                 .unsqueeze(2).broadcast_to([P, n, B, NOFF]),
                                 in1=rep(mask, NOFF).unsqueeze(1).broadcast_to([P, n, B, NOFF]), op=ALU.mult)\
                    .then_inc(v0.sem, v0.step(f"comp{i}"))
            def tap_step(j, t, dst, name):
                win = qkvp[:, j, t // 3:t // 3 + H, t % 3:t % 3 + W]
                w = f["wdw"][:, j * K2 + t:j * K2 + t + 1]
                if t == 0:
                    nv.tensor_scalar(dst, win, w, f["bdw"][:, j:j + 1], ALU.mult, ALU.add)\
                        .then_inc(v0.sem, v0.step(name))
                else:
                    nv.scalar_tensor_tensor(out=dst, in0=win, scalar=w, in1=dst, op0=ALU.mult, op1=ALU.add)\
                        .then_inc(v0.sem, v0.step(name))

            q_in = img(q_mid)
            dve.wait_ge(g0.sem, g0["kvpad"])
            dve.wait_ge(a0.sem, a0["q"])
            for t in range(K2):
                if t:
                    dve.wait_ge(v0.sem, v0[f"q{t - 1}"])
                tap_step(0, t, q_in, f"q{t}")
            dve.wait_ge(t0.sem, t0["select"])
            for r in (2, 3):
                for s in range(2):
                    shifted_queries(nv.tensor_copy, r, s).then_inc(v0.sem, v0.step(f"s{r}{s}"))
            dve.wait_ge(a0.sem, a0["v"])
            for t in range(K2):
                for j, nm in ((1, "k"), (2, "v")):
                    if t:
                        dve.wait_ge(v0.sem, v0[f"{nm}{t - 1}"])
                    tap_step(j, t, img(kvv[:, j - 1, 0:N]), f"{nm}{t}")

            dve.wait_ge(t0.sem, t0["offsets"])
            off = ps[:, 2:2 + NH, 0:B * NOFF].rearrange("p h (b n) -> p h b n", b=B)
            hbn = lambda ap: ap.rearrange("p (b h n) -> p h b n", b=B, h=NH)
            nv.tensor_tensor(out=hbn(pos), in0=off[:, :, :, 0:2 * J],
                             in1=base[:].rearrange("p (h n) -> p h n", h=NH).unsqueeze(2).broadcast_to([P, NH, B, 2 * J]),
                             op=ALU.add).then_inc(v0.sem, v0.step("pos"))
            nv.tensor_tensor(out=hbn(gate_m[:]), in0=off[:, :, :, 2 * J:],
                             in1=c["boff"][:, 2 * J:].unsqueeze(1).unsqueeze(1).broadcast_to([P, NH, B, K2]), op=ALU.add)\
                .then_inc(v0.sem, v0.step("gate"))
            dve.wait_ge(v0.sem, v0["pos"])
            nv.tensor_scalar(pos, pos, -2.0, H + 1.0, ALU.max, ALU.min).then_inc(v0.sem, v0.step("clamp"))
            dve.wait_ge(v0.sem, v0["clamp"])
            nv.tensor_scalar(near, pos, -0.5, ROUND, ALU.add, ALU.add).then_inc(v0.sem, v0.step("near0"))
            dve.wait_ge(v0.sem, v0["near0"])
            nv.tensor_scalar(near, near, -ROUND, 0.0, ALU.add, ALU.max).then_inc(v0.sem, v0.step("near1"))
            dve.wait_ge(v0.sem, v0["near1"])
            nv.tensor_scalar(near, near, H - 2.0, None, ALU.min).then_inc(v0.sem, v0.step("near"))
            dve.wait_ge(v0.sem, v0["near"])
            yx = near.rearrange("p (n a) -> p n a", a=2)
            nv.scalar_tensor_tensor(out=index[:], in0=yx[:, :, 0], scalar=float(W), in1=yx[:, :, 1],
                                    op0=ALU.mult, op1=ALU.add).then_inc(v0.sem, v0.step("index"))
            rst = lambda i: rest[:, i * BANK:(i + 1) * BANK].rearrange("p (s k d) -> p s k d", s=B * G, k=4)
            tab = lambda i, part: tabv[:, i // 2, part, :, :, (i % 2) * HC:(i % 2 + 1) * HC]
            for i in range(4):
                dve.wait_ge(a0.sem, a0[f"high{i}"])
                nv.tensor_tensor(out=rst(i), in0=ps[:, TB[i], :].rearrange("p (k s d) -> p s k d", k=4, s=B * G),
                                 in1=tab(i, 0), op=ALU.subtract).then_inc(v0.sem, v0.step(f"rest{i}"))
            for i in range(4):
                dve.wait_ge(a0.sem, a0[f"mid{i}"])
                nv.tensor_tensor(out=tab(i, 2), in0=rst(i), in1=tab(i, 1), op=ALU.subtract)\
                    .then_inc(v0.sem, v0.step(f"low{i}"))
            def one_hots(u, half):
                js = slice(half * J // 2, (half + 1) * J // 2)
                dve.wait_ge(s_bce, 9 * u + (5 if half == 0 else 9))
                if u >= 2 and half == 0:
                    dve.wait_ge(s_un, u - 1)
                for q in range(2):
                    ins = nv.tensor_scalar(ohv[:, u % 2, q, js, :], ixb[:, u % 2, js, :], c["pidx"][:, q:q + 1],
                                           None, ALU.is_equal)
                ins.then_inc(s_oh, 1)

            def weights(u):
                dve.wait_ge(s_px, u + 1)
                nv.tensor_tensor(out=w4p[:].rearrange("p (n k) -> p n k", k=4),
                                 in0=w4[:, u * J * 4:(u + 1) * J * 4].rearrange("p (n k) -> p n k", k=4),
                                 in1=rep(pexp[:], 4), op=ALU.mult).then_inc(v1.sem, v1.step(f"w4p{u}"))

            def logits(u):
                if u >= POOL_K:
                    dve.wait_ge(s_ge, groups(u))
                    keys_product(nv, u).then_inc(s_pk, 1)
                dve.wait_ge(s_pk, u + 1)
                nv.reduce_sum(dots[:], prod_k.rearrange("p (n d) -> p n d", d=HC), axis=AX.X)\
                    .then_inc(v1.sem, v1.step(f"dots{u}"))
                dve.wait_ge(v1.sem, v1[f"dots{u}"])
                nv.tensor_tensor(out=dots[:], in0=dots[:], in1=w4[:, u * J * 4:(u + 1) * J * 4], op=ALU.mult)\
                    .then_inc(v1.sem, v1.step(f"wdots{u}"))
                dve.wait_ge(v1.sem, v1[f"wdots{u}"])
                nv.reduce_sum(logit[:], dots[:].rearrange("p (n k) -> p n k", k=4), axis=AX.X)\
                    .then_inc(v1.sem, v1.step(f"logit{u}"))
                dve.wait_ge(v1.sem, v1[f"logit{u}"])
                nv.tensor_reduce(peak[:], logit[:].rearrange("p (s k) -> p s k", k=K2), AX.X, ALU.min)\
                    .then_inc(v1.sem, v1.step(f"peak{u}"))

            def attended(u):
                if u >= POOL_V:
                    dve.wait_ge(v1.sem, v1[f"w4p{u}"])
                    values_product(nv, u).then_inc(s_pv, 1)
                dve.wait_ge(s_pv, u + 1)
                b, h = u // NH, u % NH
                nv.reduce_sum(tokhb(att[:])[:, h, b, :], prod_v.rearrange("p (n k) -> p n k", k=4 * K2), axis=AX.X)\
                    .then_inc(v1.sem, v1.step(f"mixed{u}"))

            def attention(u):
                if 4 <= u <= T:
                    attended(u - 4)
                if u >= 3:
                    weights(u - 3)
                if 2 <= u < T + 2:
                    logits(u - 2)
                if u >= T:
                    attended(u - 3)

            for u in range(T):
                one_hots(u, 0)
                one_hots(u, 1)
                if u == 0:
                    nv.tensor_tensor(out=away, in0=pos, in1=near, op=ALU.subtract).then_inc(v0.sem, v0.step("away"))
                    dve.wait_ge(v0.sem, v0["away"])
                    nv.scalar_tensor_tensor(out=hat0, in0=away, scalar=-1.0, in1=away, op0=ALU.mult, op1=ALU.min).then_inc(v0.sem, v0.step("hat0a"))
                    dve.wait_ge(v0.sem, v0["hat0a"])
                    nv.tensor_scalar(hats.rearrange("p (n z) -> p n z", z=2)[:, :, 0], hat0, 1.0, 0.0, ALU.add, ALU.max)\
                        .then_inc(v0.sem, v0.step("hat0"))
                    dve.wait_ge(a0.sem, a0["sigexp"])
                    nv.tensor_scalar(gate_m[:], gate_m[:], 1.0, None, ALU.add).then_inc(v0.sem, v0.step("gate1"))
                    dve.wait_ge(v0.sem, v0["gate1"])
                    nv.reciprocal(gate_m[:], gate_m[:]).then_inc(v0.sem, v0.step("sigmoid"))
                    dve.wait_ge(v0.sem, v0["sigmoid"])
                    nv.tensor_copy(mask_x[:].rearrange("p (t g k) -> p t g k", t=T, g=G),
                                   gate_m[:].rearrange("p (t k) -> p t k", t=T).unsqueeze(2).broadcast_to([P, T, G, K2]))\
                        .then_inc(v0.sem, v0.step("maskx"))
                    dve.wait_ge(v0.sem, v0["maskx"])
                    dve.wait_ge(a0.sem, a0["hat1"])
                    hv = hats.rearrange("p (n a z) -> p n a z", a=2, z=2)
                    nv.tensor_tensor(out=hv[:, :, 0, :], in0=hv[:, :, 0, :], in1=rep(mask_x[:], 2), op=ALU.mult)\
                        .then_inc(v0.sem, v0.step("hatm"))
                    dve.wait_ge(v0.sem, v0["hatm"])
                    nv.tensor_tensor(out=w4[:].rearrange("p (n y z) -> p n y z", y=2, z=2), in0=rep(hv[:, :, 0, :], 2),
                                     in1=hv[:, :, 1, :].unsqueeze(2).broadcast_to([P, T * J, 2, 2]), op=ALU.mult)\
                        .then_inc(v0.sem, v0.step("w4"))

                    nv.tensor_tensor(out=zsel[:], in0=c["logw"], in1=c["gumbel"], op=ALU.add).then_inc(vz.sem, vz.step("z"))
                    dve.wait_ge(vz.sem, vz["z"])
                    nv.reduce_max(zmax[:], zsel[:], axis=AX.X).then_inc(vz.sem, vz.step("zmax"))
                    dve.wait_ge(vz.sem, vz["zmax"])
                    nv.tensor_scalar(zmax[:], zmax[:], -1.0, None, ALU.mult).then_inc(vz.sem, vz.step("zneg"))

                if u == 1:
                    dve.wait_ge(az.sem, az["exp"])
                    nv.reciprocal(zsum[:], zsum[:]).then_inc(vz.sem, vz.step("zinv"))
                    dve.wait_ge(vz.sem, vz["zinv"])
                    nv.tensor_scalar(soft[:], soft[:], zsum[:], None, ALU.mult).then_inc(vz.sem, vz.step("soft"))
                    dve.wait_ge(vz.sem, vz["soft"])
                    sj = soft[:].unsqueeze(1).broadcast_to([P, NSC, NSC])
                    z44 = lambda ap: ap.rearrange("p (i j) -> p i j", i=NSC)
                    nv.tensor_tensor(out=z44(zgt[:]), in0=sj, in1=rep(soft[:], NSC), op=ALU.is_gt)\
                        .then_inc(vz.sem, vz.step("zgt"))
                    nv.tensor_tensor(out=z44(zeq[:]), in0=sj, in1=rep(soft[:], NSC), op=ALU.is_equal)\
                        .then_inc(vz.sem, vz.step("zeq"))
                    dve.wait_ge(vz.sem, vz["zeq"])
                    nv.tensor_tensor(out=zeq[:], in0=zeq[:], in1=c["lt4"], op=ALU.mult).then_inc(vz.sem, vz.step("zeqlt"))
                    dve.wait_ge(vz.sem, vz["zeqlt"])
                    nv.tensor_tensor(out=zgt[:], in0=zgt[:], in1=zeq[:], op=ALU.add).then_inc(vz.sem, vz.step("zadd"))
                    dve.wait_ge(vz.sem, vz["zadd"])
                    nv.reduce_sum(hard[:], z44(zgt[:]), axis=AX.X).then_inc(vz.sem, vz.step("rank"))
                    dve.wait_ge(vz.sem, vz["rank"])
                    nv.tensor_scalar(hard[:], hard[:], 0.0, None, ALU.is_equal).then_inc(vz.sem, vz.step("hard"))
                    dve.wait_ge(vz.sem, vz["hard"])
                    nv.tensor_tensor(out=wsel[:], in0=hard[:], in1=soft[:], op=ALU.subtract).then_inc(vz.sem, vz.step("diff"))
                    dve.wait_ge(vz.sem, vz["diff"])
                    nv.tensor_tensor(out=wsel[:], in0=wsel[:], in1=soft[:], op=ALU.add).then_inc(vz.sem, vz.step("w"))
                    nv.tensor_tensor(out=hard[:], in0=hard[:], in1=c["frac"], op=ALU.mult).then_inc(vz.sem, vz.step("lenp"))
                    dve.wait_ge(vz.sem, vz["lenp"])
                    nv.reduce_sum(length[:], hard[:], axis=AX.X).then_inc(vz.sem, vz.step("length"))
                    dve.wait_ge(vz.sem, vz["length"])
                    nv.tensor_scalar(window[:], c["tokidx"], length[:], None, ALU.is_lt).then_inc(vz.sem, vz.step("win"))
                    nv.tensor_tensor(out=wscale[:], in0=wsel[:], in1=c["bmask"], op=ALU.mult).then_inc(vz.sem, vz.step("wrow"))
                    dve.wait_ge(vz.sem, vz["wrow"])
                    nv.reduce_sum(wcol[:], wscale[:], axis=AX.X).then_inc(vz.sem, vz.step("wcol"))
                    dve.wait_ge(vz.sem, vz["wcol"])
                    nv.tensor_scalar(wpick[:].rearrange("p (r e) -> p r e", r=4),
                                     c["fold"].unsqueeze(1).broadcast_to([P, 4, C]), wcol[:], None, ALU.mult)\
                        .then_inc(vz.sem, vz.step("wpick"))
                    dve.wait_ge(vz.sem, vz["wpick"])
                    nv.tensor_scalar(nwpick[:], wpick[:], -1.0, None, ALU.mult).then_inc(vz.sem, vz.step("nwpick"))
                attention(u)
            for u in range(T, T + 3):
                attention(u)
            nv.reciprocal(pinv[:], psum_[:]).then_inc(v1.sem, v1.step("inv"))
            dve.wait_ge(v1.sem, v1["inv"])
            nv.tensor_tensor(out=att[:].rearrange("p (n d) -> p n d", d=HC), in0=att[:].rearrange("p (n d) -> p n d", d=HC),
                             in1=rep(pinv[:], HC), op=ALU.mult).then_inc(v1.sem, v1.step("att"))

            dve.wait_ge(t2.sem, t2["proj"])
            nv.scalar_tensor_tensor(out=x1[:], in0=ps[:, 1, 0:N], scalar=p1["bproj"], in1=x[:], op0=ALU.add, op1=ALU.add)\
                .then_inc(v2.sem, v2.step("x1"))
            dve.wait_ge(v2.sem, v2["x1"])
            moments_of(x1[:], v2)
            dve.wait_ge(g0.sem, g0["rstd1"])
            nv.tensor_scalar(xp[:, 1:1 + H, 1:1 + W], img(x1[:]), moments[:, 0:1], rstd[:, 0:1], ALU.subtract, ALU.mult)\
                .then_inc(v2.sem, v2.step("xpad"))
            dve.wait_ge(v2.sem, v2["xpad"])
            nv.tensor_reduce(pool[:], xp[:, 1:1 + H, 1:1 + W], AX.XY, ALU.add).then_inc(v2.sem, v2.step("pool"))
            dve.wait_ge(v2.sem, v2["pool"])
            nv.tensor_scalar(pool_bd[:], c["bmask"], pool[:], 1.0 / N, ALU.mult, ALU.mult).then_inc(v2.sem, v2.step("poolbd"))
            dve.wait_ge(t2.sem, t2["katt"])
            nv.reduce_max(kmax[:], ps[:, 3, 0:4], axis=AX.X).then_inc(v2.sem, v2.step("kmax"))
            dve.wait_ge(v2.sem, v2["kmax"])
            nv.tensor_scalar(kmax[:], kmax[:], -1.0 / 30.0, None, ALU.mult).then_inc(v2.sem, v2.step("kneg"))
            dve.wait_ge(a2.sem, a2["kexp"])
            nv.reciprocal(kinv[:], ksum_[:]).then_inc(v2.sem, v2.step("kinv"))
            dve.wait_ge(v2.sem, v2["kinv"])
            nv.tensor_scalar(katt[:], kexp[:], kinv[:], None, ALU.mult).then_inc(v2.sem, v2.step("katt"))
            for k in range(4):
                ck = p1["convk"][:, k * K2 * C:(k + 1) * K2 * C]
                if k == 0:
                    dve.wait_ge(v2.sem, v2["katt"])
                    nv.tensor_scalar(wmix, ck, katt[:, 0:1], None, ALU.mult).then_inc(v2.sem, v2.step("mix0"))
                else:
                    dve.wait_ge(v2.sem, v2[f"mix{k - 1}"])
                    nv.scalar_tensor_tensor(out=wmix, in0=ck, scalar=katt[:, k:k + 1], in1=wmix,
                                            op0=ALU.mult, op1=ALU.add).then_inc(v2.sem, v2.step(f"mix{k}"))
            dve.wait_ge(v2.sem, v2["mix3"])
            for i in range(3):
                taps = slice(3 * i, 3 * i + 3)
                nv.tensor_tensor(out=wmix_bd.rearrange("p (t b o) -> p t b o", t=K2, b=B)[:, taps],
                                 in0=wmix.rearrange("p (t o) -> p t o", t=K2)[:, taps].unsqueeze(2)
                                 .broadcast_to([P, 3, B, C]),
                                 in1=rep(c["bmask"].unsqueeze(1).broadcast_to([P, 3, B]), C), op=ALU.mult)\
                    .then_inc(v2.sem, v2.step(f"mixbd{i}"))
            nv.tensor_tensor(out=bmix[:], in0=katt[:], in1=p1["kbias"], op=ALU.mult).then_inc(v2.sem, v2.step("bmix"))
            dve.wait_ge(v2.sem, v2["bmix"])
            nv.reduce_sum(bsum[:], bmix[:], axis=AX.X).then_inc(v2.sem, v2.step("bsum"))
            dve.wait_ge(g0.sem, g0["bninv"])
            dve.wait_ge(v2.sem, v2["bsum"])
            nv.tensor_scalar(bn_inv[:], bn_inv[:], p1["bnscale"], None, ALU.mult).then_inc(v2.sem, v2.step("binv"))
            dve.wait_ge(v2.sem, v2["binv"])
            nv.tensor_scalar(bshift[:], bsum[:], p1["bnmean"], bn_inv[:], ALU.subtract, ALU.mult)\
                .then_inc(v2.sem, v2.step("bcent"))
            dve.wait_ge(v2.sem, v2["bcent"])
            nv.tensor_tensor(out=bshift[:], in0=bshift[:], in1=p1["bnbias"], op=ALU.add).then_inc(v2.sem, v2.step("bshift"))
            dve.wait_ge(a2.sem, a2["y1"])
            nv.tensor_tensor(out=x2, in0=x1[:], in1=y1, op=ALU.add).then_inc(v2.sem, v2.step("x2"))
            dve.wait_ge(t2.sem, t2["x2T"])
            nv.tensor_copy(x2t[:], ps[:, 5, 0:N]).then_inc(v2.sem, v2.step("x2t"))
            dve.wait_ge(v2.sem, v2["x2t"])

            layernorm(x2t[:], v3, "rstd2")
            dve.wait_ge(t3.sem, t3["kc"])
            nv.tensor_copy(kc, ps[:, 2, 0:N]).then_inc(v3.sem, v3.step("kc"))
            sc = score.rearrange("p (b k) -> p b k", b=B)
            sx = smax[:].rearrange("p (h b) -> p h b", h=NH)
            dve.wait_ge(d_l2, 16)
            for b in range(B + 1):
                if b < B:
                    dve.wait_ge(t3.sem, t3[f"score{b}"])
                    nv.scalar_tensor_tensor(out=sc[:, b], in0=ps[:, 4 + b, 0:3 * P], scalar=float(N) ** -0.5,
                                            in1=p2["causal"], op0=ALU.mult, op1=ALU.add)\
                        .then_inc(v3.sem, v3.step(f"score{b}"))
                if b:
                    dve.wait_ge(v3.sem, v3[f"score{b - 1}"])
                    nv.reduce_max(sx[:, 0, b - 1:b], sc[:, b - 1, 0:P], axis=AX.X).then_inc(v3.sem, v3.step(f"first{b - 1}"))
                    nv.reduce_max(sx[:, 1, b - 1:b], sc[:, b - 1, P:], axis=AX.X).then_inc(v3.sem, v3.step(f"second{b - 1}"))
                    dve.wait_ge(v3.sem, v3[f"second{b - 1}"])
                    nv.tensor_scalar(sx[:, :, b - 1], sx[:, :, b - 1], -1.0, None, ALU.mult)\
                        .then_inc(v3.sem, v3.step(f"neg{b - 1}"))
            dve.wait_ge(a3.sem, a3[f"exp{T - 1}"])
            nv.reciprocal(sinv[:], ssum[:]).then_inc(v3.sem, v3.step("sinv"))
            for b in (1, 3):
                dve.wait_ge(t3.sem, t3[f"pt{b}"])
                nv.tensor_copy(prob_t[:, b * 3 * P:(b + 1) * 3 * P], ps[:, b, 0:3 * P])\
                    .then_inc(v3.sem, v3.step(f"pt{b}"))
            dve.wait_ge(t3.sem, t3["pv"])
            nv.tensor_tensor(out=tok(ctx_n), in0=tok(ps[:, 4, 0:N]), in1=rep(sinv[:], C), op=ALU.mult)\
                .then_inc(v3.sem, v3.step("ctx"))
            dve.wait_ge(v3.sem, v3["ctx"])
            nv.tensor_tensor(out=x3t, in0=x2t[:], in1=ctx_n, op=ALU.add).then_inc(v3.sem, v3.step("x3"))
            dve.wait_ge(v3.sem, v3["x3"])

            less_mean(x3t, v4, 0)
            variance(v4, 0)
            less_mean(x3t, v4, 1)
            variance(v4, 1)
            normalised(v4, 0, "rstd3")
            low(v4, a4, 0)
            normalised(v4, 1, "rstd3")
            low(v4, a4, 1)
            dve.wait_ge(t4.sem, t4["st1"])
            nv.tensor_copy(stack1[:, BANK:], stacked_half(1)).then_inc(v4.sem, v4.step("s1b"))
            nv.tensor_copy(stack2[0:2 * C, BANK:], stacked_half(1)[0:2 * C, :]).then_inc(v4.sem, v4.step("s2b"))
            te = lambda ap: ap.rearrange("p (t e) -> p t e", e=E)
            tee = lambda ap: ap.rearrange("p (t i j) -> p t i j", i=E, j=E)

            def ranked(q):
                logits, gt, eq = half_of(rlog[:], q), half_of(rgt, q), half_of(req, q)
                dve.wait_ge(t4.sem, t4[f"experts{q}"])
                nv.tensor_copy(te(logits), ps[:, 4 * q:4 * (q + 1), E * C:E * C + E]).then_inc(v4.sem, v4.step(f"rlog{q}"))
                dve.wait_ge(v4.sem, v4[f"rlog{q}"])
                lj, li = te(logits).unsqueeze(2).broadcast_to([P, T // 2, E, E]), rep(te(logits), E)
                nv.tensor_tensor(out=tee(gt), in0=lj, in1=li, op=ALU.is_gt).then_inc(v4.sem, v4.step(f"rgt{q}"))
                nv.tensor_tensor(out=tee(eq), in0=lj, in1=li, op=ALU.is_equal).then_inc(v4.sem, v4.step(f"req{q}"))
                dve.wait_ge(v4.sem, v4[f"req{q}"])
                eq3 = eq.rearrange("p (t n) -> p t n", t=T // 2)
                nv.tensor_tensor(out=eq3, in0=eq3, in1=c["lt8"].unsqueeze(1).broadcast_to([P, T // 2, E * E]), op=ALU.mult)\
                    .then_inc(v4.sem, v4.step(f"reqlt{q}"))
                dve.wait_ge(v4.sem, v4[f"reqlt{q}"])
                nv.tensor_tensor(out=gt, in0=gt, in1=eq, op=ALU.add).then_inc(v4.sem, v4.step(f"rsum{q}"))
                dve.wait_ge(v4.sem, v4[f"rsum{q}"])
                nv.reduce_sum(half_of(rank[:], q), gt.rearrange("p (n j) -> p n j", j=E), axis=AX.X)\
                    .then_inc(v4.sem, v4.step(f"rank{q}"))

            ranked(0)
            ranked(1)
            nv.reduce_max(rmax[:], te(rlog[:]), axis=AX.X).then_inc(v4.sem, v4.step("rmax"))
            dve.wait_ge(v4.sem, v4["rmax"])
            nv.tensor_tensor(out=te(rexp[:]), in0=te(rlog[:]), in1=rep(rmax[:], E), op=ALU.subtract)\
                .then_inc(v4.sem, v4.step("rsub"))
            nv.tensor_scalar(chosen[:], rank[:], 2.0, None, ALU.is_lt).then_inc(v4.sem, v4.step("chosen"))
            dve.wait_ge(v4.sem, v4["chosen"])
            dve.wait_ge(a4.sem, a4["rexp"])
            nv.tensor_tensor(out=chosen[:], in0=chosen[:], in1=rexp[:], op=ALU.mult).then_inc(v4.sem, v4.step("esel"))
            dve.wait_ge(v4.sem, v4["esel"])
            nv.reduce_sum(rsum[:], te(chosen[:]), axis=AX.X).then_inc(v4.sem, v4.step("esum"))
            dve.wait_ge(v4.sem, v4["esum"])
            nv.reciprocal(rsum[:], rsum[:]).then_inc(v4.sem, v4.step("einv"))
            dve.wait_ge(v4.sem, v4["einv"])
            nv.tensor_tensor(out=tce(gated[:, 0:NV * E * C]),
                             in0=ps[:, 0:NV, 0:E * C].rearrange("p t (e c) -> p t c e", e=E),
                             in1=te(chosen[:])[:, 0:NV].unsqueeze(2).broadcast_to([P, NV, C, E]), op=ALU.mult)\
                .then_inc(v4.sem, v4.step("gated"))
            def experts_sum(q):
                y = half_of(lsq, q)
                dve.wait_ge(v4.sem, v4["gated"])
                if q:
                    dve.wait_ge(g0.sem, g0["gated"])
                nv.reduce_sum(y, half_of(gated, q).rearrange("p (n e) -> p n e", e=E), axis=AX.X).then_inc(v4.sem, v4.step(f"y{q}"))
                dve.wait_ge(v4.sem, v4[f"y{q}"])
                nv.tensor_tensor(out=tiles4(y), in0=tiles4(y), in1=rep(half_of(rsum[:], q), C), op=ALU.mult)\
                    .then_inc(v4.sem, v4.step(f"ynorm{q}"))
                dve.wait_ge(v4.sem, v4[f"ynorm{q}"])
                nv.tensor_tensor(out=half_of(x4t, q), in0=half_of(x3t, q), in1=y, op=ALU.add).then_inc(v4.sem, v4.step(f"x4{q}"))
                dve.wait_ge(v4.sem, v4[f"x4{q}"])

            experts_sum(0)
            less_mean(x4t, v5, 0)
            variance(v5, 0)
            experts_sum(1)
            normalised(v5, 0, "rstd4")
            less_mean(x4t, v5, 1)
            low(v5, a5, 0)
            variance(v5, 1)
            for h in range(NH):
                nv.tensor_copy(vcs.rearrange("p (h n k) -> p h n k", h=NH, k=HCOLS)[:, h, :, 2 * P:],
                               c["cs"][:, 2 * h:2 * h + 2].unsqueeze(1).broadcast_to([P, B * HG, 2]))\
                    .then_inc(v5.sem, v5.step(f"cs{h}"))
            normalised(v5, 1, "rstd4")
            low(v5, a5, 1)
            dve.wait_ge(t5.sem, t5["st1"])
            nv.tensor_copy(stack1[:, BANK:], stacked_half(1)).then_inc(v5.sem, v5.step("s1b"))
            nv.tensor_copy(stack2[0:2 * C, BANK:], stacked_half(1)[0:2 * C, :]).then_inc(v5.sem, v5.step("s2b"))

            for t in range(T):
                h = t // B
                blk = slice(t * BANK, (t + 1) * BANK)
                dve.wait_ge(a5.sem, a5[f"ek{t}"])
                nv.scalar_tensor_tensor(out=fk[:, blk], in0=fk[:, blk], scalar=1.0, in1=ps[:, 2 * t % 8, :],
                                        op0=ALU.min, op1=ALU.max).then_inc(v5.sem, v5.step(f"fk{t}"))
                dve.wait_ge(a5.sem, a5[f"vc{t}"])
                nv.tensor_scalar(vcv[:, t, :, P:2 * P], ps[:, (2 * t + 1) % 8, :].rearrange("p (g n) -> p g n", g=HG),
                                 c["cs"][:, 2 * h + 1:2 * h + 2], None, ALU.mult).then_inc(v5.sem, v5.step(f"vs{t}"))
            for i in range(8):
                blk = slice(i * BANK, (i + 1) * BANK)
                dve.wait_ge(a5.sem, a5[f"eq{i}"])
                nv.scalar_tensor_tensor(out=fq[:, blk], in0=fq[:, blk], scalar=1.0, in1=ps[:, i % 4, :],
                                        op0=ALU.min, op1=ALU.max).then_inc(v5.sem, v5.step(f"fq{i}"))
                if i in (3, 7):
                    dve.wait_ge(t5.sem, t5[f"kv{i // 2}"])
                    keys_sums(nv.tensor_copy, i // 2).then_inc(v5.sem, v5.step(f"ks{i // 2}"))
                if i == 3:
                    heads_products(nv.tensor_copy, 1).then_inc(v5.sem, v5.step("kv1"))
            dve.wait_ge(v5.sem, v5["ks3"])
            dve.wait_ge(a5.sem, a5["kv2"])
            nv.tensor_tensor(out=ks_bd.rearrange("p (g n h) -> p g n h", g=HG, h=NHEAD),
                             in0=rep(ks_sb[:].rearrange("p (g n) -> p g n", g=HG), NHEAD),
                             in1=c["headsel"].rearrange("p (g h) -> p g h", g=HG).unsqueeze(2)
                             .broadcast_to([P, HG, 2 * B, NHEAD]), op=ALU.mult).then_inc(v5.sem, v5.step("ksb"))
            heads_products(nv.tensor_copy, 3).then_inc(v5.sem, v5.step("kv3"))
            nv.tensor_tensor(out=x4d.rearrange("p (b h c) -> p h b c", b=B, h=NH), in0=tokhb(x4t),
                             in1=p3["denseb"].unsqueeze(1).unsqueeze(1).broadcast_to([P, NH, B, D]),
                             op=ALU.add).then_inc(v5.sem, v5.step("bias"))
            for half in range(2):
                dv = den[:, half * 4 * NHEAD:(half + 1) * 4 * NHEAD].rearrange("p (t n) -> p t n", t=4)
                dn = dv.rearrange("p (b h) n -> p b h n", h=NH)
                dp = den_p[:, half * 4 * NPART:(half + 1) * 4 * NPART].rearrange("p (t r n) -> p t r n", t=4, r=3)
                dt = ps[:, DB[half], 0:4 * 2 * NHEAD].rearrange("p (b h s n) -> p b h s n", b=2, h=NH, s=2)
                dve.wait_ge(t5.sem, t5[f"denT{half}"])
                for h in range(NH):
                    nv.tensor_scalar(dn[:, :, h, :], dt[:, :, h, 0, :], c["cs"][:, 2 * h:2 * h + 1], 1e-5, ALU.mult, ALU.add)\
                        .then_inc(v5.sem, v5.step(f"cos{half}{h}"))
                for h in range(NH):
                    dve.wait_ge(v5.sem, v5[f"cos{half}{h}"])
                    nv.scalar_tensor_tensor(out=dn[:, :, h, :], in0=dt[:, :, h, 1, :], scalar=c["cs"][:, 2 * h + 1:2 * h + 2],
                                            in1=dn[:, :, h, :], op0=ALU.mult, op1=ALU.add)\
                        .then_inc(v5.sem, v5.step(f"den{half}{h}"))
                dve.wait_ge(v5.sem, v5[f"den{half}1"])
                nv.reciprocal(dv, dv).then_inc(v5.sem, v5.step(f"inv{half}"))
                dve.wait_ge(v5.sem, v5[f"inv{half}"])
                for part, name, less in ((0, f"dh{half}", f"dr{half}"), (1, f"dm{half}", f"ds{half}")):
                    nv.tensor_copy(dp[:, :, part, :], dv).then_inc(v5.sem, v5.step(name))
                    dve.wait_ge(v5.sem, v5[name])
                    nv.tensor_tensor(out=dv, in0=dv, in1=dp[:, :, part, :], op=ALU.subtract).then_inc(v5.sem, v5.step(less))
                    dve.wait_ge(v5.sem, v5[less])
                nv.tensor_copy(dp[:, :, 2, :], dv).then_inc(v5.sem, v5.step(f"dl{half}"))
            for i in range(8):
                half, hg = i // HG, i % HG
                q = fqv[:, hg, :, 2 * half:2 * half + 2, :].rearrange("p h b n -> p b h n")
                dve.wait_ge(t5.sem, t5[f"ex{i}"])
                nv.tensor_tensor(out=q, in0=q, in1=ps[:, EB[i % len(EB)], :].rearrange("p (b h n) -> p b h n", b=2, h=NH),
                                 op=ALU.mult).then_inc(v5.sem, v5.step(f"qn{i}"))
            def turned(q):
                dve.wait_ge(t5.sem, t5[f"out{q}"])
                nv.tensor_tensor(out=oc[:, q * BANK:(q + 1) * BANK].rearrange("p (b n) -> p b n", b=2),
                                 in0=ps[0:2 * D, 1 + q, :].rearrange("p (b n) -> p b n", b=2),
                                 in1=turns["cs_out"][0:2 * D, :].unsqueeze(1).broadcast_to([2 * D, 2, N]), op=ALU.mult)\
                    .then_inc(v5.sem, v5.step(f"oc{q}"))

            def centred(q):
                xq = half_of(x5t, q)
                dve.wait_ge(t5.sem, t5[f"fold{q}"])
                nv.tensor_tensor(out=xq, in0=half_of(x4d, q), in1=ps[:, (0, 3)[q], 0:P], op=ALU.add)\
                    .then_inc(v5.sem, v5.step(f"x5{q}"))
                dve.wait_ge(v5.sem, v5[f"x5{q}"])
                less_mean(x5t, v6, q)

            dve.wait_ge(d_late, 32)
            turned(0)
            centred(0)
            variance(v6, 0)
            turned(1)
            normalised(v6, 0, "rstd5")
            centred(1)
            low(v6, a6, 0)
            variance(v6, 1)
            normalised(v6, 1, "rstd5")
            low(v6, a6, 1)
            dve.wait_ge(t6.sem, t6["st1"])
            nv.tensor_copy(stack1[:, BANK:], stacked_half(1)).then_inc(v6.sem, v6.step("s1b"))

            for i, (t, _, _) in enumerate(TILES):
                dve.wait_ge(t6.sem, t6[f"v{i}"])
                nv.tensor_copy(v_diff.rearrange("p (k t e) -> p k t e", k=NF, t=T)[:, :, t, :],
                               ps[:, 2 * (i % 3) + 1, :].rearrange("p (k e) -> p k e", k=NF))\
                    .then_inc(v6.sem, v6.step(f"vm{i}"))
            taps, by_parity = small(1)
            nv.tensor_copy(arp[:, :, :, 1, :], taps.rearrange("p (i r n) -> p i r n", i=KU, r=2)).then_inc(v6.sem, v6.step("ar1"))
            nv.tensor_copy(x5pv[:, :, 1, :], by_parity.rearrange("p (r n) -> p r n", r=2)).then_inc(v6.sem, v6.step("x5p1"))
            dve.wait_ge(v6.sem, v6["x5p1"])
            dve.wait_ge(t6.sem, t6["out"])
            for parity_of in range(2):
                cols = slice(parity_of * B * D, (parity_of + 1) * B * D)
                nv.scalar_tensor_tensor(out=x6t[:, cols], in0=ps[:, 4, cols], scalar=window[:, parity_of:parity_of + 1],
                                        in1=x5p[:, cols], op0=ALU.mult, op1=ALU.add)\
                    .then_inc(v6.sem, v6.step(("x6a", "x6")[parity_of]))

        @block.tensor
        def _(pe):
            def mm(out_ap, lhsT, rhs, start=True, stop=True):
                return nc.tensor.matmul(out_ap, lhsT, rhs, start=start, stop=stop)

            pe.wait_ge(d_pw, 16)
            for i in range(3):
                ins = mm(ps[:, 6, i * NOFF:(i + 1) * NOFF], pw[:, i * P:(i + 1) * P], pw[:, 3 * P:])
            ins.then_inc(t0.sem, t0.step("comp"))
            pe.wait_ge(d_front, 16)
            pe.wait_ge(v0.sem, v0["xg"])
            for j, (name, dst) in enumerate((("q", ps[:, 0, 0:N]), ("k", ps[:, 0, N:2 * N]), ("v", ps[:, 1, 0:N]))):
                mm(dst, f["wqkv"][:, j * P:(j + 1) * P], xg[:]).then_inc(t0.sem, t0.step(name))
            pe.wait_ge(v0.sem, v0["q8"])
            mm(ps[:, 7, 0:N + 2 * (W + 1)], f["select"], q_flat[:]).then_inc(t0.sem, t0.step("select"))
            pe.wait_ge(a0.sem, a0["s11"])
            pe.wait_ge(v0.sem, v0["s31"])
            for h in range(NH):
                hs = slice(h * P, (h + 1) * P)
                for i, q in enumerate((q_stack[:, 0:N][:, hs], q_stack[:, N:][:, hs], q_mid[:, hs])):
                    ins = mm(ps[:, 2 + h, 0:B * NOFF], q, comp_bd[:, i * B * NOFF:(i + 1) * B * NOFF],
                             start=i == 0, stop=i == 2)
            ins.then_inc(t0.sem, t0.step("offsets"))
            for h in range(NH):
                ins = nc.tensor.transpose(ps[:, 1, N + h * P:N + (h + 1) * P], q_mid[:, h * P:(h + 1) * P], ident)
            ins.then_inc(t0.sem, t0.step("qtok"))
            pe.wait_ge(v0.sem, v0["v8"])
            for i in range(4):
                if i == 2:
                    pe.wait_ge(v0.sem, v0["gate"])
                for k in range(4):
                    at = (i // 2) * P + (k // 2) * W + k % 2
                    ins = nc.tensor.transpose(ps[:, TB[i], k * P:(k + 1) * P], kvv[:, i % 2, at:at + P], ident)
                ins.then_inc(t0.sem, t0.step(f"table{i}"))

            def index_group(u, i):
                n = u * 9 + i
                if n >= 4:
                    pe.wait_ge(s_bce, n - 3)
                for q in range(4):
                    ins = mm(ps[:, IB[n % 4], q * P:(q + 1) * P],
                             index[:, u * J + 4 * i + q:u * J + 4 * i + q + 1].broadcast_to([P, P]), identb[:])
                ins.then_inc(s_bc, 1)

            pe.wait_ge(v0.sem, v0["index"])
            pe.wait_ge(a0.sem, a0["qtok"])
            for i in range(9):
                index_group(0, i)
            pe.wait_ge(v0.sem, v0["low3"])
            for u in range(T):
                b = u // NH
                for i in range(9):
                    if u + 1 < T:
                        index_group(u + 1, i)
                    for j in range(4 * i, 4 * i + 4):
                        n, slot = (u * J + j) // 8, (u * J + j) % 8
                        if j in (0, J // 2):
                            pe.wait_ge(s_oh, 2 * u + 1 + (j > 0))
                        if slot == 0 and n >= 4:
                            pe.wait_ge(s_ge, n - 3)
                        for q in range(2):
                            for part in range(3):
                                ins = mm(ps[:, 2 + n % 4, slot * SLOT:(slot + 1) * SLOT], ohv[:, u % 2, q, j, :],
                                         tabv[:, q, part, b * G + j // K2, :, :].rearrange("p k d -> p (k d)"),
                                         start=(q, part) == (0, 0), stop=(q, part) == (1, 2))
                        if slot == 7:
                            ins.then_inc(s_gp, 1)
                        if j == J - 1:
                            if slot == 7:
                                pe.wait_ge(s_gp, n + 1)
                                pe.sem_inc(s_un, 1)
                            else:
                                ins.then_inc(s_un, 1)

            pe.wait_ge(d_l3, 32)
            for h in range(NHEAD):
                hg, rows = h // 4, slice(h % 4 * D, (h % 4 + 1) * D)
                dense = p3["dense"][rows, hg * D:(hg + 1) * D]
                bank = WB[h % 4]
                mm(ps[:, bank, hg * D:(hg + 1) * D], p3["wv"][rows, hg * P:(hg + 1) * P], dense)
                ins = mm(ps[0:3, bank, (HG + hg) * D:(HG + hg + 1) * D], p3["bv"][rows, 3 * hg:3 * hg + 3], dense)
            ins.then_inc(tw.sem, tw.step("wd"))

            pe.wait_ge(vz.sem, vz["nwpick"])
            pe.wait_ge(d_stu, 32)
            pe.wait_ge(s_ge, B * GRP)
            for bank, at, n in SELECTED:
                if bank == AR_BANK:
                    ins = mm(ps[:, bank, 0:n], wpick[:], stu[:, at:at + n])
                else:
                    mm(ps[:, bank, 0:n], wpick[:], stu[:, 0:n], stop=False)
                    mm(ps[:, bank, 0:n], (wpick if at == 0 else nwpick)[:], stu[:, n:2 * n], start=False)
            ins.then_inc(tw.sem, tw.step("sel"))

            pe.wait_ge(v1.sem, v1["att"])
            pe.wait_ge(aw.sem, aw["wdb3"])
            for h in range(NH):
                ins = nc.tensor.transpose(ps[:, 0, h * P:(h + 1) * P], att[:, h * P:(h + 1) * P], ident)
            ins.then_inc(t2.sem, t2.step("attT"))
            pe.wait_ge(d_l1, 32)
            pe.wait_ge(a2.sem, a2["attT"])
            mm(ps[:, 1, 0:N], p1["wproj"], att_ch).then_inc(t2.sem, t2.step("proj"))
            pe.wait_ge(v2.sem, v2["poolbd"])
            mm(ps[0:4, 2, 0:B], p1["red"], pool_bd[:]).then_inc(t2.sem, t2.step("poolred"))
            pe.wait_ge(a2.sem, a2["poolred"])
            mm(ps[:, 3, 0:4], pool_red[:], attk[:]).then_inc(t2.sem, t2.step("katt"))
            for t in range(K2):
                if t % 3 == 0:
                    pe.wait_ge(v2.sem, v2[f"mixbd{t // 3}"])
                ins = mm(ps[:, 4, 0:N], wmix_bd[:, t * P:(t + 1) * P], xp[:, t // 3:t // 3 + H, t % 3:t % 3 + W],
                         start=t == 0, stop=t == K2 - 1)
            ins.then_inc(t2.sem, t2.step("conv"))
            pe.wait_ge(v2.sem, v2["x2"])
            for h in range(NH):
                ins = nc.tensor.transpose(ps[:, 5, h * P:(h + 1) * P], x2[:, h * P:(h + 1) * P], ident)
            ins.then_inc(t2.sem, t2.step("x2T"))

            pe.wait_ge(v3.sem, v3["ln"])
            for h in range(NH):
                ins = nc.tensor.transpose(ps[:, 0, h * P:(h + 1) * P], ln[:, h * P:(h + 1) * P], ident)
            ins.then_inc(t3.sem, t3.step("lnT"))
            pe.wait_ge(d_l2, 16)
            pe.wait_ge(a3.sem, a3["lnT"])
            mm(ps[:, 1, 0:N], p2["wq"], ln_ch).then_inc(t3.sem, t3.step("qc"))
            mm(ps[:, 2, 0:N], p2["wk"], ln_ch).then_inc(t3.sem, t3.step("kc"))
            for h in range(NH):
                ins = mm(ps[:, 3, h * P:(h + 1) * P], ln_ch[:, h * P:(h + 1) * P], p2["wv"])
            ins.then_inc(t3.sem, t3.step("vt"))
            pe.wait_ge(a3.sem, a3["qc"])
            pe.wait_ge(v3.sem, v3["kc"])
            for b in range(B):
                rows = slice(b * C, (b + 1) * C)
                mm(ps[:, 4 + b, 0:P], qc[rows, 0:P], kc[rows, 0:P])
                mm(ps[:, 4 + b, P:3 * P], qc[rows, P:2 * P], kc[rows, :]).then_inc(t3.sem, t3.step(f"score{b}"))
            pe.wait_ge(v3.sem, v3[f"score{B - 1}"])
            pe.wait_ge(a3.sem, a3["vt"])
            def turned(b):
                pe.wait_ge(a3.sem, a3[f"exp{B + b}"])
                for r in range(3):
                    ins = nc.tensor.transpose(ps[:, b, r * P:(r + 1) * P], prob[:, (b * 3 + r) * P:(b * 3 + r + 1) * P],
                                              ident)
                ins.then_inc(t3.sem, t3.step(f"pt{b}"))

            def mixed_values(b):
                pe.wait_ge(*((v3.sem, v3[f"pt{b}"]) if b % 2 else (a3.sem, a3[f"pt{b}"])))
                blk = lambda r: prob_t[:, (b * 3 + r) * P:(b * 3 + r + 1) * P]
                vals = lambda h: vt[:, h * P + b * C:h * P + (b + 1) * C]
                first, second = (ps[:, 4, (h * B + b) * C:(h * B + b + 1) * C] for h in range(NH))
                mm(first, blk(0), vals(0))
                mm(second, blk(1), vals(0), stop=False)
                return mm(second, blk(2), vals(1), start=False)

            turned(0)
            for b in range(B):
                if b + 1 < B:
                    turned(b + 1)
                ins = mixed_values(b)
            ins.then_inc(t3.sem, t3.step("pv"))

            def stack_half(v, a, t, q):
                pe.wait_ge(v.sem, v[f"pl{q}"])
                pe.wait_ge(a.sem, a[f"pd{q}"])
                for i in range(4):
                    ins = nc.tensor.transpose(stacked_half(q)[:, i * P:(i + 1) * P],
                                              parts[:, (4 * q + i) * P:(4 * q + i + 1) * P], identb[:])
                ins.then_inc(t.sem, t.step(f"st{q}"))

            def two_passes(out_ap, first, second, tokens_first=True):
                (l0, r0), (l1_, r1) = first, second
                nc.tensor.matmul(out_ap, l0, r0, start=True, stop=False)
                return nc.tensor.matmul(out_ap, l1_, r1, start=False, stop=True)

            BK = 2 * C + 3

            stack_half(v4, a4, t4, 0)
            stack_half(v4, a4, t4, 1)
            pe.wait_ge(a4.sem, a4["s2a"])
            pe.wait_ge(g0.sem, g0["ones"])
            pe.wait_ge(aw.sem, aw["mw2h"])
            pe.wait_ge(gw.sem, gw["mlow"])
            for t in range(T):
                ts = slice(t * P, (t + 1) * P)
                if t == 4:
                    pe.wait_ge(v4.sem, v4["s2b"])
                ins = two_passes(ps[:, t, 0:E * C + E], (stack1[:, ts], moe_w1[:]), (stack2[0:BK, ts], moe_w2[0:BK, :]))
                if t % 4 == 3:
                    ins.then_inc(t4.sem, t4.step(f"experts{t // 4}"))

            stack_half(v5, a5, t5, 0)
            pe.wait_ge(a5.sem, a5["s2a"])
            pe.wait_ge(aw.sem, aw["lw2h"])
            pe.wait_ge(gw.sem, gw["llow"])
            for t in range(T):
                ts = slice(t * P, (t + 1) * P)
                if t == 2:
                    stack_half(v5, a5, t5, 1)
                if t == 3:
                    pe.wait_ge(v5.sem, v5["s2b"])
                if t >= 4:
                    pe.wait_ge(v5.sem, v5[f"vs{t - 4}"])
                for j, name, bank in ((1, "k", 2 * t % 8), (2, "v", (2 * t + 1) % 8)):
                    w = slice(j * DH, (j + 1) * DH)
                    two_passes(ps[:, bank, :], (stack1[:, ts], w1[:, w]), (stack2[0:BK, ts], w2[0:BK, w]))\
                        .then_inc(t5.sem, t5.step(f"{name}{t}"))
            for hg in range(HG):
                w = slice(hg * P, (hg + 1) * P)
                for half in range(2):
                    i, ts = 2 * hg + half, slice(half * BANK, (half + 1) * BANK)
                    if i >= 4:
                        pe.wait_ge(v5.sem, v5[f"fq{i - 4}"])
                    elif half == 0:
                        pe.wait_ge(v5.sem, v5[f"vs{4 + hg}"])
                    two_passes(ps[:, i % 4, :], (w1[:, w], stack1[:, ts]), (w2[0:BK, w], stack2[0:BK, ts]))\
                        .then_inc(t5.sem, t5.step(f"q{i}"))
                if hg == 0:
                    pe.wait_ge(v5.sem, v5[f"vs{T - 1}"])
                elif hg % 2:
                    pe.wait_ge(a5.sem, a5[f"kv{hg - 1}"])
                else:
                    pe.wait_ge(v5.sem, v5[f"kv{hg - 1}"])
                for b in range(B):
                    for h in range(NH):
                        t = h * B + b
                        ins = mm(ps[:, 4 + b, 0:HCOLS], fk[:, t * BANK + hg * P:t * BANK + (hg + 1) * P], vcv[:, t, hg, :],
                                 start=h == 0, stop=h == NH - 1)
                ins.then_inc(t5.sem, t5.step(f"kv{hg}"))
            pe.wait_ge(v5.sem, v5["ksb"])
            def to_tokens(half):
                if half:
                    pe.wait_ge(v5.sem, v5["kv3"])
                pe.wait_ge(a5.sem, a5[f"dc{half}"])
                for i in range(4):
                    at = (4 * half + i) * P
                    ins = nc.tensor.transpose(ps[:, DB[half], i * 32:(i + 1) * 32], den_ch[:, at:at + P], ident[0:32, 0:32])
                ins.then_inc(t5.sem, t5.step(f"denT{half}"))

            def to_rows(half):
                pe.wait_ge(v5.sem, v5[f"dl{half}"])
                if half:
                    pe.wait_ge(a5.sem, a5["dp0"])
                for i in range(4):
                    t = 4 * half + i
                    ins = nc.tensor.transpose(psb[0][0:NPART, i * P:(i + 1) * P], den_p[:, t * NPART:(t + 1) * NPART], identb[:])
                ins.then_inc(t5.sem, t5.step(f"dp{half}"))

            for b in range(B):
                if b == 3:
                    to_tokens(0)
                for hg in range(HG):
                    ins = mm(ps[0:32, b // 2, b % 2 * N:(b % 2 + 1) * N], ks_bd[:, (hg * B + b) * 32:(hg * B + b + 1) * 32],
                             fqv[:, hg, :, b, :], start=hg == 0, stop=hg == HG - 1)
                if b % 2:
                    ins.then_inc(t5.sem, t5.step(f"den{b // 2}"))
            to_tokens(1)
            to_rows(0)
            pe.wait_ge(a5.sem, a5["expand"])
            def expand(i):
                half, hg = i // HG, i % HG
                if hg == 0:
                    pe.wait_ge(a5.sem, a5[f"dp{half}"])
                if i >= len(EB):
                    pe.wait_ge(v5.sem, v5[f"qn{i - len(EB)}"])
                mm(ps[:, EB[i % len(EB)], :], expandb[0:NPART, hg * P:(hg + 1) * P],
                   den_parts[0:NPART, half * BANK:(half + 1) * BANK]).then_inc(t5.sem, t5.step(f"ex{i}"))

            def output(i):
                half, hg = i // HG, i % HG
                pe.wait_ge(v5.sem, v5[f"qn{i}"])
                if i == 0:
                    pe.wait_ge(v5.sem, v5["kv3"])
                for b in (2 * half, 2 * half + 1):
                    n = hg * B + b
                    ins = mm(ps[0:2 * D, 1 + half, b % 2 * N:(b % 2 + 1) * N], mcs[:, n * 2 * D:(n + 1) * 2 * D],
                             fqv[:, hg, :, b, :], start=hg == 0 and b % 2 == 0, stop=hg == HG - 1 and b % 2 == 1)
                if hg == HG - 1:
                    ins.then_inc(t5.sem, t5.step(f"out{half}"))

            for i in range(HG):
                expand(i)
            to_rows(1)
            output(0)
            for i in range(HG, 2 * HG):
                expand(i)
                if i < 2 * HG - 1:
                    output(i - HG + 1)
            def fold(q):
                pe.wait_ge(v5.sem, v5[f"oc{q}"])
                for i in range(4):
                    at = (4 * q + i) * P
                    ins = mm(ps[:, (0, 3)[q], i * D:(i + 1) * D], oc[:, at:at + P], c["fold"][0:2 * D, :])
                ins.then_inc(t5.sem, t5.step(f"fold{q}"))

            def by_parity(q):
                xq = half_of(x5t, q).rearrange("p (b h c) -> p b h c", b=2, h=NH)
                pe.wait_ge(v5.sem, v5[f"x5{q}"])
                for r in range(2):
                    for h in range(NH):
                        at = r * (PARITY // 2) + (1 - h) * (P // 2)
                        mm(small(q)[1][:, r * P // 2:(r + 1) * P // 2], parity[:, at:at + P], xq[:, :, h, :],
                           start=h == 0, stop=h == 1)

            for i in range(HG, 2 * HG):
                output(i)
                if i == 2 * HG - 2:
                    fold(0)
            pe.wait_ge(d_parity, 16)
            by_parity(0)
            fold(1)
            by_parity(1)
            stack_half(v6, a6, t6, 0)
            pe.wait_ge(a6.sem, a6["s1a"])
            pe.wait_ge(gw.sem, gw["slow"])
            tokens, two = stack1.rearrange("p (b i r) -> p b r i", b=B, r=2), 2 * C
            for i, (_, r, b) in enumerate(TILES):
                if i == 2:
                    stack_half(v6, a6, t6, 1)
                if i >= 3:
                    pe.wait_ge(a6.sem, a6[f"vp{i - 3}"])
                    pe.wait_ge(v6.sem, v6[f"vm{i - 3}"])
                if i == 4:
                    pe.wait_ge(v6.sem, v6["s1b"])
                taps = small(b // 2)[0].rearrange("p (i t e) -> p i t e", i=KU, t=4)[:, :, i % 4, :]
                for out_ap, w in ((taps, slice(2 * NF * D, STU)),
                                  (ps[:, 2 * (i % 3), :], slice(0, NF * D)), (ps[:, 2 * (i % 3) + 1, :], slice(NF * D, 2 * NF * D))):
                    ins = two_passes(out_ap, (tokens[:, b, r, :], stu_w1[:, w]), (tokens[0:two, b, r, :], stu_w2[0:two, w]))
                ins.then_inc(t6.sem, t6.step(f"v{i}"))
            EVEN, ODD, BOTH = slice(0, P), slice(P, 2 * P), slice(0, 2 * P)

            def add(to, lags, values, **kw):
                return mm(ps[:, 4, to], lags, values, **{"start": False, "stop": False, **kw})

            pe.wait_ge(d_toep, 16)
            pe.wait_ge(a6.sem, a6["vp5"])
            pe.wait_ge(v6.sem, v6["vm5"])
            for k in range(NF):
                at = k * LAGS
                add(ODD, toep[:, at + P + 1:at + LAGS], v_diff[:, k * N:k * N + P], start=k == 0)
            pe.wait_ge(a6.sem, a6["vp7"])
            pe.wait_ge(v6.sem, v6["ar1"])
            for k in range(NF):
                at = k * LAGS
                add(EVEN, toep[:, at + P:at + LAGS - 1], v_diff[:, k * N + P:(k + 1) * N])
                add(BOTH, toep[:, at:at + P], v_sum[:, k * N:(k + 1) * N])
            at, taps = NF * LAGS, [ar_v[:, i * N:(i + 1) * N] for i in range(KU)]
            shift = toep[:, at:at + P]
            add(BOTH, ident, taps[0])
            add(ODD, ident, taps[1][:, EVEN])
            add(EVEN, shift, taps[1][:, ODD])
            ins = add(BOTH, shift, taps[2], stop=True)
            ins.then_inc(t6.sem, t6.step("out"))


def kernel(**inputs):
    import numpy as np
    import concourse.bacc as bacc
    from concourse.bass_utils import run_bass_kernel_spmd

    a = {k: np.asarray(v) for k, v in inputs.items()}
    f32 = np.float32

    def pack(block, parts):
        return np.concatenate([np.asarray(parts[n], f32).reshape(-1, w) for n, w in block], axis=1)

    def rows(v, n=P):
        return np.broadcast_to(np.asarray(v, f32).reshape(1, -1), (n, np.size(v)))

    def images(v):
        v = np.asarray(v).reshape(C, -1)
        return np.concatenate([v] * B, axis=0)

    def diagonal(w):
        out = np.zeros((P, P), w.dtype)
        for b in range(B):
            out[b * C:(b + 1) * C, b * C:(b + 1) * C] = w
        return out

    p = np.arange(P)
    eye = np.eye(P, dtype=f32)
    grid = np.zeros((P, NH, G, K2, 2), f32)
    for g in range(G):
        dil = 2 * g + 1
        for t in range(K2):
            for h in range(NH):
                n = h * P + p
                grid[:, h, g, t, 0] = n // W + (t // 3 - 1) * dil
                grid[:, h, g, t, 1] = n % W + (t % 3 - 1) * dil
    turn = (1.57 * np.arange(N, dtype=f32) / N).astype(f32).reshape(NH, P).T
    cst = pack(CST, {
        "ident": eye, "bmask": (p[:, None] // C == np.arange(B)).astype(f32), "base": grid.reshape(P, -1),
        "boff": rows(np.concatenate([a["L0_conv_b_off"].reshape(-1), a["L0_conv_b_mask"]])),
        "pidx": np.stack([p, p + P], 1).astype(f32),
        "cs": np.stack([np.cos(turn), np.sin(turn)], 2).reshape(P, -1),
        "tokidx": np.stack([2 * p, 2 * p + 1], 1),
        "lt4": rows(np.tril(np.ones((4, 4)), -1)), "lt8": rows(np.tril(np.ones((8, 8)), -1)),
        "neghalf": np.full((P, 8), -0.5), "quarter": np.full((P, NF), 0.25),
        "frac": rows(np.array([N, N // 2, N // 4, N // 8])),
        "fold": p[:, None] % C == np.arange(C),
        "headsel": (np.arange(NHEAD)[None, None] == np.arange(HG)[None, :, None] * 4 + p[:, None, None] // D).reshape(P, -1),
        "gumbel": rows(a["L3_ffn_gumbel"]), "logw": rows(a["L3_ffn_log_weights"])})
    q8_image, q8_channel = p % C // HC, p % HC
    w_dw = a["L0_conv_w_dw"].reshape(3, C, K2)
    front = pack(FRONT, {
        "wqkv": np.concatenate([diagonal(a["L0_conv_w_qkv"][:, j * C:(j + 1) * C]) for j in range(3)], 1),
        "wdw": images(w_dw.transpose(1, 0, 2)), "bqkv": images(a["L0_conv_b_qkv"].reshape(3, C).T),
        "bdw": images(a["L0_conv_b_dw"].reshape(3, C).T),
        "select": (q8_image * C + q8_channel)[None, :] == p[:, None], "bmask8": q8_image[:, None] == np.arange(B)})
    wo = np.concatenate([a["L0_conv_w_off"].reshape(G * 2 * K2, C), a["L0_conv_w_mask"]], 0).T
    pw = np.zeros((PWK, 3, P), f32)
    pwo = np.zeros((PWK, NOFF), f32)
    for s in range(5):
        w = a["L0_conv_pconv_off_w"][s] if s < G else a["L0_conv_pconv_mask_w"]
        w = w.reshape(HC, HC, K2)
        rows_s, cols_s = slice(s * HC, (s + 1) * HC), slice(s * 2 * K2, (s + 1) * 2 * K2 if s < G else NOFF)
        for i in range(2):
            pw[rows_s, i] = np.repeat(w[:, :, list(AROUND[4 * i:4 * i + 4])].transpose(0, 2, 1)[:, :, None], B, 2).reshape(HC, P)
        pw[rows_s, 2].reshape(HC, B, C)[:, :, 0:HC] = w[:, None, :, K2 // 2]
        pwo[rows_s, cols_s] = wo[0:HC, cols_s]
    pw[5 * HC:, 2] = (np.arange(C)[:, None] == p % C) * (p % C >= HC)
    pwo[5 * HC:] = wo
    pw = np.concatenate([pw.reshape(PWK, -1), pwo], 1)
    l1 = pack(L1, {
        "wproj": diagonal(a["L0_conv_w_proj"]), "bproj": images(a["L0_conv_b_proj"]),
        "red": images(a["L1_conv_reduction_kernel"]),
        "convk": images(a["L1_conv_conv_kernels"].reshape(4, K2, C, C).transpose(2, 0, 1, 3)),
        "kbias": images(a["L1_conv_bias"].T), "bnscale": images(a["L1_conv_bn_scale"]),
        "bnbias": images(a["L1_conv_bn_bias"]), "bnmean": images(a["L1_conv_bn_mean"]),
        "bnvar": images(a["L1_conv_bn_var"])})
    future = np.where(p[None, :] > p[:, None], -1e12, 0.0).astype(f32)
    l2 = pack(L2, {"wq": diagonal(a["L2_attn_Wq"]), "wk": diagonal(a["L2_attn_Wk"]), "wv": diagonal(a["L2_attn_Wv"]),
                   "causal": np.concatenate([future, np.zeros((P, P), f32), future], 1)})
    def stack(v):
        return np.concatenate([v] * 4, 0)

    moe = stack(np.concatenate([a["L2_ffn_expert_w"].transpose(1, 0, 2).reshape(C, -1), a["L2_ffn_router_w"]], 1))
    moeb = rows(np.concatenate([a["L2_ffn_expert_b"].reshape(-1), a["L2_ffn_router_b"]]))
    l3w = stack(np.concatenate([a["L3_attn_wq_w"].T, a["L3_attn_wk_w"].T], 1))
    l3b = rows(np.concatenate([a["L3_attn_wq_b"], a["L3_attn_wk_b"]]), 3)
    l3 = pack(L3, {"dense": a["L3_attn_dense_w"].T.reshape(HG, P, D).transpose(1, 0, 2).reshape(P, -1),
                   "denseb": rows(a["L3_attn_dense_b"]),
                   "wv": np.tile(a["L3_attn_wv_w"].reshape(HG, P, 1, C).transpose(1, 0, 2, 3), (1, 1, 4, 1)).reshape(P, -1),
                   "bv": np.repeat(a["L3_attn_wv_b"].reshape(HG, P).T, 3, 1)})
    angle = (1.57 * np.arange(N, dtype=f32) / N).astype(f32)
    turn_rows = lambda n: np.concatenate([np.tile(np.cos(angle), (n, 1)), np.tile(np.sin(angle), (n, 1)),
                                          np.zeros((P - 2 * n, N), f32)], 0)
    ex = np.zeros((P, DH), f32)
    ex[0:NPART] = np.arange(NPART)[:, None] % NHEAD == np.arange(DH)[None, :] // D
    turn = pack(TURN, {"cs_out": turn_rows(D), "expand": ex})
    mphi = np.stack([a["L3_ffn_M_phi_plus"], a["L3_ffn_M_phi_minus"]], 1)
    stu = np.concatenate([mphi.transpose(0, 3, 1, 2, 4).reshape(P, -1),
                          a["L3_ffn_M_u"].transpose(0, 2, 1, 3).reshape(P, -1)], 1)
    phi = np.concatenate([np.zeros((N, NF), f32), a["L3_ffn_phi"][:N]], 0)
    even = phi[2 * (p[None, :] - p[:, None]) + N]
    odd = phi[2 * (np.arange(XT)[None, :] - p[:, None]) - 1 + N]
    toep = np.concatenate([np.concatenate([even, odd], 1).transpose(0, 2, 1).reshape(P, -1),
                           np.arange(XT)[None, :] == p[:, None] + 1], 1)
    parity = np.zeros((P, 2, 3, P // 2), f32)
    for r in range(2):
        parity[:, r, 1] = p[:, None] == 2 * np.arange(P // 2)[None, :] + r
    parity = parity.reshape(P, -1)
    x_ch = a["x"].reshape(B, N, C).transpose(0, 2, 1).reshape(P, N)

    host = dict(x_ch=x_ch, cst=cst, front=front, pw=pw, l1=l1, attk=a["L1_conv_attention_kernel"], l2=l2, moe=moe,
                moeb=moeb, l3w=l3w, l3b=l3b, l3=l3, turn=turn, sigma=rows(a["L3_ffn_sigma"]), stu=stu, toep=toep, parity=parity)
    nc = bacc.Bacc("TRN2", target_bir_lowering=False, num_devices=1)
    arrays, args = {}, []
    for name, v in host.items():
        v = np.ascontiguousarray(v, dtype=f32)
        arrays[f"in_{name}"] = v
        args.append(nc.dram_tensor(f"in_{name}", v.shape, F32, kind="ExternalInput").ap())
    args.append(nc.dram_tensor("out_x", (P, T * C), F32, kind="ExternalOutput").ap())
    hybrid(nc, *args)
    r = run_bass_kernel_spmd(nc, [arrays], core_ids=[0])
    got = r.results[0]["out_x"]
    return got.reshape(P, 2, B, C).transpose(2, 0, 1, 3).reshape(B, H, W, C)
```
